# Optimizing a Trainium2 kernel written in Bass

```python
import numpy as np
import jax
import jax.numpy as jnp

def _softmax(x, axis=-1):
    return jax.nn.softmax(x, axis=axis)

def _gelu(x):
    return jax.nn.gelu(x, approximate=True)

def _silu(x):
    return jax.nn.silu(x)

def _sigmoid(x):
    return jax.nn.sigmoid(x)

def _layernorm(x, axis=-1, eps=1e-05):
    m = jnp.mean(x, axis=axis, keepdims=True)
    v = jnp.var(x, axis=axis, keepdims=True)
    return (x - m) / jnp.sqrt(v + eps)

def _scatter_add(tgt, idx, src, axis=0):
    return tgt.at[idx].add(src)

def _segment_sum(src, seg, n):
    return jax.ops.segment_sum(src, seg, n)
kernel_name = 'mk_adaln_d2_jaxref_r8_f1003e'

def setup_inputs(seed: int=0):
    np.random.seed(seed)
    _w = jnp.asarray

    def _L0_attn_setup():
        import jax, jax.numpy as jnp
        import numpy as np
        B, S, E = (4, 256, 128)
        TOP_K = 32
        key = jax.random.key(seed)
        ks = jax.random.split(key, 7)
        scale = 1.0 / np.sqrt(E)
        return {'x': jax.random.normal(ks[0], (B, S, E), dtype=jnp.float32), 'Wq': jax.random.uniform(ks[1], (E, E), jnp.float32, -scale, scale), 'bq': jax.random.uniform(ks[2], (E,), jnp.float32, -scale, scale), 'Wk': jax.random.uniform(ks[3], (E, E), jnp.float32, -scale, scale), 'bk': jax.random.uniform(ks[4], (E,), jnp.float32, -scale, scale), 'Wv': jax.random.uniform(ks[5], (E, E), jnp.float32, -scale, scale), 'bv': jax.random.uniform(ks[6], (E,), jnp.float32, -scale, scale)}
    _L0_attn_in = _L0_attn_setup()

    def _L0_ffn_setup():
        import jax, jax.numpy as jnp
        import numpy as np
        DIM = 128
        DEPTH = 6
        HEADS = 16
        DIM_HEAD = 64
        WINDOW = 32
        INNER = HEADS * DIM_HEAD
        DIM_INNER = int(DIM * 4 * 2 / 3)
        QK_SCALE = 8.0

        def shift_tokens(t):
            a, s = jnp.split(t, 2, -1)
            s = jnp.pad(s, ((0, 0), (1, 0), (0, 0)))[:, :-1]
            return jnp.concatenate([a, s], -1)

        def l2norm(t):
            return t / jnp.maximum(jnp.linalg.norm(t, axis=-1, keepdims=True), 1e-12)

        def rotate_half(x):
            x1, x2 = jnp.split(x, 2, -1)
            return jnp.concatenate([-x2, x1], -1)

        def rotary_tables(n):
            half = jnp.arange(0, DIM_HEAD, 2, dtype=jnp.float32)
            inv_freq = 1.0 / 10000.0 ** (half / DIM_HEAD)
            t = jnp.arange(n, dtype=jnp.float32)
            freqs = t[:, None] * inv_freq[None, :]
            freqs = jnp.concatenate([freqs, freqs], -1)
            base_scale = (half + 0.4 * DIM_HEAD) / (1.4 * DIM_HEAD)
            power = (t - n // 2) / (WINDOW // 2)
            scale = base_scale[None, :] ** power[:, None]
            scale = jnp.concatenate([scale, scale], -1)
            return (freqs, scale)

        def local_attention(q, k, v):
            b, h, n, d = q.shape
            w = WINDOW
            nw = n // w
            bq = q.reshape(b, h, nw, w, d)
            bk = k.reshape(b, h, nw, w, d)
            bv = v.reshape(b, h, nw, w, d)

            def look(t):
                p = jnp.pad(t, ((0, 0), (0, 0), (1, 0), (0, 0), (0, 0)))
                return jnp.concatenate([p[:, :, :nw], p[:, :, 1:]], axis=3)
            bk2, bv2 = (look(bk), look(bv))
            seq = jnp.arange(n).reshape(nw, w)
            seq_p = jnp.pad(seq, ((1, 0), (0, 0)), constant_values=-1)
            jt = jnp.concatenate([seq_p[:nw], seq_p[1:]], axis=1)
            it = seq[:, :, None]
            jb = jt[:, None, :]
            mask = (it < jb) | (it > jb + w) | (jb == -1)
            sim = jnp.einsum('bhwie,bhwje->bhwij', bq, bk2) * QK_SCALE
            sim = jnp.where(mask, -jnp.finfo(sim.dtype).max, sim)
            attn = jax.nn.softmax(sim, -1)
            out = jnp.einsum('bhwij,bhwje->bhwie', attn, bv2)
            return out.reshape(b, h, n, d)

        def attn_layer(x, Wqkv, qs, ksc, Wo):
            b, n, _ = x.shape
            qkv = x @ Wqkv
            q, k, v = jnp.split(qkv, 3, -1)
            sh = lambda t: t.reshape(b, n, HEADS, DIM_HEAD).transpose(0, 2, 1, 3)
            q, k, v = (sh(q), sh(k), sh(v))
            q = l2norm(q) * qs
            k = l2norm(k) * ksc
            freqs, scale = rotary_tables(n)
            cos, sin = (jnp.cos(freqs), jnp.sin(freqs))
            q = q * cos * scale + rotate_half(q) * sin * scale
            inv = 1.0 / scale
            k = k * cos * inv + rotate_half(k) * sin * inv
            out = local_attention(q, k, v)
            out = out.transpose(0, 2, 1, 3).reshape(b, n, INNER)
            return out @ Wo

        def ffn_layer(x, g, bln, W1, b1, W2, b2):
            mu = x.mean(-1, keepdims=True)
            var = ((x - mu) ** 2).mean(-1, keepdims=True)
            xn = (x - mu) / jnp.sqrt(var + 1e-05) * g + bln
            hg = xn @ W1 + b1
            a, gate = jnp.split(hg, 2, -1)
            return a * jax.nn.gelu(gate, approximate=False) @ W2 + b2
        key = jax.random.key(seed)
        ks = jax.random.split(key, 8)
        B, N = (2, 256)
        init = lambda k, shape: jax.random.normal(k, shape, jnp.float32) * 0.02
        return {'x': jax.random.normal(ks[0], (B, N, DIM), jnp.float32), 'Wqkv': init(ks[1], (DEPTH, DIM, 3 * INNER)), 'q_scale': jnp.ones((DEPTH, DIM_HEAD), jnp.float32), 'k_scale': jnp.ones((DEPTH, DIM_HEAD), jnp.float32), 'Wo': init(ks[2], (DEPTH, INNER, DIM)), 'ln_g': jnp.ones((DEPTH, DIM), jnp.float32), 'ln_b': jnp.zeros((DEPTH, DIM), jnp.float32), 'W1': init(ks[3], (DEPTH, DIM, 2 * DIM_INNER)), 'b1': jnp.zeros((DEPTH, 2 * DIM_INNER), jnp.float32), 'W2': init(ks[4], (DEPTH, DIM_INNER, DIM)), 'b2': jnp.zeros((DEPTH, DIM), jnp.float32)}
    _L0_ffn_in = _L0_ffn_setup()
    _L0_c = _w((lambda *s: np.random.randn(*s).astype(np.float32) * 0.05)(16, 128))
    _L0_wmod = _w((lambda *s: np.random.randn(*s).astype(np.float32) * 0.05)(128, 6 * 128) * 128 ** (-0.5))

    def _L1_attn_setup():
        import jax, jax.numpy as jnp
        import numpy as np
        B, S, IN_DIM = (2, 256, 128)
        OUT_DIM, H = (128, 16)
        D = OUT_DIM // H
        W1, W2 = (16, 16)
        LN_EPS = 1e-05

        def _causal_windows(t, w):
            b, s, h, d = t.shape
            padded = jnp.concatenate([jnp.zeros((b, w - 1, h, d), t.dtype), t], axis=1)
            return jnp.stack([padded[:, j:j + s] for j in range(w)], axis=2)

        def _forward(x, Wq, Wk, Wv, Wkp, Wo, gamma, beta):
            b, s, _ = x.shape
            proj = lambda W: (x @ W.T).reshape(b, s, H, D)
            Q, K, V, Kp = (proj(Wq), proj(Wk), proj(Wv), proj(Wkp))
            K_win = _causal_windows(K, W1)
            Kp_win = _causal_windows(Kp, W2)
            V_win = _causal_windows(V, W1)
            Vp_win = _causal_windows(V, W2)
            A = jnp.einsum('bshd,bsjhd,bskhd->bshjk', Q, K_win, Kp_win) / jnp.sqrt(jnp.float32(D))
            s_idx = jnp.arange(s)[:, None]
            m1 = jnp.arange(W1)[None, :] >= W1 - 1 - s_idx
            m2 = jnp.arange(W2)[None, :] >= W2 - 1 - s_idx
            mask = m1[:, :, None] & m2[:, None, :]
            A = jnp.where(mask[None, :, None], A, -jnp.inf)
            P = jax.nn.softmax(A.reshape(b, s, H, W1 * W2), axis=-1).reshape(b, s, H, W1, W2)
            Z = jnp.einsum('bshjk,bsjhd,bskhd->bshd', P, V_win, Vp_win)
            out = Z.reshape(b, s, OUT_DIM) @ Wo.T + x
            mu = jnp.mean(out, axis=-1, keepdims=True)
            var = jnp.mean(jnp.square(out - mu), axis=-1, keepdims=True)
            return (out - mu) / jnp.sqrt(var + LN_EPS) * gamma + beta
        key = jax.random.key(seed)
        ks = jax.random.split(key, 8)
        sc_in = 1.0 / np.sqrt(IN_DIM)
        sc_out = 1.0 / np.sqrt(OUT_DIM)
        return {'x': jax.random.normal(ks[0], (B, S, IN_DIM), dtype=jnp.float32), 'Wq': jax.random.normal(ks[1], (OUT_DIM, IN_DIM), dtype=jnp.float32) * sc_in, 'Wk': jax.random.normal(ks[2], (OUT_DIM, IN_DIM), dtype=jnp.float32) * sc_in, 'Wv': jax.random.normal(ks[3], (OUT_DIM, IN_DIM), dtype=jnp.float32) * sc_in, 'Wkp': jax.random.normal(ks[4], (OUT_DIM, IN_DIM), dtype=jnp.float32) * sc_in, 'Wo': jax.random.normal(ks[5], (OUT_DIM, OUT_DIM), dtype=jnp.float32) * sc_out, 'gamma': jnp.ones((OUT_DIM,), dtype=jnp.float32), 'beta': jnp.zeros((OUT_DIM,), dtype=jnp.float32)}
    _L1_attn_in = _L1_attn_setup()

    def _L1_ffn_setup():
        import jax, jax.numpy as jnp
        import numpy as np
        from math import ceil
        CAPACITY_FACTOR = 2.0
        MIN_CAPACITY = 4
        key = jax.random.key(seed)
        ks = jax.random.split(key, 4)
        B, S, D, Di, E = (4, 256, 128, 512, 8)
        x = jax.random.normal(ks[0], (B, S, D), dtype=jnp.float32)
        Wr = jax.random.normal(ks[1], (D, E), dtype=jnp.float32) * D ** (-0.5)
        W1 = jax.random.normal(ks[2], (E, D, Di), dtype=jnp.float32) * D ** (-0.5)
        b1 = jnp.zeros((E, Di), dtype=jnp.float32)
        W2 = jax.random.normal(ks[3], (E, Di, D), dtype=jnp.float32) * Di ** (-0.5)
        b2 = jnp.zeros((E, D), dtype=jnp.float32)
        return {'x': x, 'Wr': Wr, 'W1': W1, 'b1': b1, 'W2': W2, 'b2': b2}
    _L1_ffn_in = _L1_ffn_setup()
    _L1_c = _w((lambda *s: np.random.randn(*s).astype(np.float32) * 0.05)(16, 128))
    _L1_wmod = _w((lambda *s: np.random.randn(*s).astype(np.float32) * 0.05)(128, 6 * 128) * 128 ** (-0.5))
    _d = {'L0_attn_x': _L0_attn_in['x'], 'L0_attn_Wq': _L0_attn_in['Wq'], 'L0_attn_bq': _L0_attn_in['bq'], 'L0_attn_Wk': _L0_attn_in['Wk'], 'L0_attn_bk': _L0_attn_in['bk'], 'L0_attn_Wv': _L0_attn_in['Wv'], 'L0_attn_bv': _L0_attn_in['bv'], 'L0_ffn_Wqkv': _L0_ffn_in['Wqkv'], 'L0_ffn_q_scale': _L0_ffn_in['q_scale'], 'L0_ffn_k_scale': _L0_ffn_in['k_scale'], 'L0_ffn_Wo': _L0_ffn_in['Wo'], 'L0_ffn_ln_g': _L0_ffn_in['ln_g'], 'L0_ffn_ln_b': _L0_ffn_in['ln_b'], 'L0_ffn_W1': _L0_ffn_in['W1'], 'L0_ffn_b1': _L0_ffn_in['b1'], 'L0_ffn_W2': _L0_ffn_in['W2'], 'L0_ffn_b2': _L0_ffn_in['b2'], 'L0_c': _L0_c, 'L0_wmod': _L0_wmod, 'L1_attn_Wq': _L1_attn_in['Wq'], 'L1_attn_Wk': _L1_attn_in['Wk'], 'L1_attn_Wv': _L1_attn_in['Wv'], 'L1_attn_Wkp': _L1_attn_in['Wkp'], 'L1_attn_Wo': _L1_attn_in['Wo'], 'L1_attn_gamma': _L1_attn_in['gamma'], 'L1_attn_beta': _L1_attn_in['beta'], 'L1_ffn_Wr': _L1_ffn_in['Wr'], 'L1_ffn_W1': _L1_ffn_in['W1'], 'L1_ffn_b1': _L1_ffn_in['b1'], 'L1_ffn_W2': _L1_ffn_in['W2'], 'L1_ffn_b2': _L1_ffn_in['b2'], 'L1_c': _L1_c, 'L1_wmod': _L1_wmod}
    _x0 = _d['L0_attn_x']
    _d['L0_attn_x'] = jax.random.normal(jax.random.fold_in(jax.random.key(seed), 1), (16, 256, 128), dtype=_x0.dtype)
    del _x0
    return _d

def reference(L0_attn_x, L0_attn_Wq, L0_attn_bq, L0_attn_Wk, L0_attn_bk, L0_attn_Wv, L0_attn_bv, L0_ffn_Wqkv, L0_ffn_q_scale, L0_ffn_k_scale, L0_ffn_Wo, L0_ffn_ln_g, L0_ffn_ln_b, L0_ffn_W1, L0_ffn_b1, L0_ffn_W2, L0_ffn_b2, L0_c, L0_wmod, L1_attn_Wq, L1_attn_Wk, L1_attn_Wv, L1_attn_Wkp, L1_attn_Wo, L1_attn_gamma, L1_attn_beta, L1_ffn_Wr, L1_ffn_W1, L1_ffn_b1, L1_ffn_W2, L1_ffn_b2, L1_c, L1_wmod):

    def _L0_attn_ref(x, Wq, bq, Wk, bk, Wv, bv):
        import jax, jax.numpy as jnp
        import numpy as np
        B, S, E = (4, 256, 128)
        TOP_K = 32
        q = jnp.einsum('bse,fe->bsf', x, Wq) + bq
        k = jnp.einsum('bse,fe->bsf', x, Wk) + bk
        v = jnp.einsum('bse,fe->bsf', x, Wv) + bv
        scores = jnp.einsum('bqe,bke->bqk', q, k)
        topk_vals, topk_idx = jax.lax.top_k(scores, TOP_K)
        b_idx = jnp.arange(scores.shape[0])[:, None, None]
        s_idx = jnp.arange(scores.shape[1])[None, :, None]
        sparse_scores = jnp.zeros_like(scores).at[b_idx, s_idx, topk_idx].set(topk_vals)
        denom = sparse_scores.sum(axis=-1, keepdims=True) + 1e-10
        attn = sparse_scores / denom
        return jnp.einsum('bqk,bke->bqe', attn, v)

    def _L0_ffn_ref(x, Wqkv, q_scale, k_scale, Wo, ln_g, ln_b, W1, b1, W2, b2):
        import jax, jax.numpy as jnp
        import numpy as np
        DIM = 128
        DEPTH = 6
        HEADS = 16
        DIM_HEAD = 64
        WINDOW = 32
        INNER = HEADS * DIM_HEAD
        DIM_INNER = int(DIM * 4 * 2 / 3)
        QK_SCALE = 8.0

        def shift_tokens(t):
            a, s = jnp.split(t, 2, -1)
            s = jnp.pad(s, ((0, 0), (1, 0), (0, 0)))[:, :-1]
            return jnp.concatenate([a, s], -1)

        def l2norm(t):
            return t / jnp.maximum(jnp.linalg.norm(t, axis=-1, keepdims=True), 1e-12)

        def rotate_half(x):
            x1, x2 = jnp.split(x, 2, -1)
            return jnp.concatenate([-x2, x1], -1)

        def rotary_tables(n):
            half = jnp.arange(0, DIM_HEAD, 2, dtype=jnp.float32)
            inv_freq = 1.0 / 10000.0 ** (half / DIM_HEAD)
            t = jnp.arange(n, dtype=jnp.float32)
            freqs = t[:, None] * inv_freq[None, :]
            freqs = jnp.concatenate([freqs, freqs], -1)
            base_scale = (half + 0.4 * DIM_HEAD) / (1.4 * DIM_HEAD)
            power = (t - n // 2) / (WINDOW // 2)
            scale = base_scale[None, :] ** power[:, None]
            scale = jnp.concatenate([scale, scale], -1)
            return (freqs, scale)

        def local_attention(q, k, v):
            b, h, n, d = q.shape
            w = WINDOW
            nw = n // w
            bq = q.reshape(b, h, nw, w, d)
            bk = k.reshape(b, h, nw, w, d)
            bv = v.reshape(b, h, nw, w, d)

            def look(t):
                p = jnp.pad(t, ((0, 0), (0, 0), (1, 0), (0, 0), (0, 0)))
                return jnp.concatenate([p[:, :, :nw], p[:, :, 1:]], axis=3)
            bk2, bv2 = (look(bk), look(bv))
            seq = jnp.arange(n).reshape(nw, w)
            seq_p = jnp.pad(seq, ((1, 0), (0, 0)), constant_values=-1)
            jt = jnp.concatenate([seq_p[:nw], seq_p[1:]], axis=1)
            it = seq[:, :, None]
            jb = jt[:, None, :]
            mask = (it < jb) | (it > jb + w) | (jb == -1)
            sim = jnp.einsum('bhwie,bhwje->bhwij', bq, bk2) * QK_SCALE
            sim = jnp.where(mask, -jnp.finfo(sim.dtype).max, sim)
            attn = jax.nn.softmax(sim, -1)
            out = jnp.einsum('bhwij,bhwje->bhwie', attn, bv2)
            return out.reshape(b, h, n, d)

        def attn_layer(x, Wqkv, qs, ksc, Wo):
            b, n, _ = x.shape
            qkv = x @ Wqkv
            q, k, v = jnp.split(qkv, 3, -1)
            sh = lambda t: t.reshape(b, n, HEADS, DIM_HEAD).transpose(0, 2, 1, 3)
            q, k, v = (sh(q), sh(k), sh(v))
            q = l2norm(q) * qs
            k = l2norm(k) * ksc
            freqs, scale = rotary_tables(n)
            cos, sin = (jnp.cos(freqs), jnp.sin(freqs))
            q = q * cos * scale + rotate_half(q) * sin * scale
            inv = 1.0 / scale
            k = k * cos * inv + rotate_half(k) * sin * inv
            out = local_attention(q, k, v)
            out = out.transpose(0, 2, 1, 3).reshape(b, n, INNER)
            return out @ Wo

        def ffn_layer(x, g, bln, W1, b1, W2, b2):
            mu = x.mean(-1, keepdims=True)
            var = ((x - mu) ** 2).mean(-1, keepdims=True)
            xn = (x - mu) / jnp.sqrt(var + 1e-05) * g + bln
            hg = xn @ W1 + b1
            a, gate = jnp.split(hg, 2, -1)
            return a * jax.nn.gelu(gate, approximate=False) @ W2 + b2
        for i in range(DEPTH):
            x = attn_layer(shift_tokens(x), Wqkv[i], q_scale[i], k_scale[i], Wo[i]) + x
            x = ffn_layer(shift_tokens(x), ln_g[i], ln_b[i], W1[i], b1[i], W2[i], b2[i]) + x
        return x

    def _L1_attn_ref(x, Wq, Wk, Wv, Wkp, Wo, gamma, beta):
        import jax, jax.numpy as jnp
        import numpy as np
        B, S, IN_DIM = (2, 256, 128)
        OUT_DIM, H = (128, 16)
        D = OUT_DIM // H
        W1, W2 = (16, 16)
        LN_EPS = 1e-05

        def _causal_windows(t, w):
            b, s, h, d = t.shape
            padded = jnp.concatenate([jnp.zeros((b, w - 1, h, d), t.dtype), t], axis=1)
            return jnp.stack([padded[:, j:j + s] for j in range(w)], axis=2)

        def _forward(x, Wq, Wk, Wv, Wkp, Wo, gamma, beta):
            b, s, _ = x.shape
            proj = lambda W: (x @ W.T).reshape(b, s, H, D)
            Q, K, V, Kp = (proj(Wq), proj(Wk), proj(Wv), proj(Wkp))
            K_win = _causal_windows(K, W1)
            Kp_win = _causal_windows(Kp, W2)
            V_win = _causal_windows(V, W1)
            Vp_win = _causal_windows(V, W2)
            A = jnp.einsum('bshd,bsjhd,bskhd->bshjk', Q, K_win, Kp_win) / jnp.sqrt(jnp.float32(D))
            s_idx = jnp.arange(s)[:, None]
            m1 = jnp.arange(W1)[None, :] >= W1 - 1 - s_idx
            m2 = jnp.arange(W2)[None, :] >= W2 - 1 - s_idx
            mask = m1[:, :, None] & m2[:, None, :]
            A = jnp.where(mask[None, :, None], A, -jnp.inf)
            P = jax.nn.softmax(A.reshape(b, s, H, W1 * W2), axis=-1).reshape(b, s, H, W1, W2)
            Z = jnp.einsum('bshjk,bsjhd,bskhd->bshd', P, V_win, Vp_win)
            out = Z.reshape(b, s, OUT_DIM) @ Wo.T + x
            mu = jnp.mean(out, axis=-1, keepdims=True)
            var = jnp.mean(jnp.square(out - mu), axis=-1, keepdims=True)
            return (out - mu) / jnp.sqrt(var + LN_EPS) * gamma + beta
        return _forward(x, Wq, Wk, Wv, Wkp, Wo, gamma, beta)

    def _L1_ffn_ref(x, Wr, W1, b1, W2, b2):
        import jax, jax.numpy as jnp
        import numpy as np
        from math import ceil
        CAPACITY_FACTOR = 2.0
        MIN_CAPACITY = 4
        B, S, D = x.shape
        E = Wr.shape[1]
        N = B * S
        k = max(MIN_CAPACITY, ceil(N * CAPACITY_FACTOR / E))
        xt = x.reshape(N, D)
        scores = jax.nn.softmax(xt @ Wr, axis=-1)
        G, idx = jax.lax.top_k(scores.T, k)
        X_in = xt[idx]
        h = jax.nn.gelu(jnp.einsum('ekd,edh->ekh', X_in, W1) + b1[:, None, :], approximate=False)
        X_e = jnp.einsum('ekh,ehd->ekd', h, W2) + b2[:, None, :]
        contrib = (G[..., None] * X_e).reshape(E * k, D)
        out = jnp.zeros((N, D), dtype=x.dtype).at[idx.reshape(-1)].add(contrib)
        return out.reshape(B, S, D)
    x = L0_attn_x
    mod = (_silu(L0_c) @ L0_wmod).reshape(L0_c.shape[0], 6, 1, -1)
    sa, ca, ga, sb, cb, gb = (mod[:, 0], mod[:, 1], mod[:, 2], mod[:, 3], mod[:, 4], mod[:, 5])
    ga = (2 * (ga >= 0) - 1) * jnp.maximum(jnp.abs(ga), 0.25)
    gb = (2 * (gb >= 0) - 1) * jnp.maximum(jnp.abs(gb), 0.25)
    h = _layernorm(x, axis=-1) * (1 + ca) + sa
    x = x + ga * _L0_attn_ref(h, L0_attn_Wq, L0_attn_bq, L0_attn_Wk, L0_attn_bk, L0_attn_Wv, L0_attn_bv)
    h = _layernorm(x, axis=-1) * (1 + cb) + sb
    x = x + gb * _L0_ffn_ref(h, L0_ffn_Wqkv, L0_ffn_q_scale, L0_ffn_k_scale, L0_ffn_Wo, L0_ffn_ln_g, L0_ffn_ln_b, L0_ffn_W1, L0_ffn_b1, L0_ffn_W2, L0_ffn_b2)
    mod = (_silu(L1_c) @ L1_wmod).reshape(L1_c.shape[0], 6, 1, -1)
    sa, ca, ga, sb, cb, gb = (mod[:, 0], mod[:, 1], mod[:, 2], mod[:, 3], mod[:, 4], mod[:, 5])
    ga = (2 * (ga >= 0) - 1) * jnp.maximum(jnp.abs(ga), 0.25)
    gb = (2 * (gb >= 0) - 1) * jnp.maximum(jnp.abs(gb), 0.25)
    h = _layernorm(x, axis=-1) * (1 + ca) + sa
    x = x + ga * _L1_attn_ref(h, L1_attn_Wq, L1_attn_Wk, L1_attn_Wv, L1_attn_Wkp, L1_attn_Wo, L1_attn_gamma, L1_attn_beta)
    h = _layernorm(x, axis=-1) * (1 + cb) + sb
    x = x + gb * _L1_ffn_ref(h, L1_ffn_Wr, L1_ffn_W1, L1_ffn_b1, L1_ffn_W2, L1_ffn_b2)
    return x

_drawn_inputs = setup_inputs


def setup_inputs(seed=0):
    import zlib

    import numpy as np

    out = dict(_drawn_inputs(seed))
    spreads = {'L0_ffn_q_scale': (1.0, 0.6),
     'L0_ffn_k_scale': (1.0, 0.6),
     'L0_ffn_ln_g': (1.0, 0.6),
     'L0_ffn_ln_b': (0.0, 0.8),
     'L0_ffn_b1': (0.0, 0.8),
     'L0_ffn_b2': (0.0, 0.541),
     'L1_attn_gamma': (1.0, 0.6),
     'L1_attn_beta': (0.0, 2.0),
     'L1_ffn_b1': (0.0, 2.0),
     'L1_ffn_b2': (0.0, 2.0)}
    factors = {'L0_attn_bq': 8.0,
     'L0_attn_bk': 8.0,
     'L0_attn_bv': 4.052,
     'L0_ffn_W1': 6.907,
     'L0_ffn_W2': 6.809,
     'L1_attn_Wq': 8.0,
     'L1_attn_Wk': 8.0,
     'L1_attn_Wv': 4.558,
     'L1_attn_Wkp': 8.0,
     'L1_attn_Wo': 3.81,
     'L1_ffn_Wr': 3.964,
     'L1_ffn_W1': 6.545,
     'L1_ffn_W2': 4.779}
    for name, (base, spread) in spreads.items():
        noise = np.random.default_rng([zlib.crc32(name.encode()), seed]).standard_normal(out[name].shape)
        drawn = base * np.exp(spread * noise) if base else spread * noise
        out[name] = jnp.asarray(drawn.astype(out[name].dtype))
    for name, factor in factors.items():
        out[name] = (out[name] * factor).astype(out[name].dtype)
    return out
```

```python
from contextlib import ExitStack

import numpy as np

import concourse.bass as bass
from concourse import mybir

F32 = mybir.dt.float32
BF16 = mybir.dt.bfloat16
I32 = mybir.dt.int32
ACT = mybir.ActivationFunctionType
ALU = mybir.AluOpType
AX = mybir.AxisListType.X

P = 128
B = 16
S = 256
D = 128
TPB = S // P
NT = B * TPB
DEPTH = 6
HEADS, DH = 16, 64
INNER = HEADS * DH
WIN = 32
FF = int(D * 4 * 2 / 3)
FFC = [(0, 128), (128, 128), (256, FF - 256)]
TOPK = 32
NEG = -3.0e38
MASKED = -1.0e30
MAGIC = float(0x5F3759DF)
CR = 8
UPB = 4
H2 = HEADS // 2
QK_SCALE = 8.0
PER_UNIT = {"sim_ps": 2, "pv_ps": 4}


def view(t, part0, nparts, offset, dims):
    a = t[part0:part0 + nparts]
    row = a.ap[0][0]
    return bass.AP(tensor=a.tensor, offset=a.offset + offset, ap=[[row, nparts]] + [list(d) for d in dims])


class Chain:

    def __init__(self, eng, sem, per, turn, gate=None):
        self.eng, self.sem, self.k, self.per, self.base, self.gate = eng, sem, 0, per, turn * per, gate

    def __call__(self, ins):
        self.k += 1
        assert self.k <= self.per, self.sem
        ins.then_inc(self.sem, 1)
        self.eng.wait_ge(self.sem, self.base + self.k)
        if self.gate is not None:
            self.eng.sem_inc(self.gate, 1)

    def end(self):
        assert self.k == self.per, (self.sem, self.k)


RSQRT_OPS = 2 + 3 * 3


def rsqrt(nc, link, y, v, tmp):
    link(nc.vector.tensor_scalar(y.bitcast(I32), v.bitcast(I32), 1, None, ALU.logical_shift_right))
    link(nc.vector.tensor_scalar(y.bitcast(I32), y.bitcast(I32), -1.0, MAGIC, ALU.mult, ALU.add))
    for _ in range(3):
        link(nc.vector.tensor_tensor(tmp, y, y, ALU.mult))
        link(nc.vector.scalar_tensor_tensor(tmp, tmp, -0.5, v, ALU.mult, ALU.mult))
        link(nc.vector.scalar_tensor_tensor(y, tmp, 1.5, y, ALU.add, ALU.mult))


def build(nc, a, out):
    with ExitStack() as ctx:
        def sb(name, shape, dt=F32):
            return ctx.enter_context(nc.sbuf_tensor(name, shape, dt))

        def sem(name):
            return ctx.enter_context(nc.semaphore(name))

        ps = ctx.enter_context(nc.psum_tensor("ps", [P, 8, 512], F32))
        x = sb("x", [P, NT, D])
        ident = sb("ident", [P, P])
        identb = sb("identb", [P, P], BF16)
        ones = sb("ones", [P, P])

        loaded = sem("loaded")
        consts = sem("consts")
        with nc.Block() as block:
            @block.sync
            def _(sp):
                sp.dma_start(x[:, :, :], a["x"]).then_inc(loaded, 16)
                sp.dma_start(ident[:, :], a["ident"]).then_inc(loaded, 16)
                sp.wait_ge(loaded, 32)

            @block.vector
            def _(dve):
                dve.wait_ge(loaded, 32)
                nc.vector.tensor_copy(identb[:, :], ident[:, :]).then_inc(consts, 1)
                nc.vector.memset(ones[:, :], 1.0).then_inc(consts, 1)
                dve.wait_ge(consts, 2)

        y = sb("y", [P, NT, D])
        rows = sb("rows", [P, B, 4, D])
        colmod = sb("colmod", [P, 6, B])
        mv = sb("mv_x", [P, 8, NT])
        modulation(nc, a, 0, sem, ps, colmod, rows)
        norm_stats(nc, sem, x, mv, "a")
        top32_attention(nc, a, sem, ps, x, mv, colmod, rows, ident, ones)
        norm_stats(nc, sem, x, mv, "b")
        into_y(nc, sem, x, y, mv, rows)
        local_transformer(nc, a, sem, ps, y, ident, identb, ones)
        add_gated(nc, sem, x, y, rows)
        modulation(nc, a, 1, sem, ps, colmod, rows)
        norm_stats(nc, sem, x, mv, "d")
        third_order_attention(nc, a, sem, ps, x, mv, colmod, rows, ident, identb)
        norm_stats(nc, sem, x, mv, "e")
        expert_choice(nc, a, sem, ps, x, mv, colmod, rows, ident, ones)

        stored = sem("stored")
        with nc.Block() as block:
            @block.sync
            def _(sp):
                sp.dma_start(out, x[:, :, :]).then_inc(stored, 16)
                sp.wait_ge(stored, 16)


class Marks:

    def __init__(self, sem, **by_engine):
        self.s, self.by, self.f = {}, {}, {}
        for who, names in by_engine.items():
            self.by[who] = names
            for n in names:
                self.s[n] = sem(n)

    def give(self, who, eng):
        for n in self.by[who]:
            eng.sem_inc(self.s[n], CR)

    def done(self, eng, name, unit):
        eng.wait_ge(self.s[name], unit + 1 + CR)

    def mark(self, name, ins):
        ins.then_inc(self.s[name], 1)


def staged_batches(eng, lags, stages):
    def slot(b, first=False, last=None):
        for lag, fn in stages:
            if first and b - lag < 0:
                continue
            if last is not None and last - lag >= 0:
                continue
            fn(b - lag if last is None else B + last - lag)
    for b in range(lags):
        slot(b, first=True)
    with eng.Fori(lags, B) as b:
        slot(b)
    for k in range(lags):
        slot(B + k, last=k)


def modulation(nc, a, l, sem, ps, colmod, rows):
    with ExitStack() as ctx:
        sb = lambda n, s, d=F32: ctx.enter_context(nc.sbuf_tensor(n + str(l), s, d))
        cT, sT, wmod = sb("cT", [P, B]), sb("sT", [P, B]), sb("wmod", [P, 6 * D])
        big, sign = sb("big", [P, B, 2, D]), sb("sign", [P, B, 2, D])
        m_in, m_silu, m_ps, m_sb, m_d = (sem(f"{n}{l}") for n in ("m_in", "m_silu", "m_ps", "m_sb", "m_d"))
        with nc.Block() as block:
            @block.sync
            def _(sp):
                sp.dma_start(cT[:, :], a[f"cT{l}"]).then_inc(m_in, 16)
                sp.dma_start(wmod[:, :], a[f"wmod{l}"]).then_inc(m_in, 16)

            @block.scalar
            def _(act):
                act.wait_ge(m_in, 32)
                nc.scalar.activation(sT[:, :], cT[:, :], ACT.Silu).then_inc(m_silu, 1)
                for b in range(B):
                    act.wait_ge(m_ps, b + 2)
                    nc.scalar.activation(rows[:, b, :, :].rearrange("p r d -> p (r d)"), ps[:, 1 + b % 4, :], ACT.Copy).then_inc(m_sb, 1)

            @block.tensor
            def _(pe):
                pe.wait_ge(m_in, 32)
                pe.wait_ge(m_silu, 1)
                for j in range(6):
                    mm = nc.tensor.matmul(ps[:, 0, j * B:(j + 1) * B], wmod[:, j * D:(j + 1) * D], sT[:, :], start=True, stop=True)
                mm.then_inc(m_ps, 1)
                for b in range(B):
                    if b >= 4:
                        pe.wait_ge(m_sb, b - 3)
                    nc.tensor.matmul(ps[:, 1 + b % 4, :], view(sT, 0, P, b, [[0, P]]), wmod[:, 2 * D:6 * D],
                                     start=True, stop=True).then_inc(m_ps, 1)

            @block.vector
            def _(dve):
                v = nc.vector
                dve.wait_ge(m_ps, 1)
                v.tensor_copy(colmod[:, :, :].rearrange("p j b -> p (j b)"), ps[:, 0, 0:6 * B]).then_inc(m_d, 1)
                dve.wait_ge(m_d, 1)
                v.tensor_scalar(colmod[:, 1, :], colmod[:, 1, :], 1.0, None, ALU.add).then_inc(m_d, 1)
                v.tensor_scalar(colmod[:, 4, :], colmod[:, 4, :], 1.0, None, ALU.add).then_inc(m_d, 1)
                dve.wait_ge(m_sb, B)
                v.tensor_scalar(rows[:, :, 2, :], rows[:, :, 2, :], 1.0, None, ALU.add).then_inc(m_d, 1)
                for k, r in enumerate((0, 3)):
                    v.tensor_scalar(sign[:, :, k, :], rows[:, :, r, :], 0.0, 2.0, ALU.is_ge, ALU.mult).then_inc(m_d, 1)
                dve.wait_ge(m_d, 6)
                for k, r in enumerate((0, 3)):
                    v.scalar_tensor_tensor(big[:, :, k, :], sign[:, :, k, :], -1.0, rows[:, :, r, :], ALU.add, ALU.mult).then_inc(m_d, 1)
                dve.wait_ge(m_d, 8)
                v.tensor_scalar(big[:, :, :, :], big[:, :, :, :], 0.25, None, ALU.max).then_inc(m_d, 1)
                dve.wait_ge(m_d, 9)
                for k, r in enumerate((0, 3)):
                    v.scalar_tensor_tensor(rows[:, :, r, :], sign[:, :, k, :], -1.0, big[:, :, k, :], ALU.add, ALU.mult).then_inc(m_d, 1)
                dve.wait_ge(m_d, 11)


def norm_stats(nc, sem, src, mv, name):
    with ExitStack() as ctx:
        st = ctx.enter_context(nc.sbuf_tensor("st_" + name, [P, NT, 6], F32))
        s_st, s_ch = sem("st_" + name), sem("stch_" + name)
        with nc.Block() as block:
            @block.vector
            def _(dve):
                for t in range(NT):
                    nc.vector.bn_stats(st[:, t, :], src[:, t, :]).then_inc(s_st, 1)
                dve.wait_ge(s_st, NT)
                link = Chain(dve, s_ch, 7 + RSQRT_OPS, 0)
                mean_rstd(nc, link, st, mv)
                link.end()


def top32_attention(nc, a, sem, ps, x, mv, colmod, rows, ident, ones):
    with ExitStack() as ctx:
        sb = lambda n, s, d=F32: ctx.enter_context(nc.sbuf_tensor(n, s, d))
        w, bcol, bvrow = sb("a_w", [P, 3, D]), sb("a_b", [P, 2]), sb("a_bv", [1, D])
        xn, hT = sb("a_xn", [P, TPB, D]), sb("a_hT", [P, S])
        qT, kT, vn = sb("a_qT", [P, S]), sb("a_kT", [P, S]), sb("a_v", [P, TPB, D])
        sc, work = sb("a_sc", [P, TPB, S]), sb("a_work", [P, TPB, S])
        m8, kept = sb("a_m8", [P, TPB, 8]), sb("a_kept", [P, TPB, S])
        den, rden = sb("a_den", [P, TPB]), sb("a_rden", [P, TPB])
        kT2, upd = sb("a_keptT", [P, TPB, S]), sb("a_upd", [P, TPB, D])
        M = Marks(sem, DVE=("a_norm", "a_hTs", "a_top", "a_den", "a_x"), PE=("a_turned", "a_qkv", "a_scores", "a_keptT", "a_out"),
                  ACT=("a_qk", "a_s", "a_kT", "a_vs"))
        a_in, topch, resch, gate = sem("a_in"), sem("a_topch"), sem("a_resch"), sem("a_gate")
        with nc.Block() as block:
            @block.sync
            def _(sp):
                for dst, key in ((w[:, :, :], "a_w"), (bcol[:, :], "a_b"), (bvrow[:, :], "a_bv")):
                    sp.dma_start(dst, a[key]).then_inc(a_in, 16)

            @block.tensor
            def _(pe):
                M.give("PE", pe)
                pe.wait_ge(a_in, 48)

                def turn(b):
                    M.done(pe, "a_norm", b)
                    M.done(pe, "a_hTs", b - 1)
                    for t in range(TPB):
                        mm = nc.tensor.transpose(ps[:, 0, t * P:t * P + P], xn[:, t, :], ident[:, :])
                    M.mark("a_turned", mm)

                def project(b):
                    M.done(pe, "a_hTs", b)
                    M.done(pe, "a_qk", b - 1)
                    M.done(pe, "a_vs", b - 1)
                    for m in range(2):
                        nc.tensor.matmul(ps[:, 1, m * S:m * S + S], w[:, m, :], hT[:, :], start=True, stop=True)
                    for t in range(TPB):
                        nc.tensor.matmul(ps[:, 2, t * P:t * P + P], hT[:, t * P:t * P + P], w[:, 2, :], start=True, stop=False)
                        mm = nc.tensor.matmul(ps[:, 2, t * P:t * P + P], ones[0:1, :], bvrow[0:1, :], start=False, stop=True)
                    M.mark("a_qkv", mm)

                def score(b):
                    M.done(pe, "a_qk", b)
                    M.done(pe, "a_s", b - 1)
                    for t in range(TPB):
                        mm = nc.tensor.matmul(ps[:, 3, t * S:t * S + S], qT[:, t * P:t * P + P], kT[:, :], start=True, stop=True)
                    M.mark("a_scores", mm)

                def turn_kept(b):
                    M.done(pe, "a_top", b)
                    M.done(pe, "a_kT", b - 1)
                    for k in range(TPB):
                        for t in range(TPB):
                            mm = nc.tensor.transpose(ps[:, 4, k * S + t * P:k * S + t * P + P], kept[:, t, k * P:k * P + P], ident[:, :])
                    M.mark("a_keptT", mm)

                def attend(b):
                    M.done(pe, "a_kT", b)
                    M.done(pe, "a_vs", b)
                    M.done(pe, "a_x", b - 1)
                    for t in range(TPB):
                        for k in range(TPB):
                            mm = nc.tensor.matmul(ps[:, 5, t * P:t * P + P], kT2[:, k, t * P:t * P + P], vn[:, k, :],
                                                  start=(k == 0), stop=(k == TPB - 1))
                    M.mark("a_out", mm)

                staged_batches(pe, 1, [(0, turn), (0, project), (0, score), (1, turn_kept), (1, attend)])

            @block.scalar
            def _(act):
                M.give("ACT", act)
                act.wait_ge(a_in, 48)

                def evac_qk(b):
                    M.done(act, "a_qkv", b)
                    M.done(act, "a_scores", b - 1)
                    nc.scalar.activation(qT[:, :], ps[:, 1, 0:S], ACT.Identity, bias=bcol[:, 0:1])
                    M.mark("a_qk", nc.scalar.activation(kT[:, :], ps[:, 1, S:2 * S], ACT.Identity, bias=bcol[:, 1:2]))

                def evac_scores(b):
                    M.done(act, "a_scores", b)
                    M.done(act, "a_top", b - 1)
                    M.mark("a_s", nc.scalar.activation(sc[:, :, :].rearrange("p t s -> p (t s)"), ps[:, 3, :], ACT.Copy))

                def evac_kept(b):
                    M.done(act, "a_keptT", b)
                    M.done(act, "a_out", b - 1)
                    M.mark("a_kT", nc.scalar.activation(kT2[:, :, :].rearrange("p t s -> p (t s)"), ps[:, 4, :], ACT.Copy))

                def evac_v(b):
                    M.done(act, "a_qkv", b)
                    M.done(act, "a_out", b - 1)
                    M.mark("a_vs", nc.scalar.activation(vn[:, :, :].rearrange("p t d -> p (t d)"), ps[:, 2, 0:TPB * D], ACT.Copy))

                staged_batches(act, 1, [(0, evac_qk), (1, evac_kept), (0, evac_scores), (0, evac_v)])

            @block.vector
            def _(dve):
                M.give("DVE", dve)
                dve.wait_ge(a_in, 48)

                def normalise(b):
                    M.done(dve, "a_turned", b - 1)
                    for t in range(TPB):
                        ins = nc.vector.tensor_scalar(xn[:, t, :], x[:, bass.ds(b * TPB + t, 1), :].rearrange("p o d -> p (o d)"),
                                                      mv[:, 1, bass.ds(b * TPB + t, 1)], mv[:, 6, bass.ds(b * TPB + t, 1)],
                                                      ALU.subtract, ALU.mult)
                    M.mark("a_norm", ins)

                def modulate(b):
                    M.done(dve, "a_turned", b)
                    M.done(dve, "a_qkv", b - 1)
                    M.mark("a_hTs", nc.vector.tensor_scalar(hT[:, :], ps[:, 0, 0:S], colmod[:, 1, bass.ds(b, 1)],
                                                            colmod[:, 0, bass.ds(b, 1)], ALU.mult, ALU.add))

                def top(b):
                    link = Chain(dve, topch, 2 * TOPK // 8 + 1, b, gate)
                    M.done(dve, "a_s", b)
                    M.done(dve, "a_keptT", b - 1)
                    dve.sem_inc(gate, 1)
                    for r in range(TOPK // 8):
                        src = sc if r == 0 else work
                        for t in range(TPB):
                            ins = nc.vector.max(m8[:, t, :], src[:, t, :])
                        link(ins)
                        for t in range(TPB):
                            ins = nc.vector.match_replace(work[:, t, :], m8[:, t, :], src[:, t, :], NEG)
                        link(ins)
                    for t in range(TPB):
                        ins = nc.vector.scalar_tensor_tensor(kept[:, t, :], work[:, t, :], NEG, sc[:, t, :], ALU.is_equal, ALU.mult,
                                                             accum_out=den[:, t:t + 1])
                    M.mark("a_top", ins)
                    M.done(dve, "a_top", b)
                    link(nc.vector.tensor_scalar(den[:, :], den[:, :], 1e-10, None, ALU.add))
                    nc.vector.reciprocal(rden[:, :], den[:, :]).then_inc(M.s["a_den"], 1)
                    link.end()

                def residual(b):
                    link = Chain(dve, resch, 1, b)
                    M.done(dve, "a_out", b)
                    M.done(dve, "a_den", b)
                    for t in range(TPB):
                        ins = nc.vector.scalar_tensor_tensor(upd[:, t, :], ps[:, 5, t * P:t * P + P], rden[:, t:t + 1],
                                                             rows[:, bass.ds(b, 1), 0, :].rearrange("p o d -> p (o d)"), ALU.mult, ALU.mult)
                    link(ins)
                    xt = x[:, bass.ds(b * TPB, TPB), :]
                    M.mark("a_x", nc.vector.tensor_tensor(xt, xt, upd[:, :, :], ALU.add))
                    M.done(dve, "a_x", b)

                staged_batches(dve, 1, [(0, normalise), (0, modulate), (1, residual), (0, top)])


def into_y(nc, sem, x, y, mv, rows):
    s = sem("into_y")
    with nc.Block() as block:
        @block.vector
        def _(dve):
            for t in range(NT):
                nc.vector.tensor_scalar(y[:, t, :], x[:, t, :], mv[:, 1, t:t + 1], mv[:, 6, t:t + 1], ALU.subtract, ALU.mult).then_inc(s, 1)
            dve.wait_ge(s, NT)
            yv = y[:, :, :].rearrange("p (b t) d -> p b t d", t=TPB)
            nc.vector.tensor_tensor(yv, yv, view(rows, 0, P, 2 * D, [[4 * D, B], [0, TPB], [1, D]]), ALU.mult).then_inc(s, 1)
            dve.wait_ge(s, NT + 1)
            nc.vector.tensor_tensor(yv, yv, view(rows, 0, P, D, [[4 * D, B], [0, TPB], [1, D]]), ALU.add).then_inc(s, 1)
            dve.wait_ge(s, NT + 2)


def add_gated(nc, sem, x, y, rows):
    s = sem("add_y")
    with nc.Block() as block:
        @block.vector
        def _(dve):
            yv = y[:, :, :].rearrange("p (b t) d -> p b t d", t=TPB)
            nc.vector.tensor_tensor(yv, yv, view(rows, 0, P, 3 * D, [[4 * D, B], [0, TPB], [1, D]]), ALU.mult).then_inc(s, 1)
            dve.wait_ge(s, 1)
            nc.vector.tensor_tensor(x[:, :, :], x[:, :, :], y[:, :, :], ALU.add).then_inc(s, 1)
            dve.wait_ge(s, 2)


H3, D3, W3 = 16, 8, 16
G3 = 8
PAIRS = S // (2 * G3)
BLKS = S // G3


def third_order_attention(nc, a, sem, ps, x, mv, colmod, rows, ident, identb):
    with ExitStack() as ctx:
        sb = lambda n, s, d=F32: ctx.enter_context(nc.sbuf_tensor(n, s, d))
        pad = W3 - 1
        w = sb("d_w", [P, 5, D])
        bd = sb("d_bd", [P, H3])
        mask_in, mask = sb("d_mask_in", [P, 3, 3 * P]), sb("d_mask", [P, 3, 3 * P], BF16)
        lnrow = sb("d_lnrow", [P, 2, D])
        xn, hT = sb("d_xn", [P, TPB, D]), sb("d_hT", [P, S])
        QT, KT, KpT, VT = sb("d_QT", [P, S]), sb("d_KT", [P, pad + S]), sb("d_KpT", [P, S]), sb("d_VT", [P, pad + S])
        U = sb("d_U", [P, S, W3])
        KBD, VBD = sb("d_KBD", [P, 2 + BLKS, P]), sb("d_VBD", [P, 2 + BLKS, P])
        VTrep = sb("d_VTrep", [P, BLKS, H3, G3])
        onesBD = sb("d_onesBD", [P, P])
        mx, mxh = sb("d_mx", [P, 2, 2, G3]), sb("d_mxh", [2 * G3, 2, H3])
        mxr = sb("d_mxr", [2 * G3, 2, H3, G3])
        hi, lo = sb("d_hi", [P, 2, 2 * G3], BF16), sb("d_lo", [P, 2, 2 * G3], BF16)
        pr = sb("d_pr", [P, 2, 2, 3 * P])
        psum = sb("d_psum", [P, 2, 2, P])
        wv = sb("d_wv", [P, 2, 2 * P])
        zs, dn, rdn = sb("d_zs", [P, 2, 2 * G3]), sb("d_dn", [P, 2, 2 * G3]), sb("d_rdn", [P, 2, 2 * G3])
        ZT = sb("d_ZT", [P, S])
        st, mv2 = sb("d_st", [P, TPB, 6]), sb("d_mv", [P, 8, TPB])
        nrm = sb("d_nrm", [P, TPB, D])
        M = Marks(sem,
                  DVE=("d_norm", "d_hTs", "d_mx", "d_mxh", "d_hl", "d_z", "d_vbd", "d_x", "d_zd"),
                  PE=("d_turned", "d_proj", "d_vt", "d_a", "d_t", "d_r", "d_sub", "d_w_", "d_o"),
                  ACT=("d_pj", "d_exp"), POOL=("d_ukbd", "d_ps", "d_psa"))
        d_in, once, lnch, z_ch, h_ch, r_ch, v_ch = (sem(n) for n in ("d_in", "d_once", "d_lnch", "d_zch", "d_hch", "d_rch", "d_vch"))
        with nc.Block() as block:
            @block.sync
            def _(sp):
                for dst, key in ((w[:, :, :], "d_w"), (bd[:, :], "d_bd"), (mask_in[:, :, :], "d_mask"), (lnrow[:, :, :], "d_ln")):
                    sp.dma_start(dst, a[key]).then_inc(d_in, 16)

            @block.vector
            def _(dve):
                M.give("DVE", dve)
                v = nc.vector
                for t in (KT, VT):
                    v.memset(t[:, 0:pad], 0.0).then_inc(once, 1)
                for t in (KBD, VBD):
                    v.memset(t[:, 0:2, :], 0.0).then_inc(once, 1)
                dve.wait_ge(d_in, 64)
                v.tensor_copy(mask[:, :, :], mask_in[:, :, :]).then_inc(once, 1)
                v.tensor_copy(onesBD[:, :].rearrange("p (h d) -> p h d", d=D3), view(bd, 0, P, 0, [[1, H3], [0, D3]])).then_inc(once, 1)
                dve.wait_ge(once, 6)

            @block.tensor
            def _(pe):
                M.give("PE", pe)

            @block.scalar
            def _(act):
                M.give("ACT", act)

            @block.gpsimd
            def _(pool):
                M.give("POOL", pool)

        def groups(gp):
            return [2 * gp, 2 * gp + 1]

        with nc.Block() as block:
            @block.tensor
            def _(pe):
                with pe.Fori(0, B) as b:
                    M.done(pe, "d_norm", b)
                    M.done(pe, "d_hTs", b - 1)
                    for t in range(TPB):
                        mm = nc.tensor.transpose(ps[:, 0, t * P:t * P + P], xn[:, t, :], ident[:, :])
                    M.mark("d_turned", mm)
                    M.done(pe, "d_hTs", b)
                    M.done(pe, "d_exp", PAIRS * b - 1)
                    for m in range(4):
                        mm = nc.tensor.matmul(ps[:, 1 + m // 2, (m % 2) * S:(m % 2) * S + S], w[:, m, :], hT[:, :], start=True, stop=True)
                    M.mark("d_proj", mm)
                    M.done(pe, "d_pj", b)
                    for q in range(BLKS // 4):
                        M.done(pe, "d_vbd", (BLKS // 4) * b + q - 2)
                        for k in range(4):
                            mm = nc.tensor.transpose(ps[:, 5 + q % 2, k * P:k * P + P],
                                                     VTrep[:, 4 * q + k, :, :].rearrange("p h s -> p (h s)"), ident[:, :])
                        M.mark("d_vt", mm)
                    M.done(pe, "d_ukbd", b)
                    M.done(pe, "d_vbd", (BLKS // 4) * b + BLKS // 4 - 1)

                    def score(gp):
                        u = PAIRS * b + gp
                        M.done(pe, "d_exp", u - 2)
                        for gi, g in enumerate(groups(gp)):
                            bank = 1 + 2 * (gp % 2) + gi
                            nc.tensor.matmul(ps[:, bank, 0:3 * P], identb[:, :], mask[:, min(g, 2), :], start=True, stop=False,
                                             skip_group_check=True)
                            for k in range(3):
                                mm = nc.tensor.matmul(ps[:, bank, k * P:k * P + P], KBD[:, g + k, :],
                                                      U[:, g * G3:g * G3 + G3, :].rearrange("p s j -> p (s j)"),
                                                      start=False, stop=(k == 2), skip_group_check=True)
                        M.mark("d_a", mm)

                    def turn_max(gp):
                        u = PAIRS * b + gp
                        M.done(pe, "d_mx", u)
                        M.done(pe, "d_hl", u - 1)
                        M.mark("d_t", nc.tensor.transpose(ps[0:2 * G3, 0, 0:P], mx[:, gp % 2, :, :].rearrange("p g s -> p (g s)"), ident[:, :]))

                    def spread_max(gp):
                        u = PAIRS * b + gp
                        M.done(pe, "d_mxh", u)
                        M.mark("d_r", nc.tensor.matmul(ps[:, 0, 128:128 + 2 * G3], mxr[:, gp % 2, :, :].rearrange("p h s -> p (h s)"),
                                                       ident[0:2 * G3, 0:2 * G3], start=True, stop=True))

                    def subtract_max(gp):
                        u = PAIRS * b + gp
                        M.done(pe, "d_hl", u)
                        for gi in range(2):
                            for part in (hi, lo):
                                mm = nc.tensor.matmul(ps[:, 1 + 2 * (gp % 2) + gi, 0:3 * P], identb[:, :],
                                                      view(part, 0, P, (gp % 2) * 2 * G3 + gi * G3, [[0, 3], [1, G3], [0, W3]]),
                                                      start=False, stop=True, skip_group_check=True)
                        M.mark("d_sub", mm)

                    def weigh(gp):
                        u = PAIRS * b + gp
                        M.done(pe, "d_exp", u)
                        M.done(pe, "d_ps", u)
                        M.done(pe, "d_zd", u - 1)
                        for gi, g in enumerate(groups(gp)):
                            for k in range(3):
                                nc.tensor.matmul(ps[:, 5, gi * P:gi * P + P], VBD[:, g + k, :],
                                                 pr[:, gp % 2, gi, k * P:k * P + P], start=(k == 0), stop=(k == 2))
                        mm = nc.tensor.matmul(ps[:, 6, 0:2 * P], onesBD[:, :], psum[:, gp % 2, :, :].rearrange("p g n -> p (g n)"),
                                              start=True, stop=True)
                        M.mark("d_w_", mm)

                    for s in range(PAIRS + 2):
                        if 1 <= s <= PAIRS:
                            turn_max(s - 1)
                        if s < PAIRS:
                            score(s)
                        if 1 <= s <= PAIRS:
                            spread_max(s - 1)
                        if s >= 2:
                            weigh(s - 2)
                        if 1 <= s <= PAIRS:
                            subtract_max(s - 1)
                    M.done(pe, "d_z", PAIRS * b + PAIRS - 1)
                    M.done(pe, "d_x", b - 1)
                    for t in range(TPB):
                        nc.tensor.matmul(ps[:, 7, t * P:t * P + P], ZT[:, t * P:t * P + P], w[:, 4, :], start=True, stop=False)
                        mm = nc.tensor.matmul(ps[:, 7, t * P:t * P + P], hT[:, t * P:t * P + P], ident[:, :], start=False, stop=True)
                    M.mark("d_o", mm)

            @block.scalar
            def _(act):
                with act.Fori(0, B) as b:
                    M.done(act, "d_proj", b)
                    M.done(act, "d_z", PAIRS * b - 1)
                    nc.scalar.activation(QT[:, :], ps[:, 1, 0:S], ACT.Copy, scale=float(D3) ** -0.5)
                    nc.scalar.activation(KT[:, pad:pad + S], ps[:, 1, S:2 * S], ACT.Copy)
                    nc.scalar.activation(KpT[:, :], ps[:, 2, 0:S], ACT.Copy)
                    nc.scalar.activation(VT[:, pad:pad + S], ps[:, 2, S:2 * S], ACT.Copy).then_inc(v_ch, 1)
                    act.wait_ge(v_ch, b + 1)
                    M.mark("d_pj", nc.scalar.activation(VTrep[:, :, :, :], view(VT, 0, P, pad, [[G3, BLKS], [0, H3], [1, G3]]), ACT.Copy))

                    for gp in range(PAIRS):
                        u = PAIRS * b + gp
                        M.done(act, "d_sub", u)
                        M.done(act, "d_w_", u - 2)
                        M.done(act, "d_ps", u - 2)
                        bank = 1 + 2 * (gp % 2)
                        M.mark("d_exp", nc.scalar.activation(pr[:, gp % 2, :, :], ps[:, bank:bank + 2, 0:3 * P], ACT.Exp))

            @block.gpsimd
            def _(pool):
                with pool.Fori(0, B) as b:
                    M.done(pool, "d_pj", b)
                    M.done(pool, "d_w_", PAIRS * b - 1)
                    nc.gpsimd.tensor_tensor(view(KBD, 0, P, 2 * P, [[P, BLKS], [G3, H3], [1, G3]]),
                                            view(KpT, 0, P, 0, [[G3, BLKS], [0, H3], [1, G3]]),
                                            view(bd, 0, P, 0, [[0, BLKS], [1, H3], [0, G3]]), ALU.mult)
                    M.mark("d_ukbd", nc.gpsimd.tensor_tensor(U[:, :, :], view(QT, 0, P, 0, [[1, S], [0, W3]]),
                                                             view(KT, 0, P, 0, [[1, S], [1, W3]]), ALU.mult))
                    for gp in range(PAIRS):
                        u = PAIRS * b + gp
                        M.done(pool, "d_exp", u)
                        M.done(pool, "d_w_", u - 2)
                        M.mark("d_psa", nc.gpsimd.tensor_tensor(psum[:, gp % 2, :, :], pr[:, gp % 2, :, 0:P], pr[:, gp % 2, :, P:2 * P], ALU.add))
                        M.done(pool, "d_psa", u)
                        M.mark("d_ps", nc.gpsimd.tensor_tensor(psum[:, gp % 2, :, :], psum[:, gp % 2, :, :], pr[:, gp % 2, :, 2 * P:3 * P], ALU.add))

            @block.vector
            def _(dve):
                v = nc.vector
                with dve.Fori(0, B) as b:
                    M.done(dve, "d_turned", b - 1)
                    for t in range(TPB):
                        ins = v.tensor_scalar(xn[:, t, :], x[:, bass.ds(b * TPB + t, 1), :].rearrange("p o d -> p (o d)"),
                                              mv[:, 1, bass.ds(b * TPB + t, 1)], mv[:, 6, bass.ds(b * TPB + t, 1)],
                                              ALU.subtract, ALU.mult)
                    M.mark("d_norm", ins)
                    M.done(dve, "d_turned", b)
                    M.done(dve, "d_o", b - 1)
                    M.mark("d_hTs", v.tensor_scalar(hT[:, :], ps[:, 0, 0:S], colmod[:, 1, bass.ds(b, 1)],
                                                    colmod[:, 0, bass.ds(b, 1)], ALU.mult, ALU.add))
                    for q in range(BLKS // 4):
                        M.done(dve, "d_vt", (BLKS // 4) * b + q)
                        M.mark("d_vbd", v.tensor_tensor(view(VBD, 0, P, (2 + 4 * q) * P, [[P, 4], [D3, H3], [1, D3]]),
                                                        view(ps, 0, P, (5 + q % 2) * 512, [[P, 4], [D3, H3], [1, D3]]),
                                                        view(bd, 0, P, 0, [[0, 4], [1, H3], [0, D3]]), ALU.mult))

                    def maxima(gp):
                        u = PAIRS * b + gp
                        M.done(dve, "d_a", u)
                        M.done(dve, "d_t", u - 2)
                        for gi in range(2):
                            ins = v.tensor_reduce(mx[:, gp % 2, gi, :], view(ps, 0, P, (1 + 2 * (gp % 2) + gi) * 512, [[W3, G3], [P, 3], [1, W3]]),
                                                  mybir.AxisListType.XY, ALU.max)
                        M.mark("d_mx", ins)

                    def head_maxima(gp):
                        u = PAIRS * b + gp
                        M.done(dve, "d_t", u)
                        M.done(dve, "d_r", u - 2)
                        link = Chain(dve, r_ch, 1, u)
                        link(v.tensor_reduce(mxh[:, gp % 2, :], view(ps, 0, 2 * G3, 0, [[G3, H3], [1, G3]]), AX, ALU.max))
                        M.mark("d_mxh", v.tensor_copy(mxr[:, gp % 2, :, :], view(mxh, 0, 2 * G3, (gp % 2) * H3, [[1, H3], [0, G3]])))

                    def split_max(gp):
                        u = PAIRS * b + gp
                        link = Chain(dve, h_ch, 1, u)
                        M.done(dve, "d_r", u)
                        M.done(dve, "d_sub", u - 2)
                        src = ps[:, 0, 128:128 + 2 * G3]
                        link(v.tensor_scalar(hi[:, gp % 2, :], src, -1.0, None, ALU.mult))
                        M.mark("d_hl", v.scalar_tensor_tensor(lo[:, gp % 2, :], src, -1.0, hi[:, gp % 2, :], ALU.mult, ALU.subtract))

                    def combine(gp):
                        u = PAIRS * b + gp
                        link = Chain(dve, z_ch, 2, u)
                        M.done(dve, "d_w_", u)
                        s0, q = 2 * G3 * gp, gp % 2
                        v.tensor_reduce(dn[:, q, :], view(ps, 0, P, 6 * 512, [[W3, 2 * G3], [1, W3]]), AX, ALU.add)
                        M.mark("d_zd", v.tensor_tensor(wv[:, q, :].rearrange("p (s j) -> p s j", j=W3),
                                                       view(ps, 0, P, 5 * 512, [[W3, 2 * G3], [1, W3]]),
                                                       view(VT, 0, P, s0, [[1, 2 * G3], [1, W3]]), ALU.mult))
                        M.done(dve, "d_zd", u)
                        v.reciprocal(rdn[:, q, :], dn[:, q, :])
                        link(v.tensor_reduce(zs[:, q, :], wv[:, q, :].rearrange("p (s j) -> p s j", j=W3), AX, ALU.add))
                        link(v.tensor_tensor(ZT[:, s0:s0 + 2 * G3], zs[:, q, :], rdn[:, q, :], ALU.mult))
                        v.sem_inc(M.s["d_z"], 1)

                    for s in range(PAIRS + 2):
                        if 1 <= s <= PAIRS:
                            head_maxima(s - 1)
                        if s < PAIRS:
                            maxima(s)
                        if 1 <= s <= PAIRS:
                            split_max(s - 1)
                        if s >= 2:
                            combine(s - 2)
                    link = Chain(dve, lnch, 1 + 7 + RSQRT_OPS + 4, b)
                    M.done(dve, "d_o", b)
                    v.bn_stats(st[:, 0, :], ps[:, 7, 0:P])
                    link(v.bn_stats(st[:, 1, :], ps[:, 7, P:2 * P]))
                    mean_rstd(nc, link, st, mv2)
                    for t in range(TPB):
                        ins = v.tensor_scalar(nrm[:, t, :], ps[:, 7, t * P:t * P + P], mv2[:, 1, t:t + 1], mv2[:, 6, t:t + 1], ALU.subtract, ALU.mult)
                    link(ins)
                    link(v.tensor_tensor(nrm[:, :, :], nrm[:, :, :], view(lnrow, 0, P, 0, [[0, TPB], [1, D]]), ALU.mult))
                    link(v.tensor_tensor(nrm[:, :, :], nrm[:, :, :], view(lnrow, 0, P, D, [[0, TPB], [1, D]]), ALU.add))
                    for t in range(TPB):
                        ins = v.tensor_tensor(nrm[:, t, :], nrm[:, t, :], rows[:, bass.ds(b, 1), 0, :].rearrange("p o d -> p (o d)"), ALU.mult)
                    link(ins)
                    link.end()
                    xt = x[:, bass.ds(b * TPB, TPB), :]
                    M.mark("d_x", v.tensor_tensor(xt, xt, nrm[:, :, :], ALU.add))
                    M.done(dve, "d_x", b)


EXPERTS, DI = 8, 512
KEEP = max(4, -(-B * S * 2 // EXPERTS))
CHUNK = 4


def expert_choice(nc, a, sem, ps, x, mv, colmod, rows, ident, ones):
    with ExitStack() as ctx:
        sb = lambda n, s, d=F32: ctx.enter_context(nc.sbuf_tensor(n, s, d))
        wr, w1, w2 = sb("e_wr", [P, EXPERTS]), sb("e_w1", [P, EXPERTS, DI]), sb("e_w2", [P, EXPERTS, DI // P, D])
        b1, b2 = sb("e_b1", [P, EXPERTS, DI // P]), sb("e_b2", [CHUNK * EXPERTS, CHUNK, D])
        below = sb("e_below", [P, P])
        xn, hT, hall = sb("e_xn", [P, TPB, D]), sb("e_hT", [P, S]), sb("e_hall", [P, NT * P])
        G, GE = sb("e_G", [P, NT, EXPERTS]), sb("e_cmp", [P, NT, EXPERTS])
        eq, rank = sb("e_eq", [P, NT, EXPERTS]), sb("e_rank", [P, NT, EXPERTS])
        tot, tot2 = sb("e_tot", [P, NT, EXPERTS]), sb("e_tot2", [P, NT, EXPERTS])
        small = sb("e_small", [P, NT])
        cnt, need, okf = sb("e_cnt", [P, EXPERTS]), sb("e_need", [P, EXPERTS]), sb("e_ok", [P, EXPERTS])
        thr, cand, bit, oki = (sb(n, [P, EXPERTS], I32) for n in ("e_thr", "e_cand", "e_bit", "e_oki"))
        g4, gT = sb("e_g4", [P, CHUNK * EXPERTS]), sb("e_gT", [CHUNK * EXPERTS, P])
        hid = sb("e_hid", [P, 2, DI // P, CHUNK * P])
        acc = sb("e_acc", [P, CHUNK, D])
        M = Marks(sem, DVE=("e_norm", "e_hTs", "e_cmpd", "e_g4s", "e_gTs", "e_acc", "e_x", "e_b"),
                  PE=("e_turned", "e_lg", "e_count", "e_gt", "e_b2s", "e_h", "e_y"), ACT=("e_log", "e_gelu", "e_copy"))
        e_in, ch, sch, bch, ach = (sem(n) for n in ("e_in", "e_ch", "e_sch", "e_bch", "e_ach"))
        loads = ((wr[:, :], "e_wr"), (w1[:, :, :], "e_w1"), (w2[:, :, :, :], "e_w2"), (b1[:, :, :], "e_b1"),
                 (b2[:, :, :], "e_b2"), (below[:, :], "e_below"))
        with nc.Block() as block:
            @block.sync
            def _(sp):
                for dst, key in loads:
                    sp.dma_start(dst, a[key]).then_inc(e_in, 16)

            @block.vector
            def _(dve):
                M.give("DVE", dve)
                dve.wait_ge(e_in, 16 * len(loads))
                v = nc.vector
                with dve.Fori(0, B) as b:
                    M.done(dve, "e_turned", b - 1)
                    for t in range(TPB):
                        ins = v.tensor_scalar(xn[:, t, :], x[:, bass.ds(b * TPB + t, 1), :].rearrange("p o d -> p (o d)"),
                                              mv[:, 1, bass.ds(b * TPB + t, 1)], mv[:, 6, bass.ds(b * TPB + t, 1)],
                                              ALU.subtract, ALU.mult)
                    M.mark("e_norm", ins)
                    M.done(dve, "e_turned", b)
                    M.done(dve, "e_lg", b - 1)
                    M.done(dve, "e_copy", b - 1)
                    M.mark("e_hTs", v.tensor_scalar(hT[:, :], ps[:, 0, 0:S], colmod[:, 4, bass.ds(b, 1)],
                                                    colmod[:, 3, bass.ds(b, 1)], ALU.mult, ALU.add))
                link = Chain(dve, sch, 5, 0)
                dve.wait_ge(M.s["e_log"], B + CR)
                bc = lambda t: view(t, 0, P, 0, [[1, NT], [0, EXPERTS]])
                link(v.tensor_reduce(small[:, :], G[:, :, :], AX, ALU.max))
                link(v.tensor_tensor(G[:, :, :], G[:, :, :], bc(small), ALU.subtract))
                dve.wait_ge(M.s["e_log"], B + 1 + CR)
                link(v.tensor_reduce(small[:, :], G[:, :, :], AX, ALU.add))
                link(v.reciprocal(small[:, :], small[:, :]))
                link(v.tensor_tensor(G[:, :, :], G[:, :, :], bc(small), ALU.mult))
                link.end()

            @block.tensor
            def _(pe):
                M.give("PE", pe)
                pe.wait_ge(e_in, 16 * len(loads))
                with pe.Fori(0, B) as b:
                    M.done(pe, "e_norm", b)
                    M.done(pe, "e_hTs", b - 1)
                    for t in range(TPB):
                        mm = nc.tensor.transpose(ps[:, 0, t * P:t * P + P], xn[:, t, :], ident[:, :])
                    M.mark("e_turned", mm)
                    M.done(pe, "e_hTs", b)
                    M.done(pe, "e_log", b - 1)
                    for t in range(TPB):
                        mm = nc.tensor.matmul(ps[:, 1, t * EXPERTS:(t + 1) * EXPERTS], hT[:, t * P:t * P + P], wr[:, :], start=True, stop=True)
                    M.mark("e_lg", mm)

            @block.scalar
            def _(act):
                M.give("ACT", act)
                with act.Fori(0, B) as b:
                    M.done(act, "e_hTs", b)
                    M.mark("e_copy", nc.scalar.activation(hall[:, bass.ds(b * S, S)], hT[:, :], ACT.Copy))
                    M.done(act, "e_lg", b)
                    M.mark("e_log", nc.scalar.activation(G[:, bass.ds(b * TPB, TPB), :].rearrange("p t e -> p (t e)"),
                                                         ps[:, 1, 0:TPB * EXPERTS], ACT.Copy))
                act.wait_ge(sch, 2)
                M.mark("e_log", nc.scalar.activation(G[:, :, :], G[:, :, :], ACT.Exp))

        BITS = 30
        with nc.Block() as block:
            @block.vector
            def _(dve):
                v = nc.vector
                over = lambda t: view(t, 0, P, 0, [[0, NT], [1, EXPERTS]])
                link = Chain(dve, ch, 2, 0)
                link(v.memset(thr[:, :], 0))
                link(v.memset(bit[:, :], 1 << (BITS - 1)))
                with dve.Fori(0, BITS) as i:
                    link = Chain(dve, bch, 6, i)
                    link(v.tensor_tensor(cand[:, :], thr[:, :], bit[:, :], ALU.bitwise_or))
                    link(v.tensor_tensor(GE[:, :, :], G[:, :, :], over(cand).bitcast(F32), ALU.is_ge))
                    M.mark("e_cmpd", v.tensor_reduce(cnt[:, :], GE[:, :, :].rearrange("p t e -> p e t"), AX, ALU.add))
                    M.done(dve, "e_count", i)
                    link(v.tensor_scalar(oki[:, :], ps[:, 0, 0:EXPERTS], float(KEEP), None, ALU.is_ge))
                    link(v.tensor_tensor(oki[:, :], oki[:, :], bit[:, :], ALU.mult))
                    link(v.tensor_tensor(thr[:, :], thr[:, :], oki[:, :], ALU.bitwise_or))
                    link(v.tensor_scalar(bit[:, :], bit[:, :], 1, None, ALU.logical_shift_right))
                    link.end()
                link = Chain(dve, ach, 6 + 5 + 5, 0)
                thf = view(thr, 0, P, 0, [[0, NT], [1, EXPERTS]]).bitcast(F32)
                link(v.tensor_tensor(GE[:, :, :], G[:, :, :], thf, ALU.is_gt))
                link(v.tensor_tensor(eq[:, :, :], G[:, :, :], thf, ALU.is_equal))
                link(v.tensor_reduce(cnt[:, :], GE[:, :, :].rearrange("p t e -> p e t"), AX, ALU.add))
                v.sem_inc(M.s["e_cmpd"], 1)
                M.done(dve, "e_count", BITS)
                link(v.tensor_scalar(need[:, :], ps[:, 0, 0:EXPERTS], -1.0, float(KEEP), ALU.mult, ALU.add))
                link(v.tensor_copy(rank[:, :, :].rearrange("p t e -> p (t e)"), ps[:, 1, 0:NT * EXPERTS]))
                link(v.tensor_copy(tot[:, :, :].rearrange("p t e -> p (t e)"), ps[:, 2, 0:NT * EXPERTS]))
                src, dst, k = tot, tot2, 1
                while k < NT:
                    v.tensor_copy(dst[:, 0:k, :], src[:, 0:k, :])
                    link(v.tensor_tensor(dst[:, k:NT, :], src[:, k:NT, :], src[:, 0:NT - k, :], ALU.add))
                    src, dst, k = dst, src, 2 * k
                link(v.tensor_tensor(rank[:, 1:NT, :], rank[:, 1:NT, :], src[:, 0:NT - 1, :], ALU.add))
                link(v.tensor_tensor(rank[:, :, :], rank[:, :, :], view(need, 0, P, 0, [[0, NT], [1, EXPERTS]]), ALU.is_lt))
                link(v.tensor_tensor(eq[:, :, :], eq[:, :, :], rank[:, :, :], ALU.mult))
                link(v.tensor_tensor(GE[:, :, :], GE[:, :, :], eq[:, :, :], ALU.add))
                link(v.tensor_tensor(G[:, :, :], G[:, :, :], GE[:, :, :], ALU.mult))
                link.end()

            @block.tensor
            def _(pe):
                with pe.Fori(0, BITS) as i:
                    M.done(pe, "e_cmpd", i)
                    M.mark("e_count", nc.tensor.matmul(ps[:, 0, 0:EXPERTS], ones[:, :], cnt[:, :], start=True, stop=True))
                M.done(pe, "e_cmpd", BITS)
                nc.tensor.matmul(ps[:, 1, 0:NT * EXPERTS], below[:, :], eq[:, :, :].rearrange("p t e -> p (t e)"), start=True, stop=True)
                nc.tensor.matmul(ps[:, 2, 0:NT * EXPERTS], ones[:, :], eq[:, :, :].rearrange("p t e -> p (t e)"), start=True, stop=True)
                M.mark("e_count", nc.tensor.matmul(ps[:, 0, 0:EXPERTS], ones[:, :], cnt[:, :], start=True, stop=True))

        NCH = NT // CHUNK
        with nc.Block() as block:
            @block.tensor
            def _(pe):
                with pe.Fori(0, NCH) as c:
                    M.done(pe, "e_g4s", c)
                    M.mark("e_gt", nc.tensor.transpose(ps[0:CHUNK * EXPERTS, 7, 0:P], g4[:, :], ident[:, :]))

                    def up(e):
                        u = c * EXPERTS + e
                        M.done(pe, "e_gelu", u - 1)
                        for k in range(DI // P):
                            mm = nc.tensor.matmul(ps[:, k, :], w1[:, e, k * P:k * P + P], hall[:, bass.ds(c * (CHUNK * P), CHUNK * P)], start=True, stop=True)
                        M.mark("e_h", mm)

                    def down(e):
                        u = c * EXPERTS + e
                        M.done(pe, "e_gelu", u)
                        M.done(pe, "e_acc", u - 2)
                        for t in range(CHUNK):
                            for k in range(DI // P):
                                mm = nc.tensor.matmul(ps[:, 4 + e % 2, t * P:t * P + P], hid[:, e % 2, k, t * P:t * P + P], w2[:, e, k, :],
                                                      start=(k == 0), stop=(k == DI // P - 1))
                        M.mark("e_y", mm)
                    up(0)
                    M.done(pe, "e_gTs", c)
                    M.done(pe, "e_b", c - 1)
                    for t in range(CHUNK):
                        mm = nc.tensor.matmul(ps[:, 6, t * P:t * P + P], gT[:, :], b2[:, t, :], start=True, stop=True)
                    M.mark("e_b2s", mm)
                    for e in range(EXPERTS):
                        if e + 1 < EXPERTS:
                            up(e + 1)
                        down(e)

            @block.scalar
            def _(act):
                with act.Fori(0, NCH) as c:
                    for e in range(EXPERTS):
                        u = c * EXPERTS + e
                        M.done(act, "e_h", u)
                        M.done(act, "e_y", u - 2)
                        for k in range(DI // P):
                            ins = nc.scalar.activation(hid[:, e % 2, k, :], ps[:, k, :], ACT.Gelu, bias=b1[:, e, k:k + 1])
                        M.mark("e_gelu", ins)

            @block.vector
            def _(dve):
                v = nc.vector
                with dve.Fori(0, NCH) as c:
                    M.done(dve, "e_x", c - 1)
                    M.done(dve, "e_gt", c - 1)
                    M.mark("e_g4s", v.tensor_copy(g4[:, :].rearrange("p (t e) -> p t e", e=EXPERTS), G[:, bass.ds(c * CHUNK, CHUNK), :]))
                    M.done(dve, "e_gt", c)
                    M.done(dve, "e_b2s", c - 1)
                    M.mark("e_gTs", v.tensor_copy(gT[:, :], ps[0:CHUNK * EXPERTS, 7, 0:P]))
                    M.done(dve, "e_b2s", c)
                    M.mark("e_b", v.tensor_copy(acc[:, :, :].rearrange("p t d -> p (t d)"), ps[:, 6, :]))
                    M.done(dve, "e_b", c)
                    for e in range(EXPERTS):
                        u = c * EXPERTS + e
                        M.done(dve, "e_y", u)
                        for t in range(CHUNK):
                            ins = v.scalar_tensor_tensor(acc[:, t, :], ps[:, 4 + e % 2, t * P:t * P + P], g4[:, t * EXPERTS + e:t * EXPERTS + e + 1],
                                                         acc[:, t, :], ALU.mult, ALU.add)
                        M.mark("e_acc", ins)
                        M.done(dve, "e_acc", u)
                    for t in range(CHUNK):
                        bt = c * (CHUNK // TPB) + t // TPB
                        ins = v.tensor_tensor(acc[:, t, :], acc[:, t, :], rows[:, bass.ds(bt, 1), 3, :].rearrange("p o d -> p (o d)"), ALU.mult)
                    ins.then_inc(bch, 1)
                    dve.wait_ge(bch, 6 * BITS + c + 1)
                    xt = x[:, bass.ds(c * CHUNK, CHUNK), :]
                    M.mark("e_x", v.tensor_tensor(xt, xt, acc[:, :, :], ALU.add))
                    M.done(dve, "e_x", c)


def local_transformer(nc, a, sem, ps, y, ident, identb, ones):
    with ExitStack() as ctx:
        def sb(name, shape, dt=F32):
            return ctx.enter_context(nc.sbuf_tensor(name, shape, dt))

        wqkv = sb("wqkv", [P, 3 * INNER])
        wo = sb("wo", [P, HEADS // 2, D])
        w1 = sb("w1", [P, 2 * FF])
        w2 = sb("w2", [P, len(FFC), D])
        ffcols = sb("ffcols", [P, 8])
        b2row = sb("b2row", [1, D])
        scales = sb("scales", [P, 4, DH])
        tab0 = sb("tab0", [P, TPB, 4, DH])
        tab = sb("tab", [P, TPB, 4, DH])
        yl = sb("yl", [P, TPB, D])
        hT = sb("hT", [P, S])
        raw = sb("raw", [P, 2, H2, DH])
        sq = sb("sq", [P, 2, H2, DH])
        t1 = sb("t1", [P, 2, H2, DH])
        t2 = sb("t2", [P, 2, H2, DH])
        qkn = sb("qkn", [P, 2, H2, DH])
        ss = sb("ss", [P, 2 * H2])
        rn = sb("rn", [P, 2 * H2])
        rtmp = sb("rtmp", [P, 2 * H2])
        qT = sb("qT", [P, H2 // 2, P])
        kT = sb("kT", [P, HEADS // 2, WIN + S])
        V = sb("V", [P, TPB, INNER])
        Vp = sb("Vp", [P, TPB, INNER])
        maskb = sb("maskb", [P, 2, H2 // 2 * 2 * WIN], BF16)
        rowmax = sb("rowmax", [P, H2])
        sim = sb("sim", [P, H2, 2 * WIN])
        prob = sb("prob", [P, H2, 2 * WIN])
        rowsum = sb("rowsum", [P, 2, H2])
        rsum = sb("rsum", [P, 2, H2])
        pT = sb("pT", [P, H2, 2, WIN])
        on = sb("on", [P, H2 // 2, P])
        oT = sb("oT", [P, H2 // 2, P])
        yf = sb("yf", [P, TPB, D])
        st = sb("st", [P, TPB, 6])
        mv = sb("mv", [P, 8, TPB])
        xn = sb("xn", [P, TPB, D])
        fT = sb("fT", [P, S])
        gg = sb("gg", [P, len(FFC), S])
        hid = sb("hid", [P, len(FFC), S])

        w_in, w_in2 = sem("w_in"), sem("w_in2")
        tab_sem = sem("tab_ready")
        N = {k: sem(k) for k in (
            "yl_ready", "hT_ps", "hT_sb", "proj_ps", "raw_sb", "v_sb", "sq_sb", "ropech", "summed", "normed",
            "qkT_ps", "qkT_sb", "sim_ps", "smch", "shifted", "prob_sb", "sumch", "pT_sb", "pv_ps", "on_sb",
            "oT_ps", "oT_sb", "wo_ps", "y_sum", "rn_sb",
            "f_yl", "f_lnch", "f_xn", "f_hT_ps", "f_hT", "f_a_ps", "f_g", "f_hid", "f_o_ps", "f_y", "f_dve_gate", "f_pe_gate")}
        vp_sem = [sem(f"vp_ready{u}") for u in range(UPB)]
        by = {"PE": ("hT_ps", "proj_ps", "qkT_ps", "sim_ps", "pv_ps", "oT_ps", "wo_ps", "f_hT_ps", "f_a_ps", "f_o_ps"),
              "ACT": ("hT_sb", "raw_sb", "v_sb", "sq_sb", "qkT_sb", "prob_sb", "oT_sb", "f_g"),
              "DVE": ("summed", "rn_sb", "shifted", "pT_sb", "on_sb", "y_sum", "f_xn", "f_hT", "f_hid", "f_y"),
              "POOL": ("normed",)}

        def credit(eng, who):
            for k in by[who]:
                eng.sem_inc(N[k], CR * PER_UNIT.get(k, 1))

        once = sem("lt_once")
        pe_gate, sp_gate = sem("pe_gate"), sem("sp_gate")
        with nc.Block() as block:
            @block.sync
            def _(sp):
                sp.dma_start(tab0[:, :, :, :], a["tables"]).then_inc(once, 16)
                sp.wait_ge(once, 16)

            @block.tensor
            def _(pe):
                credit(pe, "PE")

            @block.scalar
            def _(act):
                credit(act, "ACT")

            @block.gpsimd
            def _(pool):
                credit(pool, "POOL")
                lt_m = sem("lt_mask")
                nc.gpsimd.memset(maskb[:, :, :], 0.0).then_inc(lt_m, 1)
                pool.wait_ge(lt_m, 1)
                k = 1
                for v in range(2):
                    for w in range(4):
                        part = maskb[32 * w:32 * w + 32, v, :].rearrange("p (h c) -> p h c", c=2 * WIN)
                        low = WIN if (v == 0 and w == 0) else 0
                        if low:
                            nc.gpsimd.memset(part[:, :, 0:low], MASKED).then_inc(lt_m, 1)
                            k += 1
                            pool.wait_ge(lt_m, k)
                        else:
                            nc.gpsimd.affine_select(out=part, in_=part, compare_op=ALU.is_ge, fill=MASKED, base=0,
                                                    pattern=[[0, H2 // 2], [1, 2 * WIN]], channel_multiplier=-1).then_inc(lt_m, 1)
                            k += 1
                            pool.wait_ge(lt_m, k)
                        nc.gpsimd.affine_select(out=part, in_=part, compare_op=ALU.is_ge, fill=MASKED, base=WIN,
                                                pattern=[[0, H2 // 2], [-1, 2 * WIN]], channel_multiplier=1).then_inc(lt_m, 1)
                        k += 1
                        pool.wait_ge(lt_m, k)

            @block.vector
            def _(dve):
                credit(dve, "DVE")
                z = sem("lt_zero")
                nc.vector.memset(yl[0:1, 0, D // 2:D], 0.0).then_inc(z, 1)
                nc.vector.memset(yf[0:1, 0, D // 2:D], 0.0).then_inc(z, 1)
                nc.vector.memset(kT[:, :, 0:WIN], 0.0).then_inc(z, 1)
                nc.vector.memset(Vp[0:32, 0, :], 0.0).then_inc(z, 1)
                dve.wait_ge(z, 4)

        def load_shifted(sp, dst, b, ready):
            half = slice(D // 2, D)
            sp.dma_start(dst[:, :, 0:D // 2], y[:, bass.ds(TPB * b, TPB), 0:D // 2]).then_inc(ready, 16)
            sp.dma_start(dst[1:P, :, half], y[0:P - 1, bass.ds(TPB * b, TPB), half]).then_inc(ready, 16)
            sp.dma_start(dst[0:1, 1:2, half], y[P - 1:P, bass.ds(TPB * b, 1), half]).then_inc(ready, 16)

        LAGS = 4
        units_left = [0]

        def staged(eng, i, stages):
            def slots(b, first, last):
                for j in range(LAGS if last else UPB):
                    for lag, fn in stages:
                        k = j - lag
                        if (first and k < 0) or (last and k >= 0):
                            continue
                        units_left[0] = -k - 1 if last else UPB
                        fn(i * (B * UPB) + b * UPB + k, k % UPB, b + k // UPB)
            slots(0, True, False)
            with eng.Fori(1, B) as b:
                slots(b, False, False)
            slots(B, False, True)

        with nc.Fori(0, DEPTH) as i:
            with nc.Block() as block:
                @block.sync
                def _(sp):
                    sp.dma_start(wqkv[:, :], a["Wqkv"][bass.ds(i, 1), :, :].rearrange("o p n -> p (o n)")).then_inc(w_in, 16)
                    sp.dma_start(wo[:, :, :], a["Wo"][bass.ds(i, 1), :, :, :].rearrange("o p c n -> p (o c) n")).then_inc(w_in, 16)
                    sp.dma_start(scales[:, :, :], a["scales"][bass.ds(i, 1), :, :, :].rearrange("o p c n -> p (o c) n")).then_inc(w_in, 16)

                    def load(U, u, b):
                        if u == 0:
                            sp.wait_ge(N["hT_ps"], U - UPB + 1 + CR)
                            load_shifted(sp, yl, b, N["yl_ready"])

                    def shift_v(U, u, b):
                        t, c = u // 2, slice((u % 2) * 512, (u % 2) * 512 + 512)
                        sp.wait_ge(N["v_sb"], U + 1 + CR)
                        sp.sem_inc(sp_gate, 1)
                        if t == 0:
                            sp.wait_ge(N["pv_ps"], (U - 2 + 1 + CR) * 4)
                            sp.dma_start(Vp[0:32, 1, c], V[96:128, 0, c]).then_inc(vp_sem[u], 16)
                        else:
                            sp.wait_ge(N["pv_ps"], (U - 4 + 1 + CR) * 4)
                        sp.dma_start(Vp[32:128, t, c], V[0:96, t, c]).then_inc(vp_sem[u], 16)

                    staged(sp, i, [(1, shift_v), (0, load)])

                @block.tensor
                def _(pe):
                    pe.wait_ge(w_in, 16 * 3 * (i + 1))

                    def turn_qk(U, u, b):
                        pe.wait_ge(N["normed"], U + 1 + CR)
                        pe.wait_ge(N["oT_sb"], U - 3 + 1 + CR)
                        pe.wait_ge(N["y_sum"], U - 3 + 1 + CR)
                        for qk in range(2):
                            for hp in range(H2 // 2):
                                mm = nc.tensor.transpose(ps[:, 3 + qk, hp * P:hp * P + P],
                                                         qkn[:, qk, 2 * hp:2 * hp + 2, :].rearrange("p h d -> p (h d)"), ident[:, :])
                        mm.then_inc(N["qkT_ps"], 1)

                    def project(U, u, b):
                        t, c = u // 2, (u % 2) * 512
                        if u == 0:
                            pe.wait_ge(N["hT_sb"], U + 4 + CR)
                        pe.wait_ge(N["v_sb"], U - 1 + 1 + CR)
                        pe.wait_ge(N["raw_sb"], U - 1 + 1 + CR)
                        pe.wait_ge(N["sq_sb"], U - 1 + 1 + CR)
                        for m in range(3):
                            mm = nc.tensor.matmul(ps[:, m, :], hT[:, t * P:t * P + P], wqkv[:, m * INNER + c:m * INNER + c + 512],
                                                  start=True, stop=True)
                        mm.then_inc(N["proj_ps"], 1)

                    def turn_h(U, u, b):
                        if u == 0:
                            pe.wait_ge(N["yl_ready"], (i * B + b) * 48 + 48)
                            pe.wait_ge(N["qkT_sb"], U - 2 + 1 + CR)
                            for t in range(TPB):
                                mm = nc.tensor.transpose(ps[:, 4, t * P:t * P + P], yl[:, t, :], ident[:, :])
                            mm.then_inc(N["hT_ps"], 4)

                    def turn_o(U, u, b):
                        pe.wait_ge(N["on_sb"], U + 1 + CR)
                        pe.wait_ge(N["qkT_sb"], U + min(2, units_left[0]) + 1 + CR)
                        for hp in range(H2 // 2):
                            mm = nc.tensor.transpose(ps[:, 3, hp * P:hp * P + P], on[:, hp, :], ident[:, :])
                        mm.then_inc(N["oT_ps"], 1)

                    def scores(U, u, b):
                        t, c = u // 2, (u % 2) * (H2 // 2)
                        pe.wait_ge(N["qkT_sb"], U + 1 + CR)
                        pe.wait_ge(N["shifted"], U - 1 + 1 + CR)
                        for odd in range(2):
                            nc.tensor.matmul(ps[:, 5 + odd, 0:256], identb[:, :], maskb[:, t, :], start=True, stop=False,
                                             skip_group_check=True)
                        for h in range(H2):
                            r = 64 * (h % 2)
                            for w in range(4):
                                mm = nc.tensor.matmul(ps[32 * w:32 * w + 32, 5 + h % 2, (h // 2) * 64:(h // 2) * 64 + 64],
                                                      qT[r:r + 64, h // 2, 32 * w:32 * w + 32],
                                                      kT[r:r + 64, c + h // 2, t * P + 32 * w:t * P + 32 * w + 64],
                                                      start=False, stop=(h >= H2 - 2), skip_group_check=True)
                            if h >= H2 - 2:
                                mm.then_inc(N["sim_ps"], 1)

                    def attend(U, u, b):
                        t, c = u // 2, (u % 2) * 512
                        pe.wait_ge(N["pT_sb"], U + 1 + CR)
                        pe.wait_ge(vp_sem[u], ((i * B + b) + 1) * (32 if t == 0 else 16))
                        if t == 1:
                            pe.wait_ge(vp_sem[u - 2], ((i * B + b) + 1) * 32)
                        pe.wait_ge(N["on_sb"], U - 1 + 1 + CR)
                        pe.sem_inc(pe_gate, 1)
                        for h in range(H2):
                            for part, v in ((1, V), (0, Vp)):
                                for w in range(4):
                                    mm = nc.tensor.matmul(ps[32 * w:32 * w + 32, 7, h * 64:h * 64 + 64],
                                                          pT[32 * w:32 * w + 32, 4 * (h % 2) + h // 2, part, :],
                                                          v[32 * w:32 * w + 32, t, c + h * 64:c + h * 64 + 64],
                                                          start=(part == 1), stop=(part == 0), skip_group_check=True)
                                    if h == H2 - 1 and part == 0:
                                        mm.then_inc(N["pv_ps"], 1)

                    def out_proj(U, u, b):
                        c = (u % 2) * (H2 // 2)
                        pe.wait_ge(N["oT_sb"], U + 1 + CR)
                        pe.wait_ge(N["y_sum"], U - 1 + 1 + CR)
                        for hp in range(H2 // 2):
                            mm = nc.tensor.matmul(ps[:, 4, 0:D], oT[:, hp, :], wo[:, c + hp, :], start=(hp == 0), stop=(hp == H2 // 2 - 1))
                        mm.then_inc(N["wo_ps"], 1)

                    staged(pe, i, [(1, project), (2, turn_qk), (0, turn_h), (4, turn_o), (2, scores), (3, attend), (4, out_proj)])

                @block.scalar
                def _(act):
                    def evac_qk(U, u, b):
                        t, c = u // 2, (u % 2) * (H2 // 2)
                        act.wait_ge(N["qkT_ps"], U + 1 + CR)
                        act.wait_ge(N["sim_ps"], (U - 1 + 1 + CR) * 2)
                        nc.scalar.activation(qT[:, :, :], ps[:, 3, :].rearrange("p (c n) -> p c n", n=P), ACT.Copy)
                        nc.scalar.activation(kT[:, c:c + H2 // 2, WIN + t * P:WIN + t * P + P],
                                             ps[:, 4, :].rearrange("p (c n) -> p c n", n=P), ACT.Copy).then_inc(N["qkT_sb"], 1)

                    def evac_proj(U, u, b):
                        t, c = u // 2, (u % 2) * 512
                        act.wait_ge(N["proj_ps"], U + 1 + CR)
                        act.wait_ge(N["summed"], U - 1 + 1 + CR)
                        nc.scalar.activation(raw[:, :, :, :].rearrange("p a h d -> p (a h d)"),
                                             ps[:, 0:2, :].rearrange("p a n -> p (a n)"), ACT.Copy).then_inc(N["raw_sb"], 1)
                        act.wait_ge(N["rn_sb"], U - 1 + 1 + CR)
                        nc.scalar.activation(sq[:, :, :, :].rearrange("p a h d -> p (a h d)"),
                                             ps[:, 0:2, :].rearrange("p a n -> p (a n)"), ACT.Square).then_inc(N["sq_sb"], 1)
                        act.wait_ge(N["pv_ps"], (U - 4 + 1 + CR) * 4)
                        nc.scalar.activation(V[:, t, c:c + 512], ps[:, 2, :], ACT.Copy).then_inc(N["v_sb"], 1)

                    def evac_h(U, u, b):
                        if u == 0:
                            act.wait_ge(N["hT_ps"], U + 4 + CR)
                            act.wait_ge(N["proj_ps"], U - 1 + 1 + CR)
                            nc.scalar.activation(hT[:, :], ps[:, 4, 0:S], ACT.Copy).then_inc(N["hT_sb"], 4)

                    def evac_o(U, u, b):
                        act.wait_ge(N["oT_ps"], U + 1 + CR)
                        act.wait_ge(N["wo_ps"], U - 1 + 1 + CR)
                        nc.scalar.activation(oT[:, :, :], ps[:, 3, :].rearrange("p (c n) -> p c n", n=P), ACT.Copy).then_inc(N["oT_sb"], 1)

                    def exps(U, u, b):
                        act.wait_ge(N["shifted"], U + 1 + CR)
                        act.wait_ge(N["pT_sb"], U - 1 + 1 + CR)
                        nc.scalar.activation(prob[:, :, :], sim[:, :, :], ACT.Exp, scale=QK_SCALE).then_inc(N["prob_sb"], 1)

                    staged(act, i, [(2, evac_qk), (1, evac_proj), (0, evac_h), (4, evac_o), (2, exps)])

                @block.gpsimd
                def _(pool):
                    def normalise(U, u, b):
                        pool.wait_ge(N["rn_sb"], U + 1 + CR)
                        pool.wait_ge(N["summed"], U + 1 + CR)
                        pool.wait_ge(N["qkT_ps"], U - 1 + 1 + CR)
                        nc.gpsimd.tensor_tensor(qkn[:, :, :, :].rearrange("p a h d -> p (a h) d"),
                                                t1[:, :, :, :].rearrange("p a h d -> p (a h) d"),
                                                view(rn, 0, P, 0, [[1, 2 * H2], [0, DH]]), ALU.mult).then_inc(N["normed"], 1)
                    staged(pool, i, [(1, normalise)])

                @block.vector
                def _(dve):
                    dve.wait_ge(w_in, 16 * 3 * (i + 1))
                    nc.vector.tensor_tensor(tab[:, :, :, :].rearrange("p t c d -> p t (c d)"),
                                            tab0[:, :, :, :].rearrange("p t c d -> p t (c d)"),
                                            view(scales, 0, P, 0, [[0, TPB], [1, 4 * DH]]), ALU.mult).then_inc(tab_sem, 1)
                    dve.wait_ge(tab_sem, i + 1)

                    def rope(U, u, b):
                        t = u // 2
                        link = Chain(dve, N["ropech"], RSQRT_OPS + 3, U)
                        dve.wait_ge(N["raw_sb"], U + 1 + CR)
                        dve.wait_ge(N["normed"], U - 1 + 1 + CR)
                        nc.vector.tensor_tensor(t1[:, :, :, :], raw[:, :, :, :],
                                                view(tab, 0, P, t * 256, [[128, 2], [0, H2], [1, DH]]), ALU.mult)
                        for r in range(2):
                            ins = nc.vector.tensor_tensor(t2[:, :, :, 32 * r:32 * r + 32], raw[:, :, :, 32 - 32 * r:64 - 32 * r],
                                                          view(tab, 0, P, t * 256 + 64 + 32 * r, [[128, 2], [0, H2], [1, 32]]), ALU.mult)
                            if r == 1:
                                link(ins)
                        dve.wait_ge(N["sq_sb"], U + 1 + CR)
                        nc.vector.tensor_tensor(t1[:, :, :, :].rearrange("p a h d -> p (a h d)"),
                                                t1[:, :, :, :].rearrange("p a h d -> p (a h d)"),
                                                t2[:, :, :, :].rearrange("p a h d -> p (a h d)"), ALU.add).then_inc(N["summed"], 1)
                        link(nc.vector.tensor_reduce(ss[:, :], sq[:, :, :, :].rearrange("p a h d -> p (a h) d"), AX, ALU.add))
                        link(nc.vector.tensor_scalar(ss[:, :], ss[:, :], 1e-24, None, ALU.max))
                        rsqrt(nc, link, rn[:, :], ss[:, :], rtmp[:, :])
                        link.end()
                        dve.sem_inc(N["rn_sb"], 1)

                    def softmax_a(U, u, b):
                        link = Chain(dve, N["smch"], 1, U)
                        dve.wait_ge(N["sim_ps"], (U + 1 + CR) * 2)
                        dve.wait_ge(N["prob_sb"], U - 1 + 1 + CR)
                        s5 = view(ps, 0, P, 5 * 512, [[512, 2], [64, 4], [1, 64]])
                        link(nc.vector.tensor_reduce(rowmax[:, :].rearrange("p (a h) -> p a h", a=2), s5, AX, ALU.max))
                        nc.vector.tensor_tensor(sim[:, :, :].rearrange("p (a h) c -> p a h c", a=2), s5,
                                                view(rowmax, 0, P, 0, [[4, 2], [1, 4], [0, 64]]), ALU.subtract)\
                            .then_inc(N["shifted"], 1)
                        link.end()

                    def softmax_b(U, u, b):
                        link = Chain(dve, N["sumch"], 2, U)
                        dve.wait_ge(N["prob_sb"], U + 1 + CR)
                        dve.wait_ge(N["pv_ps"], (U - 1 + 1 + CR) * 4)
                        link(nc.vector.tensor_reduce(rowsum[:, u % 2, :], prob[:, :, :], AX, ALU.add))
                        link(nc.vector.reciprocal(rsum[:, u % 2, :], rowsum[:, u % 2, :]))
                        nc.vector.transpose(pT[:, :, :, :].rearrange("p h a q -> p (h a q)"),
                                            prob[:, :, :].rearrange("p h c -> p (h c)")).then_inc(N["pT_sb"], 1)
                        link.end()

                    def scale_out(U, u, b):
                        dve.wait_ge(N["pv_ps"], (U + 1 + CR) * 4)
                        dve.wait_ge(N["oT_ps"], U - 1 + 1 + CR)
                        nc.vector.tensor_tensor(on[:, :, :].rearrange("p c (a d) -> p c a d", d=DH),
                                                ps[:, 7, :].rearrange("p (c a d) -> p c a d", a=2, d=DH),
                                                view(rsum, 0, P, (u % 2) * H2, [[1, 4], [4, 2], [0, DH]]), ALU.mult).then_inc(N["on_sb"], 1)

                    def residual(U, u, b):
                        dve.wait_ge(N["wo_ps"], U + 1 + CR)
                        dve.wait_ge(N["y_sum"], U - 1 + 1 + CR)
                        yt = y[:, bass.ds(b * TPB + u // 2, 1), :].rearrange("p o d -> p (o d)")
                        nc.vector.tensor_tensor(yt, ps[:, 4, 0:D], yt, ALU.add).then_inc(N["y_sum"], 1)

                    staged(dve, i, [(1, rope), (4, residual), (2, softmax_a), (3, scale_out), (2, softmax_b)])

            ffn_layer(nc, a, ps, y, ident, ones, i, N, w1, w2, ffcols, b2row, yf, st, mv, xn, fT, gg, hid, load_shifted, w_in2)


def ffn_layer(nc, a, ps, y, ident, ones, i, N, w1, w2, ffcols, b2row, yf, st, mv, xn, fT, gg, hid, load_shifted, w_in):
    NLN = 1 + 7 + RSQRT_OPS
    with nc.Block() as block:
        @block.sync
        def _(sp):
            sp.dma_start(w1[:, :], a["W1"][bass.ds(i, 1), :, :].rearrange("o p n -> p (o n)")).then_inc(w_in, 16)
            for c, (c0, cn) in enumerate(FFC):
                sp.dma_start(w2[0:cn, c, :], a["W2"][bass.ds(i, 1), c0:c0 + cn, :].rearrange("o p n -> p (o n)")).then_inc(w_in, 16)
            sp.dma_start(ffcols[:, :], a["ffcols"][bass.ds(i, 1), :, :].rearrange("o p n -> p (o n)")).then_inc(w_in, 16)
            sp.dma_start(b2row[:, :], a["b2"][bass.ds(i, 1), :]).then_inc(w_in, 16)
            with sp.Fori(0, B) as b:
                n = i * B + b
                sp.wait_ge(N["f_xn"], n + CR)
                load_shifted(sp, yf, b, N["f_yl"])

        @block.vector
        def _(dve):
            dve.wait_ge(w_in, 16 * 6 * (i + 1))
            dve.sem_inc(N["f_dve_gate"], 1)
            with dve.Fori(0, B) as b:
                n = i * B + b
                link = Chain(dve, N["f_lnch"], NLN, n)
                dve.wait_ge(N["f_yl"], 48 * n + 48)
                nc.vector.bn_stats(st[:, 0, :], yf[:, 0, :])
                link(nc.vector.bn_stats(st[:, 1, :], yf[:, 1, :]))
                mean_rstd(nc, link, st, mv)
                link.end()
                dve.wait_ge(N["f_hT_ps"], n + CR)
                for t in range(TPB):
                    ins = nc.vector.tensor_scalar(xn[:, t, :], yf[:, t, :], mv[:, 1, t:t + 1], mv[:, 6, t:t + 1],
                                                  ALU.subtract, ALU.mult)
                ins.then_inc(N["f_xn"], 1)
                dve.wait_ge(N["f_hT_ps"], n + 1 + CR)
                dve.wait_ge(N["f_a_ps"], n + CR)
                nc.vector.tensor_scalar(fT[:, :], ps[:, 0, 0:S], ffcols[:, 0:1], ffcols[:, 1:2], ALU.mult, ALU.add)\
                    .then_inc(N["f_hT"], 1)
                dve.wait_ge(N["f_g"], n + 1 + CR)
                dve.wait_ge(N["f_o_ps"], n + CR)
                for c, (c0, cn) in enumerate(FFC):
                    ins = nc.vector.scalar_tensor_tensor(hid[0:cn, c, :], ps[0:cn, 1 + c, 0:S], ffcols[0:cn, 2 + c:3 + c],
                                                         gg[0:cn, c, :], ALU.add, ALU.mult)
                ins.then_inc(N["f_hid"], 1)
                dve.wait_ge(N["f_o_ps"], n + 1 + CR)
                yt = y[:, bass.ds(b * TPB, TPB), :].rearrange("p t d -> p (t d)")
                nc.vector.tensor_tensor(yt, ps[:, 7, 0:S], yt, ALU.add).then_inc(N["f_y"], 1)

        @block.tensor
        def _(pe):
            pe.wait_ge(w_in, 16 * 6 * (i + 1))
            pe.sem_inc(N["f_pe_gate"], 1)
            with pe.Fori(0, B) as b:
                n = i * B + b
                pe.wait_ge(N["f_xn"], n + 1 + CR)
                pe.wait_ge(N["f_hT"], n + CR)
                for t in range(TPB):
                    mm = nc.tensor.transpose(ps[:, 0, t * P:t * P + P], xn[:, t, :], ident[:, :])
                mm.then_inc(N["f_hT_ps"], 1)
                pe.wait_ge(N["f_hT"], n + 1 + CR)
                pe.wait_ge(N["f_hid"], n + CR)
                for c, (c0, cn) in enumerate(FFC):
                    for g in range(2):
                        mm = nc.tensor.matmul(ps[0:cn, 1 + 3 * g + c, 0:S], w1[:, g * FF + c0:g * FF + c0 + cn], fT[:, :],
                                              start=True, stop=True)
                mm.then_inc(N["f_a_ps"], 1)
                pe.wait_ge(N["f_hid"], n + 1 + CR)
                pe.wait_ge(N["f_y"], n + CR)
                for t in range(TPB):
                    for c, (c0, cn) in enumerate(FFC):
                        nc.tensor.matmul(ps[:, 7, t * P:t * P + P], hid[0:cn, c, t * P:t * P + P], w2[0:cn, c, :],
                                         start=(c == 0), stop=False)
                    mm = nc.tensor.matmul(ps[:, 7, t * P:t * P + P], ones[0:1, :], b2row[0:1, :], start=False, stop=True)
                mm.then_inc(N["f_o_ps"], 1)

        @block.scalar
        def _(act):
            with act.Fori(0, B) as b:
                n = i * B + b
                act.wait_ge(N["f_a_ps"], n + 1 + CR)
                act.wait_ge(N["f_hid"], n + CR)
                for c, (c0, cn) in enumerate(FFC):
                    ins = nc.scalar.activation(gg[0:cn, c, :], ps[0:cn, 4 + c, 0:S], ACT.Gelu, bias=ffcols[0:cn, 5 + c:6 + c])
                ins.then_inc(N["f_g"], 1)


def mean_rstd(nc, link, st, mv):
    me, ve, mo, vo = (st[:, :, k] for k in (1, 2, 4, 5))
    v = nc.vector
    link(v.tensor_tensor(mv[:, 0, :], me, mo, ALU.add))
    link(v.tensor_scalar(mv[:, 1, :], mv[:, 0, :], 0.5, None, ALU.mult))
    link(v.tensor_tensor(mv[:, 2, :], me, mo, ALU.subtract))
    link(v.scalar_tensor_tensor(mv[:, 3, :], mv[:, 2, :], 0.25, mv[:, 2, :], ALU.mult, ALU.mult))
    link(v.tensor_tensor(mv[:, 4, :], ve, vo, ALU.add))
    link(v.scalar_tensor_tensor(mv[:, 5, :], mv[:, 4, :], 1.0 / D, mv[:, 3, :], ALU.mult, ALU.add))
    link(v.tensor_scalar(mv[:, 5, :], mv[:, 5, :], 1e-5, None, ALU.add))
    rsqrt(nc, link, mv[:, 6, :], mv[:, 5, :], mv[:, 7, :])


def rotary_tables():
    half = np.arange(0, DH, 2, dtype=np.float32)
    inv_freq = (1.0 / np.float32(10000.0) ** (half / np.float32(DH))).astype(np.float32)
    t = np.arange(S, dtype=np.float32)
    freqs = t[:, None] * inv_freq[None, :]
    base = (half + np.float32(0.4 * DH)) / np.float32(1.4 * DH)
    power = (t - S // 2) / np.float32(WIN // 2)
    scale = (base[None, :] ** power[:, None]).astype(np.float32)
    c, s = np.cos(freqs), np.sin(freqs)
    two = lambda u, w: np.concatenate([u, w], -1)
    rows = np.stack([two(c * scale, c * scale), two(-s * scale, s * scale),
                     two(c / scale, c / scale), two(-s / scale, s / scale)], 1)
    return np.ascontiguousarray(rows.reshape(TPB, P, 4, DH).transpose(1, 0, 2, 3), np.float32)


def third_order_masks():
    sp, k, s, j = (np.arange(n) for n in (G3, 3, G3, W3))
    out = np.full((3, G3, 3, G3, W3), MASKED, np.float32)
    for g in range(3):
        tok = G3 * g + s[None, None, :, None]
        key = G3 * (g - 2 + k[None, :, None, None]) + sp[:, None, None, None]
        ok = (tok - key >= 0) & (tok - key < W3)
        if g < 2:
            ok = ok & (key >= 0) & (tok - W3 + 1 + j[None, None, None, :] >= 0)
        ok = np.broadcast_to(ok, (G3, 3, G3, W3))
        out[g][ok] = 0.0
    out = out.reshape(3, G3, 3 * P).transpose(1, 0, 2)
    return np.ascontiguousarray(np.tile(out, (H3, 1, 1)))


def lay_out(inp):
    g = lambda n: np.asarray(inp[n])
    c = np.ascontiguousarray
    tiles = lambda v: c(v.reshape(NT, P, D).transpose(1, 0, 2))
    sw = lambda v: np.concatenate([v[:, DH // 2:], v[:, :DH // 2]], -1)
    qs, ks = g("L0_ffn_q_scale"), g("L0_ffn_k_scale")
    scales = np.stack([qs, sw(qs), ks, sw(ks)], 1)
    b1 = g("L0_ffn_b1").reshape(DEPTH, 2, FF)
    b1p = np.zeros((DEPTH, 2, 3 * P), np.float32)
    b1p[:, :, :FF] = b1
    cols = np.concatenate([g("L0_ffn_ln_g")[:, :, None], g("L0_ffn_ln_b")[:, :, None],
                           b1p.reshape(DEPTH, 6, P).transpose(0, 2, 1)], -1)
    b2big = np.zeros((CHUNK, EXPERTS, CHUNK, D), np.float32)
    for t in range(CHUNK):
        b2big[t, :, t] = g("L1_ffn_b2")
    b2big = b2big.reshape(CHUNK * EXPERTS, CHUNK, D)
    return {
        "x": tiles(g("L0_attn_x")),
        "ident": np.eye(P, dtype=np.float32),
        "Wqkv": c(g("L0_ffn_Wqkv")),
        "Wo": c(g("L0_ffn_Wo").reshape(DEPTH, HEADS // 2, P, D).transpose(0, 2, 1, 3)),
        "scales": c(np.broadcast_to(scales[:, None], (DEPTH, P, 4, DH))),
        "tables": rotary_tables(),
        "cT0": c(g("L0_c").T), "wmod0": c(g("L0_wmod")), "cT1": c(g("L1_c").T), "wmod1": c(g("L1_wmod")),
        "a_w": c(np.stack([g("L0_attn_W" + n).T for n in "qkv"], 1)),
        "a_b": c(np.stack([g("L0_attn_bq"), g("L0_attn_bk")], 1)), "a_bv": c(g("L0_attn_bv")[None]),
        "d_w": c(np.stack([g("L1_attn_" + n).T for n in ("Wq", "Wk", "Wkp", "Wv", "Wo")], 1)),
        "d_bd": np.repeat(np.eye(H3, dtype=np.float32), D3, 0), "d_mask": third_order_masks(),
        "d_ln": c(np.broadcast_to(np.stack([g("L1_attn_gamma"), g("L1_attn_beta")])[None], (P, 2, D))),
        "e_wr": c(g("L1_ffn_Wr")), "e_w1": c(g("L1_ffn_W1").transpose(1, 0, 2)),
        "e_w2": c(g("L1_ffn_W2").reshape(EXPERTS, DI // P, P, D).transpose(2, 0, 1, 3)),
        "e_b1": c(g("L1_ffn_b1").reshape(EXPERTS, DI // P, P).transpose(2, 0, 1)), "e_b2": b2big,
        "e_below": np.triu(np.ones((P, P), np.float32), 1),
        "W1": c(g("L0_ffn_W1")), "W2": c(g("L0_ffn_W2")), "ffcols": c(cols), "b2": c(g("L0_ffn_b2")),
    }


def kernel(**inputs):
    import concourse.bacc as bacc
    from concourse.bass_utils import run_bass_kernel_spmd

    nc = bacc.Bacc("TRN2", target_bir_lowering=False, num_devices=1)
    arrays = lay_out(inputs)
    aps = {k: nc.dram_tensor(f"in_{k}", v.shape, mybir.dt.from_np(v.dtype), kind="ExternalInput").ap() for k, v in arrays.items()}
    out = nc.dram_tensor("out", (P, NT, D), F32, kind="ExternalOutput").ap()
    build(nc, aps, out)
    r = run_bass_kernel_spmd(nc, [{f"in_{k}": v for k, v in arrays.items()}], core_ids=[0])
    got = r.results[0]["out"]
    return np.ascontiguousarray(got.transpose(1, 0, 2)).reshape(B, S, D)
```

```python
from contextlib import ExitStack

import numpy as np

import concourse.bass as bass
from concourse import mybir

F32 = mybir.dt.float32
BF16 = mybir.dt.bfloat16
I32 = mybir.dt.int32
ACT = mybir.ActivationFunctionType
ALU = mybir.AluOpType
AX = mybir.AxisListType.X

P = 128
B = 16
S = 256
D = 128
TPB = S // P
NT = B * TPB
DEPTH = 6
HEADS, DH = 16, 64
INNER = HEADS * DH
WIN = 32
FF = int(D * 4 * 2 / 3)
FFC = [(0, 128), (128, 128), (256, FF - 256)]
TOPK = 32
NEG = -3.0e38
MASKED = -1.0e30
MAGIC = float(0x5F3759DF)
CR = 8
UPB = 4
H2 = HEADS // 2
QK_SCALE = 8.0
PER_UNIT = {"sim_ps": 2, "pv_ps": 4}


def view(t, part0, nparts, offset, dims):
    a = t[part0:part0 + nparts]
    row = a.ap[0][0]
    return bass.AP(tensor=a.tensor, offset=a.offset + offset, ap=[[row, nparts]] + [list(d) for d in dims])


class Chain:

    def __init__(self, eng, sem, per, turn, gate=None):
        self.eng, self.sem, self.k, self.per, self.base, self.gate = eng, sem, 0, per, turn * per, gate

    def __call__(self, ins):
        self.k += 1
        assert self.k <= self.per, self.sem
        ins.then_inc(self.sem, 1)
        self.eng.wait_ge(self.sem, self.base + self.k)
        if self.gate is not None:
            self.eng.sem_inc(self.gate, 1)

    def end(self):
        assert self.k == self.per, (self.sem, self.k)


RSQRT_OPS = 2 + 3 * 3


def rsqrt(nc, link, y, v, tmp):
    link(nc.vector.tensor_scalar(y.bitcast(I32), v.bitcast(I32), 1, None, ALU.logical_shift_right))
    link(nc.vector.tensor_scalar(y.bitcast(I32), y.bitcast(I32), -1.0, MAGIC, ALU.mult, ALU.add))
    for _ in range(3):
        link(nc.vector.tensor_tensor(tmp, y, y, ALU.mult))
        link(nc.vector.scalar_tensor_tensor(tmp, tmp, -0.5, v, ALU.mult, ALU.mult))
        link(nc.vector.scalar_tensor_tensor(y, tmp, 1.5, y, ALU.add, ALU.mult))


def build(nc, a, out):
    with ExitStack() as ctx:
        def sb(name, shape, dt=F32):
            return ctx.enter_context(nc.sbuf_tensor(name, shape, dt))

        def sem(name):
            return ctx.enter_context(nc.semaphore(name))

        ps = ctx.enter_context(nc.psum_tensor("ps", [P, 8, 512], F32))
        x = sb("x", [P, NT, D])
        ident = sb("ident", [P, P])
        identb = sb("identb", [P, P], BF16)
        ones = sb("ones", [P, P])

        loaded = sem("loaded")
        consts = sem("consts")
        with nc.Block() as block:
            @block.sync
            def _(sp):
                sp.dma_start(x[:, :, :], a["x"]).then_inc(loaded, 16)
                sp.dma_start(ident[:, :], a["ident"]).then_inc(loaded, 16)
                sp.wait_ge(loaded, 32)

            @block.vector
            def _(dve):
                dve.wait_ge(loaded, 32)
                nc.vector.tensor_copy(identb[:, :], ident[:, :]).then_inc(consts, 1)
                nc.vector.memset(ones[:, :], 1.0).then_inc(consts, 1)
                dve.wait_ge(consts, 2)

        y = sb("y", [P, NT, D])
        rows = sb("rows", [P, B, 4, D])
        colmod = sb("colmod", [P, 6, B])
        mv = sb("mv_x", [P, 8, NT])
        modulation(nc, a, 0, sem, ps, colmod, rows)
        norm_stats(nc, sem, x, mv, "a")
        top32_attention(nc, a, sem, ps, x, mv, colmod, rows, ident, ones)
        norm_stats(nc, sem, x, mv, "b")
        into_y(nc, sem, x, y, mv, rows)
        local_transformer(nc, a, sem, ps, y, ident, identb, ones)
        add_gated(nc, sem, x, y, rows)
        modulation(nc, a, 1, sem, ps, colmod, rows)
        norm_stats(nc, sem, x, mv, "d")
        third_order_attention(nc, a, sem, ps, x, y, mv, colmod, rows, ident, identb)
        norm_stats(nc, sem, x, mv, "e")
        expert_choice(nc, a, sem, ps, x, mv, colmod, rows, ident, ones)

        stored = sem("stored")
        with nc.Block() as block:
            @block.sync
            def _(sp):
                sp.dma_start(out, x[:, :, :]).then_inc(stored, 16)
                sp.wait_ge(stored, 16)


class Marks:

    def __init__(self, sem, **by_engine):
        self.s, self.by, self.f = {}, {}, {}
        for who, names in by_engine.items():
            self.by[who] = names
            for n in names:
                self.s[n] = sem(n)

    def give(self, who, eng):
        for n in self.by[who]:
            eng.sem_inc(self.s[n], CR)

    def done(self, eng, name, unit):
        eng.wait_ge(self.s[name], unit + 1 + CR)

    def mark(self, name, ins):
        ins.then_inc(self.s[name], 1)


def staged_batches(eng, lags, stages, step=1):
    peeled = -(-lags // step) * step
    args = (lambda b, k: (b,)) if step == 1 else (lambda b, k: (b, k % step))
    for b in range(peeled):
        for lag, fn in stages:
            if b >= lag:
                fn(*args(b - lag, b - lag))
    with eng.Fori(peeled // step, B // step) as g:
        for k in range(step):
            for lag, fn in stages:
                fn(*args(step * g + (k - lag), k - lag))
    for b in range(B, B + lags):
        for lag, fn in stages:
            if b - lag < B:
                fn(*args(b - lag, b - lag))


def modulation(nc, a, l, sem, ps, colmod, rows):
    with ExitStack() as ctx:
        sb = lambda n, s, d=F32: ctx.enter_context(nc.sbuf_tensor(n + str(l), s, d))
        cT, sT, wmod = sb("cT", [P, B]), sb("sT", [P, B]), sb("wmod", [P, 6 * D])
        big, sign = sb("big", [P, B, 2, D]), sb("sign", [P, B, 2, D])
        m_in, m_silu, m_ps, m_sb, m_d = (sem(f"{n}{l}") for n in ("m_in", "m_silu", "m_ps", "m_sb", "m_d"))
        with nc.Block() as block:
            @block.sync
            def _(sp):
                sp.dma_start(cT[:, :], a[f"cT{l}"]).then_inc(m_in, 16)
                sp.dma_start(wmod[:, :], a[f"wmod{l}"]).then_inc(m_in, 16)

            @block.scalar
            def _(act):
                act.wait_ge(m_in, 32)
                nc.scalar.activation(sT[:, :], cT[:, :], ACT.Silu).then_inc(m_silu, 1)
                for b in range(B):
                    act.wait_ge(m_ps, b + 2)
                    nc.scalar.activation(rows[:, b, :, :].rearrange("p r d -> p (r d)"), ps[:, 1 + b % 4, :], ACT.Copy).then_inc(m_sb, 1)

            @block.tensor
            def _(pe):
                pe.wait_ge(m_in, 32)
                pe.wait_ge(m_silu, 1)
                for j in range(6):
                    mm = nc.tensor.matmul(ps[:, 0, j * B:(j + 1) * B], wmod[:, j * D:(j + 1) * D], sT[:, :], start=True, stop=True)
                mm.then_inc(m_ps, 1)
                for b in range(B):
                    if b >= 4:
                        pe.wait_ge(m_sb, b - 3)
                    nc.tensor.matmul(ps[:, 1 + b % 4, :], view(sT, 0, P, b, [[0, P]]), wmod[:, 2 * D:6 * D],
                                     start=True, stop=True).then_inc(m_ps, 1)

            @block.vector
            def _(dve):
                v = nc.vector
                dve.wait_ge(m_ps, 1)
                v.tensor_copy(colmod[:, :, :].rearrange("p j b -> p (j b)"), ps[:, 0, 0:6 * B]).then_inc(m_d, 1)
                dve.wait_ge(m_d, 1)
                v.tensor_scalar(colmod[:, 1, :], colmod[:, 1, :], 1.0, None, ALU.add).then_inc(m_d, 1)
                v.tensor_scalar(colmod[:, 4, :], colmod[:, 4, :], 1.0, None, ALU.add).then_inc(m_d, 1)
                dve.wait_ge(m_sb, B)
                v.tensor_scalar(rows[:, :, 2, :], rows[:, :, 2, :], 1.0, None, ALU.add).then_inc(m_d, 1)
                for k, r in enumerate((0, 3)):
                    v.tensor_scalar(sign[:, :, k, :], rows[:, :, r, :], 0.0, 2.0, ALU.is_ge, ALU.mult).then_inc(m_d, 1)
                dve.wait_ge(m_d, 6)
                for k, r in enumerate((0, 3)):
                    v.scalar_tensor_tensor(big[:, :, k, :], sign[:, :, k, :], -1.0, rows[:, :, r, :], ALU.add, ALU.mult).then_inc(m_d, 1)
                dve.wait_ge(m_d, 8)
                v.tensor_scalar(big[:, :, :, :], big[:, :, :, :], 0.25, None, ALU.max).then_inc(m_d, 1)
                dve.wait_ge(m_d, 9)
                for k, r in enumerate((0, 3)):
                    v.scalar_tensor_tensor(rows[:, :, r, :], sign[:, :, k, :], -1.0, big[:, :, k, :], ALU.add, ALU.mult).then_inc(m_d, 1)
                dve.wait_ge(m_d, 11)


def norm_stats(nc, sem, src, mv, name):
    with ExitStack() as ctx:
        st = ctx.enter_context(nc.sbuf_tensor("st_" + name, [P, NT, 6], F32))
        s_st, s_ch = sem("st_" + name), sem("stch_" + name)
        with nc.Block() as block:
            @block.vector
            def _(dve):
                for t in range(NT):
                    nc.vector.bn_stats(st[:, t, :], src[:, t, :]).then_inc(s_st, 1)
                dve.wait_ge(s_st, NT)
                link = Chain(dve, s_ch, 7 + RSQRT_OPS, 0)
                mean_rstd(nc, link, st, mv)
                link.end()


def top32_attention(nc, a, sem, ps, x, mv, colmod, rows, ident, ones):
    with ExitStack() as ctx:
        sb = lambda n, s, d=F32: ctx.enter_context(nc.sbuf_tensor(n, s, d))
        w, bcol, bvrow = sb("a_w", [P, 3, D]), sb("a_b", [P, 2]), sb("a_bv", [1, D])
        xn, hT = sb("a_xn", [P, TPB, D]), sb("a_hT", [P, S])
        qT, kT, vn = sb("a_qT", [P, S]), sb("a_kT", [P, S]), sb("a_v", [P, TPB, D])
        sc, work = sb("a_sc", [P, TPB, S]), sb("a_work", [P, TPB, S])
        m8, kept = sb("a_m8", [P, TPB, 8]), sb("a_kept", [P, TPB, S])
        den, rden = sb("a_den", [P, TPB]), sb("a_rden", [P, TPB])
        kT2, upd = sb("a_keptT", [P, TPB, S]), sb("a_upd", [P, TPB, D])
        M = Marks(sem, DVE=("a_norm", "a_hTs", "a_top", "a_den", "a_x"), PE=("a_turned", "a_qkv", "a_scores", "a_keptT", "a_out"),
                  ACT=("a_qk", "a_s", "a_kT", "a_vs"))
        a_in, topch, resch, gate = sem("a_in"), sem("a_topch"), sem("a_resch"), sem("a_gate")
        with nc.Block() as block:
            @block.sync
            def _(sp):
                for dst, key in ((w[:, :, :], "a_w"), (bcol[:, :], "a_b"), (bvrow[:, :], "a_bv")):
                    sp.dma_start(dst, a[key]).then_inc(a_in, 16)

            @block.tensor
            def _(pe):
                M.give("PE", pe)
                pe.wait_ge(a_in, 48)

                def turn(b):
                    M.done(pe, "a_norm", b)
                    M.done(pe, "a_hTs", b - 1)
                    for t in range(TPB):
                        mm = nc.tensor.transpose(ps[:, 0, t * P:t * P + P], xn[:, t, :], ident[:, :])
                    M.mark("a_turned", mm)

                def project(b):
                    M.done(pe, "a_hTs", b)
                    M.done(pe, "a_qk", b - 1)
                    M.done(pe, "a_vs", b - 1)
                    for m in range(2):
                        nc.tensor.matmul(ps[:, 1, m * S:m * S + S], w[:, m, :], hT[:, :], start=True, stop=True)
                    for t in range(TPB):
                        nc.tensor.matmul(ps[:, 2, t * P:t * P + P], hT[:, t * P:t * P + P], w[:, 2, :], start=True, stop=False)
                        mm = nc.tensor.matmul(ps[:, 2, t * P:t * P + P], ones[0:1, :], bvrow[0:1, :], start=False, stop=True)
                    M.mark("a_qkv", mm)

                def score(b):
                    M.done(pe, "a_qk", b)
                    M.done(pe, "a_s", b - 1)
                    for t in range(TPB):
                        mm = nc.tensor.matmul(ps[:, 3, t * S:t * S + S], qT[:, t * P:t * P + P], kT[:, :], start=True, stop=True)
                    M.mark("a_scores", mm)

                def turn_kept(b):
                    M.done(pe, "a_top", b)
                    M.done(pe, "a_kT", b - 1)
                    for k in range(TPB):
                        for t in range(TPB):
                            mm = nc.tensor.transpose(ps[:, 4, k * S + t * P:k * S + t * P + P], kept[:, t, k * P:k * P + P], ident[:, :])
                    M.mark("a_keptT", mm)

                def attend(b):
                    M.done(pe, "a_kT", b)
                    M.done(pe, "a_vs", b)
                    M.done(pe, "a_x", b - 1)
                    for t in range(TPB):
                        for k in range(TPB):
                            mm = nc.tensor.matmul(ps[:, 5, t * P:t * P + P], kT2[:, k, t * P:t * P + P], vn[:, k, :],
                                                  start=(k == 0), stop=(k == TPB - 1))
                    M.mark("a_out", mm)

                staged_batches(pe, 1, [(0, turn), (0, project), (0, score), (1, turn_kept), (1, attend)])

            @block.scalar
            def _(act):
                M.give("ACT", act)
                act.wait_ge(a_in, 48)

                def evac_qk(b):
                    M.done(act, "a_qkv", b)
                    M.done(act, "a_scores", b - 1)
                    nc.scalar.activation(qT[:, :], ps[:, 1, 0:S], ACT.Identity, bias=bcol[:, 0:1])
                    M.mark("a_qk", nc.scalar.activation(kT[:, :], ps[:, 1, S:2 * S], ACT.Identity, bias=bcol[:, 1:2]))

                def evac_scores(b):
                    M.done(act, "a_scores", b)
                    M.done(act, "a_top", b - 1)
                    M.mark("a_s", nc.scalar.activation(sc[:, :, :].rearrange("p t s -> p (t s)"), ps[:, 3, :], ACT.Copy))

                def evac_kept(b):
                    M.done(act, "a_keptT", b)
                    M.done(act, "a_out", b - 1)
                    M.mark("a_kT", nc.scalar.activation(kT2[:, :, :].rearrange("p t s -> p (t s)"), ps[:, 4, :], ACT.Copy))

                def evac_v(b):
                    M.done(act, "a_qkv", b)
                    M.done(act, "a_out", b - 1)
                    M.mark("a_vs", nc.scalar.activation(vn[:, :, :].rearrange("p t d -> p (t d)"), ps[:, 2, 0:TPB * D], ACT.Copy))

                staged_batches(act, 1, [(0, evac_qk), (1, evac_kept), (0, evac_scores), (0, evac_v)])

            @block.vector
            def _(dve):
                M.give("DVE", dve)
                dve.wait_ge(a_in, 48)

                def normalise(b):
                    M.done(dve, "a_turned", b - 1)
                    for t in range(TPB):
                        ins = nc.vector.tensor_scalar(xn[:, t, :], x[:, bass.ds(b * TPB + t, 1), :].rearrange("p o d -> p (o d)"),
                                                      mv[:, 1, bass.ds(b * TPB + t, 1)], mv[:, 6, bass.ds(b * TPB + t, 1)],
                                                      ALU.subtract, ALU.mult)
                    M.mark("a_norm", ins)

                def modulate(b):
                    M.done(dve, "a_turned", b)
                    M.done(dve, "a_qkv", b - 1)
                    M.mark("a_hTs", nc.vector.tensor_scalar(hT[:, :], ps[:, 0, 0:S], colmod[:, 1, bass.ds(b, 1)],
                                                            colmod[:, 0, bass.ds(b, 1)], ALU.mult, ALU.add))

                def top(b):
                    link = Chain(dve, topch, 2 * TOPK // 8 + 1, b, gate)
                    M.done(dve, "a_s", b)
                    M.done(dve, "a_keptT", b - 1)
                    dve.sem_inc(gate, 1)
                    for r in range(TOPK // 8):
                        src = sc if r == 0 else work
                        for t in range(TPB):
                            ins = nc.vector.max(m8[:, t, :], src[:, t, :])
                        link(ins)
                        for t in range(TPB):
                            ins = nc.vector.match_replace(work[:, t, :], m8[:, t, :], src[:, t, :], NEG)
                        link(ins)
                    for t in range(TPB):
                        ins = nc.vector.scalar_tensor_tensor(kept[:, t, :], work[:, t, :], NEG, sc[:, t, :], ALU.is_equal, ALU.mult,
                                                             accum_out=den[:, t:t + 1])
                    M.mark("a_top", ins)
                    M.done(dve, "a_top", b)
                    link(nc.vector.tensor_scalar(den[:, :], den[:, :], 1e-10, None, ALU.add))
                    nc.vector.reciprocal(rden[:, :], den[:, :]).then_inc(M.s["a_den"], 1)
                    link.end()

                def residual(b):
                    link = Chain(dve, resch, 1, b)
                    M.done(dve, "a_out", b)
                    M.done(dve, "a_den", b)
                    for t in range(TPB):
                        ins = nc.vector.scalar_tensor_tensor(upd[:, t, :], ps[:, 5, t * P:t * P + P], rden[:, t:t + 1],
                                                             rows[:, bass.ds(b, 1), 0, :].rearrange("p o d -> p (o d)"), ALU.mult, ALU.mult)
                    link(ins)
                    xt = x[:, bass.ds(b * TPB, TPB), :]
                    M.mark("a_x", nc.vector.tensor_tensor(xt, xt, upd[:, :, :], ALU.add))
                    M.done(dve, "a_x", b)

                staged_batches(dve, 1, [(0, normalise), (0, modulate), (1, residual), (0, top)])


def into_y(nc, sem, x, y, mv, rows):
    s = sem("into_y")
    with nc.Block() as block:
        @block.vector
        def _(dve):
            for t in range(NT):
                nc.vector.tensor_scalar(y[:, t, :], x[:, t, :], mv[:, 1, t:t + 1], mv[:, 6, t:t + 1], ALU.subtract, ALU.mult).then_inc(s, 1)
            dve.wait_ge(s, NT)
            yv = y[:, :, :].rearrange("p (b t) d -> p b t d", t=TPB)
            nc.vector.tensor_tensor(yv, yv, view(rows, 0, P, 2 * D, [[4 * D, B], [0, TPB], [1, D]]), ALU.mult).then_inc(s, 1)
            dve.wait_ge(s, NT + 1)
            nc.vector.tensor_tensor(yv, yv, view(rows, 0, P, D, [[4 * D, B], [0, TPB], [1, D]]), ALU.add).then_inc(s, 1)
            dve.wait_ge(s, NT + 2)


def add_gated(nc, sem, x, y, rows):
    s = sem("add_y")
    with nc.Block() as block:
        @block.vector
        def _(dve):
            yv = y[:, :, :].rearrange("p (b t) d -> p b t d", t=TPB)
            nc.vector.tensor_tensor(yv, yv, view(rows, 0, P, 3 * D, [[4 * D, B], [0, TPB], [1, D]]), ALU.mult).then_inc(s, 1)
            dve.wait_ge(s, 1)
            nc.vector.tensor_tensor(x[:, :, :], x[:, :, :], y[:, :, :], ALU.add).then_inc(s, 1)
            dve.wait_ge(s, 2)


H3, D3, W3 = 16, 8, 16
G3 = 8
PAIRS = S // (2 * G3)
BLKS = S // G3
CB = 4
CHUNKS = BLKS // CB
AT_PIECE = {1: ("block", 6), 3: ("block", 7), 4: ("out", 1), 5: ("turn",), 6: ("project", 0), 7: ("project", 1),
            9: ("block", 0), 10: ("block", 1), 11: ("block", 2), 12: ("block", 3), 13: ("block", 4),
            14: ("out", 0), 15: ("block", 5)}


def third_order_attention(nc, a, sem, ps, x, y, mv, colmod, rows, ident, identb):
    with ExitStack() as ctx:
        sb = lambda n, s, d=F32: ctx.enter_context(nc.sbuf_tensor(n, s, d))
        pad = W3 - 1
        half = S // 2
        w = sb("d_w", [P, 5, D])
        bd = sb("d_bd", [P, H3])
        mask_in, mask = sb("d_mask_in", [P, 3, 3 * P]), sb("d_mask", [P, 3, 3 * P], BF16)
        xn, hT, hTo = sb("d_xn", [P, TPB, D]), sb("d_hT", [P, S]), sb("d_hTo", [P, S])
        QT, KT, KpT = sb("d_QT", [P, S]), sb("d_KT", [P, pad + S]), sb("d_KpT", [P, S])
        VTn, VT = sb("d_VTn", [P, S]), sb("d_VT", [P, pad + S])
        U = sb("d_U", [P, S, W3])
        KBD, VBD = sb("d_KBD", [P, 2 + BLKS, P]), sb("d_VBD", [P, 2 + BLKS, P])
        VTrep = sb("d_VTrep", [P, 2, CB, H3, G3])
        onesBD = sb("d_onesBD", [P, P])
        mx, mxh = sb("d_mx", [P, 2, 2, G3]), sb("d_mxh", [2 * G3, 2, H3])
        mxr = sb("d_mxr", [2 * G3, 2, H3, G3])
        hi, lo = sb("d_hi", [P, 2, 2 * G3], BF16), sb("d_lo", [P, 2, 2 * G3], BF16)
        pr = sb("d_pr", [P, 2, 2, 3 * P])
        psum = sb("d_psum", [P, 2, 2, P])
        wv = sb("d_wv", [P, 2, 2 * P])
        zs, dn, rdn = sb("d_zs", [P, 2, 2 * G3]), sb("d_dn", [P, 2, 2 * G3]), sb("d_rdn", [P, 2, 2 * G3])
        ZT = sb("d_ZT", [P, S])
        M = Marks(sem,
                  DVE=("d_norm", "d_hTs", "d_mx", "d_mxh", "d_hl", "d_z", "d_vbd", "d_zd"),
                  PE=("d_turned", "d_proj", "d_vt", "d_a", "d_t", "d_r", "d_sub", "d_w_", "d_o"),
                  ACT=("d_pj", "d_exp", "d_vr", "d_vc", "d_hc", "d_oy"), POOL=("d_ukbd", "d_ps", "d_psa"))
        d_in, once, z_ch, h_ch, r_ch, act_gate = (sem(n) for n in ("d_in", "d_once", "d_zch", "d_hch", "d_rch", "d_actg"))
        with nc.Block() as block:
            @block.sync
            def _(sp):
                for dst, key in ((w[:, :, :], "d_w"), (bd[:, :], "d_bd"), (mask_in[:, :, :], "d_mask")):
                    sp.dma_start(dst, a[key]).then_inc(d_in, 16)

            @block.vector
            def _(dve):
                M.give("DVE", dve)
                v = nc.vector
                for t in (KT, VT):
                    v.memset(t[:, 0:pad], 0.0).then_inc(once, 1)
                for t in (KBD, VBD):
                    v.memset(t[:, 0:2, :], 0.0).then_inc(once, 1)
                dve.wait_ge(d_in, 48)
                v.tensor_copy(mask[:, :, :], mask_in[:, :, :]).then_inc(once, 1)
                v.tensor_copy(onesBD[:, :].rearrange("p (h d) -> p h d", d=D3), view(bd, 0, P, 0, [[1, H3], [0, D3]])).then_inc(once, 1)
                dve.wait_ge(once, 6)

            @block.tensor
            def _(pe):
                M.give("PE", pe)

            @block.scalar
            def _(act):
                M.give("ACT", act)

            @block.gpsimd
            def _(pool):
                M.give("POOL", pool)

        def groups(gp):
            return [2 * gp, 2 * gp + 1]

        def is_batch(n, k):
            return type(n) is int and n == k

        def blocks_free(eng, n, q):
            if not is_batch(n, 0) or q > CHUNKS - 3:
                M.done(eng, "d_w_", PAIRS * (n - 1) + min(2 * q + 2, PAIRS - 1))

        def batches(eng, slot, piece, lags):
            def pieces(b, s, first, last):
                what = AT_PIECE.get(s)
                if what is None or (what == ("out", 1) and first):
                    return
                own = what[0] == "out" or (what[0] == "block" and what[1] > CHUNKS - 3)
                if last and not own:
                    return
                piece(what, b - 1 if what == ("out", 1) else b if own else b + 1, last)

            def body(b, first=False, last=False):
                for s in range(PAIRS):
                    slot(b, s, first, lambda: pieces(b, s, first, last))
            for s in (5, 6, 7, 9, 10, 11, 12, 13, 15):
                piece(AT_PIECE[s], 0, False)
            body(0, first=True)
            with eng.Fori(1, B - 1) as b:
                body(b)
            body(B - 1, last=True)
            for s in range(lags):
                slot(B, s, False, lambda: None, tail=True)
            piece(("out", 1), B - 1, True)

        def late(b, s, lag, first, fn):
            if s >= lag:
                fn(b, s - lag)
            elif not first:
                fn(b - 1, s - lag + PAIRS)

        with nc.Block() as block:
            @block.tensor
            def _(pe):
                def piece(what, n, last):
                    if what[0] == "turn":
                        M.done(pe, "d_norm", n)
                        M.done(pe, "d_oy", 2 * n - 3)
                        for t in range(TPB):
                            mm = nc.tensor.transpose(ps[:, 7, t * P:t * P + P], xn[:, t, :], ident[:, :])
                        M.mark("d_turned", mm)
                    elif what[0] == "project":
                        M.done(pe, "d_hTs", n)
                        M.done(pe, "d_pj", 2 * n + what[1] - 1)
                        for m in range(2):
                            mm = nc.tensor.matmul(ps[:, 7, m * S:m * S + S], w[:, 2 * what[1] + m, :], hT[:, :], start=True, stop=True)
                        M.mark("d_proj", mm)
                    elif what[0] == "block":
                        q = what[1]
                        M.done(pe, "d_vr", CHUNKS * n + q)
                        M.done(pe, "d_vbd", CHUNKS * n + q - 1)
                        if q == 0:
                            M.done(pe, "d_pj", 2 * n + 1)
                        if q == 5:
                            M.done(pe, "d_oy", 2 * n - 2)
                        for k in range(CB):
                            mm = nc.tensor.transpose(ps[:, 7, k * P:k * P + P], VTrep[:, q % 2, k, :, :].rearrange("p h s -> p (h s)"), ident[:, :])
                        M.mark("d_vt", mm)
                    else:
                        t = what[1]
                        M.done(pe, "d_z", PAIRS * n + (PAIRS // 2) * (t + 1) - 1)
                        M.done(pe, "d_hc", n)
                        M.done(pe, "d_oy", 2 * n + t - 1)
                        if not last:
                            M.done(pe, "d_vbd", CHUNKS * (n + 1) + (4 if t == 0 else 7))
                        elif t == 1:
                            M.done(pe, "d_vbd", CHUNKS * B - 1)
                        nc.tensor.matmul(ps[:, 7, 0:D], ZT[:, t * P:t * P + P], w[:, 4, :], start=True, stop=False)
                        M.mark("d_o", nc.tensor.matmul(ps[:, 7, 0:D], hTo[:, t * P:t * P + P], ident[:, :], start=False, stop=True))

                def score(b, gp, gi):
                    u = PAIRS * b + gp
                    g = groups(gp)[gi]
                    bank = 1 + 2 * (gp % 2) + gi
                    if gi == 0:
                        M.done(pe, "d_exp", u - 2)
                        M.done(pe, "d_ukbd", CHUNKS * b + gp // 2)
                    nc.tensor.matmul(ps[:, bank, 0:3 * P], identb[:, :], mask[:, min(g, 2), :], start=True, stop=False,
                                     skip_group_check=True)
                    for k in range(3):
                        mm = nc.tensor.matmul(ps[:, bank, k * P:k * P + P], KBD[:, g + k, :],
                                              U[:, g * G3:g * G3 + G3, :].rearrange("p s j -> p (s j)"),
                                              start=False, stop=(k == 2), skip_group_check=True)
                    M.mark("d_a", mm)

                def turn_max(b, gp):
                    u = PAIRS * b + gp
                    M.done(pe, "d_mx", u)
                    M.done(pe, "d_hl", u - 1)
                    M.mark("d_t", nc.tensor.transpose(ps[0:2 * G3, 0, 0:P], mx[:, gp % 2, :, :].rearrange("p g s -> p (g s)"), ident[:, :]))

                def spread_max(b, gp):
                    u = PAIRS * b + gp
                    M.done(pe, "d_mxh", u)
                    M.mark("d_r", nc.tensor.matmul(ps[:, 0, 128:128 + 2 * G3], mxr[:, gp % 2, :, :].rearrange("p h s -> p (h s)"),
                                                   ident[0:2 * G3, 0:2 * G3], start=True, stop=True))

                def subtract_max(b, gp):
                    u = PAIRS * b + gp
                    M.done(pe, "d_hl", u)
                    for gi in range(2):
                        for part in (hi, lo):
                            mm = nc.tensor.matmul(ps[:, 1 + 2 * (gp % 2) + gi, 0:3 * P], identb[:, :],
                                                  view(part, 0, P, (gp % 2) * 2 * G3 + gi * G3, [[0, 3], [1, G3], [0, W3]]),
                                                  start=False, stop=True, skip_group_check=True)
                    M.mark("d_sub", mm)

                def weigh(b, gp, gi):
                    u = PAIRS * b + gp
                    if gi == 0:
                        M.done(pe, "d_exp", u)
                        M.done(pe, "d_vbd", CHUNKS * b + gp // 2)
                        M.done(pe, "d_zd", u - 1)
                    for k in range(3):
                        mm = nc.tensor.matmul(ps[:, 5, gi * P:gi * P + P], VBD[:, groups(gp)[gi] + k, :],
                                              pr[:, gp % 2, gi, k * P:k * P + P], start=(k == 0), stop=(k == 2))
                    if gi == 1:
                        M.done(pe, "d_ps", u)
                        mm = nc.tensor.matmul(ps[:, 6, 0:2 * P], onesBD[:, :], psum[:, gp % 2, :, :].rearrange("p g n -> p (g n)"),
                                              start=True, stop=True)
                        M.mark("d_w_", mm)

                def slot(b, s, first, piece_now, tail=False):
                    if s < 1 or not tail:
                        late(b, s, 1, first, turn_max)
                    if not tail:
                        score(b, s, 0)
                    if s < 1 or not tail:
                        late(b, s, 1, first, spread_max)
                    if not tail:
                        score(b, s, 1)
                    piece_now()
                    late(b, s, 2, first, lambda n, gp: weigh(n, gp, 0))
                    if s < 1 or not tail:
                        late(b, s, 1, first, subtract_max)
                    late(b, s, 2, first, lambda n, gp: weigh(n, gp, 1))

                batches(pe, slot, piece, 2)

            @block.scalar
            def _(act):
                def evacuate(c, n):
                    M.done(act, "d_proj", 2 * n + c)
                    M.done(act, "d_ukbd", CHUNKS * n - 1)
                    if c == 0:
                        nc.scalar.activation(QT[:, :], ps[:, 7, 0:S], ACT.Copy, scale=float(D3) ** -0.5)
                        M.mark("d_pj", nc.scalar.activation(KT[:, pad:pad + S], ps[:, 7, S:2 * S], ACT.Copy))
                    else:
                        M.done(act, "d_vr", CHUNKS * n - 1)
                        M.done(act, "d_vc", 2 * n - 1)
                        nc.scalar.activation(KpT[:, :], ps[:, 7, 0:S], ACT.Copy)
                        M.mark("d_pj", nc.scalar.activation(VTn[:, :], ps[:, 7, S:2 * S], ACT.Copy))

                def repeat_v(n, q):
                    M.done(act, "d_pj", 2 * n + 1)
                    M.done(act, "d_vt", CHUNKS * n + q - 2)
                    M.mark("d_vr", nc.scalar.activation(VTrep[:, q % 2, :, :, :], view(VTn, 0, P, q * CB * G3, [[G3, CB], [0, H3], [1, G3]]), ACT.Copy))

                def take_v(b, part):
                    M.done(act, "d_pj", 2 * b + 1)
                    M.done(act, "d_zd", PAIRS * (b - 1) + (PAIRS // 2 if part == 0 else PAIRS - 1))
                    M.mark("d_vc", nc.scalar.activation(VT[:, pad + part * half:pad + part * half + half], VTn[:, part * half:part * half + half], ACT.Copy))

                def take_h(b):
                    M.done(act, "d_hTs", b)
                    M.done(act, "d_o", 2 * b - 1)
                    M.mark("d_hc", nc.scalar.activation(hTo[:, :], hT[:, :], ACT.Copy))

                def keep_out(n, t):
                    M.done(act, "d_o", 2 * n + t)
                    act.sem_inc(act_gate, 1)
                    M.mark("d_oy", nc.scalar.activation(y[:, bass.ds(n * TPB + t, 1), :].rearrange("p o d -> p (o d)"), ps[:, 7, 0:D], ACT.Copy))

                def piece(what, n, last):
                    if what[0] == "project":
                        evacuate(what[1], n)
                    elif what[0] == "block" and is_batch(n, 0) and what[1] < CHUNKS - 2:
                        repeat_v(n, what[1])
                    elif what[0] == "out" and what[1] == 1 and is_batch(n, B - 1):
                        keep_out(n, 1)

                def exps(b, gp):
                    u = PAIRS * b + gp
                    M.done(act, "d_sub", u)
                    M.done(act, "d_w_", u - 2)
                    M.done(act, "d_ps", u - 2)
                    bank = 1 + 2 * (gp % 2)
                    M.mark("d_exp", nc.scalar.activation(pr[:, gp % 2, :, :], ps[:, bank:bank + 2, 0:3 * P], ACT.Exp))

                def slot(b, s, first, piece_now, tail=False):
                    if not tail:
                        before = AT_PIECE.get(s - 1)
                        now = AT_PIECE.get(s)
                        more = not is_batch(b, B - 1)
                        if before == ("out", 1) and not first:
                            keep_out(b - 1, 1)
                        if before == ("out", 0):
                            keep_out(b, 0)
                        if before is not None and before[0] == "project" and more:
                            evacuate(before[1], b + 1)
                        if s in (0, 3):
                            take_v(b, s // 3)
                        if s == 5:
                            take_h(b)
                        if now is not None and now[0] == "block":
                            own = now[1] > CHUNKS - 3
                            if own or more:
                                repeat_v(b if own else b + 1, now[1])
                    if s < 1 or not tail:
                        late(b, s, 1, first, exps)

                def first_piece(what, n, last):
                    if is_batch(n, 0) or what == ("out", 1):
                        piece(what, n, last)
                started = []

                def once_piece(what, n, last):
                    if not started or is_batch(n, B - 1):
                        first_piece(what, n, last)
                        if what == ("block", 5):
                            started.append(True)
                batches(act, slot, once_piece, 1)

            @block.gpsimd
            def _(pool):
                def piece(what, n, last):
                    if what[0] == "block":
                        q = what[1]
                        M.done(pool, "d_pj", 2 * n + 1)
                        blocks_free(pool, n, q)
                        b0, t0 = q * CB, q * CB * G3
                        nc.gpsimd.tensor_tensor(view(KBD, 0, P, (2 + b0) * P, [[P, CB], [G3, H3], [1, G3]]),
                                                view(KpT, 0, P, t0, [[G3, CB], [0, H3], [1, G3]]),
                                                view(bd, 0, P, 0, [[0, CB], [1, H3], [0, G3]]), ALU.mult)
                        M.mark("d_ukbd", nc.gpsimd.tensor_tensor(U[:, t0:t0 + CB * G3, :], view(QT, 0, P, t0, [[1, CB * G3], [0, W3]]),
                                                                 view(KT, 0, P, t0, [[1, CB * G3], [1, W3]]), ALU.mult))

                def add_up(b, gp):
                    u = PAIRS * b + gp
                    M.done(pool, "d_exp", u)
                    M.done(pool, "d_w_", u - 2)
                    M.mark("d_psa", nc.gpsimd.tensor_tensor(psum[:, gp % 2, :, :], pr[:, gp % 2, :, 0:P], pr[:, gp % 2, :, P:2 * P], ALU.add))
                    M.done(pool, "d_psa", u)
                    M.mark("d_ps", nc.gpsimd.tensor_tensor(psum[:, gp % 2, :, :], psum[:, gp % 2, :, :], pr[:, gp % 2, :, 2 * P:3 * P], ALU.add))

                def slot(b, s, first, piece_now, tail=False):
                    if s < 1 or not tail:
                        late(b, s, 1, first, add_up)
                    piece_now()
                batches(pool, slot, piece, 1)

            @block.vector
            def _(dve):
                v = nc.vector

                def normalise(n):
                    M.done(dve, "d_turned", n - 1)
                    for t in range(TPB):
                        ins = v.tensor_scalar(xn[:, t, :], x[:, bass.ds(n * TPB + t, 1), :].rearrange("p o d -> p (o d)"),
                                              mv[:, 1, bass.ds(n * TPB + t, 1)], mv[:, 6, bass.ds(n * TPB + t, 1)],
                                              ALU.subtract, ALU.mult)
                    M.mark("d_norm", ins)

                def piece(what, n, last):
                    if what[0] == "turn":
                        if is_batch(n, 0):
                            normalise(0)
                        M.done(dve, "d_turned", n)
                        M.done(dve, "d_proj", 2 * n - 1)
                        M.done(dve, "d_hc", n - 1)
                        M.mark("d_hTs", v.tensor_scalar(hT[:, :], ps[:, 7, 0:S], colmod[:, 1, bass.ds(n, 1)],
                                                        colmod[:, 0, bass.ds(n, 1)], ALU.mult, ALU.add))
                    elif what[0] == "block":
                        q = what[1]
                        M.done(dve, "d_vt", CHUNKS * n + q)
                        blocks_free(dve, n, q)
                        M.mark("d_vbd", v.tensor_tensor(view(VBD, 0, P, (2 + CB * q) * P, [[P, CB], [D3, H3], [1, D3]]),
                                                        view(ps, 0, P, 7 * 512, [[P, CB], [D3, H3], [1, D3]]),
                                                        view(bd, 0, P, 0, [[0, CB], [1, H3], [0, D3]]), ALU.mult))

                def maxima(b, gp):
                    u = PAIRS * b + gp
                    for gi in range(2):
                        dve.wait_ge(M.s["d_a"], 2 * u + gi + 1 + CR)
                        if gi == 0:
                            M.done(dve, "d_t", u - 2)
                        ins = v.tensor_reduce(mx[:, gp % 2, gi, :], view(ps, 0, P, (1 + 2 * (gp % 2) + gi) * 512, [[W3, G3], [P, 3], [1, W3]]),
                                              mybir.AxisListType.XY, ALU.max)
                    M.mark("d_mx", ins)

                def head_maxima(b, gp):
                    u = PAIRS * b + gp
                    M.done(dve, "d_t", u)
                    M.done(dve, "d_r", u - 2)
                    link = Chain(dve, r_ch, 1, u)
                    link(v.tensor_reduce(mxh[:, gp % 2, :], view(ps, 0, 2 * G3, 0, [[G3, H3], [1, G3]]), AX, ALU.max))
                    M.mark("d_mxh", v.tensor_copy(mxr[:, gp % 2, :, :], view(mxh, 0, 2 * G3, (gp % 2) * H3, [[1, H3], [0, G3]])))

                def split_max(b, gp):
                    u = PAIRS * b + gp
                    link = Chain(dve, h_ch, 1, u)
                    M.done(dve, "d_r", u)
                    M.done(dve, "d_sub", u - 2)
                    src = ps[:, 0, 128:128 + 2 * G3]
                    link(v.tensor_scalar(hi[:, gp % 2, :], src, -1.0, None, ALU.mult))
                    M.mark("d_hl", v.scalar_tensor_tensor(lo[:, gp % 2, :], src, -1.0, hi[:, gp % 2, :], ALU.mult, ALU.subtract))

                def combine(b, gp):
                    u = PAIRS * b + gp
                    link = Chain(dve, z_ch, 2, u)
                    M.done(dve, "d_w_", u)
                    M.done(dve, "d_vc", 2 * b + gp // (PAIRS // 2))
                    M.done(dve, "d_o", 2 * (b - 1) + gp // (PAIRS // 2))
                    s0, q = 2 * G3 * gp, gp % 2
                    v.tensor_reduce(dn[:, q, :], view(ps, 0, P, 6 * 512, [[W3, 2 * G3], [1, W3]]), AX, ALU.add)
                    M.mark("d_zd", v.tensor_tensor(wv[:, q, :].rearrange("p (s j) -> p s j", j=W3),
                                                   view(ps, 0, P, 5 * 512, [[W3, 2 * G3], [1, W3]]),
                                                   view(VT, 0, P, s0, [[1, 2 * G3], [1, W3]]), ALU.mult))
                    M.done(dve, "d_zd", u)
                    v.reciprocal(rdn[:, q, :], dn[:, q, :])
                    link(v.tensor_reduce(zs[:, q, :], wv[:, q, :].rearrange("p (s j) -> p s j", j=W3), AX, ALU.add))
                    link(v.tensor_tensor(ZT[:, s0:s0 + 2 * G3], zs[:, q, :], rdn[:, q, :], ALU.mult))
                    v.sem_inc(M.s["d_z"], 1)

                def slot(b, s, first, piece_now, tail=False):
                    if s < 1 or not tail:
                        late(b, s, 1, first, head_maxima)
                        late(b, s, 1, first, split_max)
                    late(b, s, 3, first, combine)
                    if not tail:
                        maxima(b, s)
                        if s == 4 and not is_batch(b, B - 1):
                            normalise(b + 1)
                    piece_now()
                batches(dve, slot, piece, 3)

        st, mv2, lnrow = sb("d_st", [P, NT, 6]), sb("d_mv", [P, 8, NT]), sb("d_lnrow", [P, 2, D])
        ln_in, ln_st, ln_ch = sem("d_ln_in"), sem("d_ln_st"), sem("d_ln_ch")
        with nc.Block() as block:
            @block.sync
            def _(sp):
                sp.dma_start(lnrow[:, :, :], a["d_ln"]).then_inc(ln_in, 16)

            @block.vector
            def _(dve):
                v = nc.vector
                for t in range(NT):
                    v.bn_stats(st[:, t, :], y[:, t, :]).then_inc(ln_st, 1)
                dve.wait_ge(ln_st, NT)
                link = Chain(dve, ln_ch, 7 + RSQRT_OPS + 5, 0)
                mean_rstd(nc, link, st, mv2)
                for t in range(NT):
                    ins = v.tensor_scalar(y[:, t, :], y[:, t, :], mv2[:, 1, t:t + 1], mv2[:, 6, t:t + 1], ALU.subtract, ALU.mult)
                link(ins)
                dve.wait_ge(ln_in, 16)
                yv = y[:, :, :].rearrange("p (b t) d -> p b t d", t=TPB)
                link(v.tensor_tensor(y[:, :, :], y[:, :, :], view(lnrow, 0, P, 0, [[0, NT], [1, D]]), ALU.mult))
                link(v.tensor_tensor(y[:, :, :], y[:, :, :], view(lnrow, 0, P, D, [[0, NT], [1, D]]), ALU.add))
                link(v.tensor_tensor(yv, yv, view(rows, 0, P, 0, [[4 * D, B], [0, TPB], [1, D]]), ALU.mult))
                link(v.tensor_tensor(x[:, :, :], x[:, :, :], y[:, :, :], ALU.add))
                link.end()


EXPERTS, DI = 8, 512
KEEP = max(4, -(-B * S * 2 // EXPERTS))
CHUNK = 4


def expert_choice(nc, a, sem, ps, x, mv, colmod, rows, ident, ones):
    with ExitStack() as ctx:
        sb = lambda n, s, d=F32: ctx.enter_context(nc.sbuf_tensor(n, s, d))
        wr, w1, w2 = sb("e_wr", [P, EXPERTS]), sb("e_w1", [P, EXPERTS, DI]), sb("e_w2", [P, EXPERTS, DI // P, D])
        b1, b2 = sb("e_b1", [P, EXPERTS, DI // P]), sb("e_b2", [CHUNK * EXPERTS, CHUNK, D])
        below = sb("e_below", [P, P])
        xn, hT, hall = sb("e_xn", [P, TPB, D]), sb("e_hT", [P, S]), sb("e_hall", [P, NT * P])
        G, GE = sb("e_G", [P, NT, EXPERTS]), sb("e_cmp", [P, NT, EXPERTS])
        eq, rank = sb("e_eq", [P, NT, EXPERTS]), sb("e_rank", [P, NT, EXPERTS])
        tot, tot2 = sb("e_tot", [P, NT, EXPERTS]), sb("e_tot2", [P, NT, EXPERTS])
        small = sb("e_small", [P, NT])
        cnt, need, okf = sb("e_cnt", [P, EXPERTS]), sb("e_need", [P, EXPERTS]), sb("e_ok", [P, EXPERTS])
        thr, cand, bit, oki = (sb(n, [P, EXPERTS], I32) for n in ("e_thr", "e_cand", "e_bit", "e_oki"))
        g4, gT = sb("e_g4", [P, CHUNK * EXPERTS]), sb("e_gT", [CHUNK * EXPERTS, P])
        hid = sb("e_hid", [P, 2, DI // P, CHUNK * P])
        acc = sb("e_acc", [P, CHUNK, D])
        M = Marks(sem, DVE=("e_norm", "e_hTs", "e_cmpd", "e_g4s", "e_gTs", "e_acc", "e_x", "e_b"),
                  PE=("e_turned", "e_lg", "e_count", "e_gt", "e_b2s", "e_h", "e_y"), ACT=("e_log", "e_gelu", "e_copy"))
        e_in, ch, sch, bch, ach = (sem(n) for n in ("e_in", "e_ch", "e_sch", "e_bch", "e_ach"))
        loads = ((wr[:, :], "e_wr"), (w1[:, :, :], "e_w1"), (w2[:, :, :, :], "e_w2"), (b1[:, :, :], "e_b1"),
                 (b2[:, :, :], "e_b2"), (below[:, :], "e_below"))
        with nc.Block() as block:
            @block.sync
            def _(sp):
                for dst, key in loads:
                    sp.dma_start(dst, a[key]).then_inc(e_in, 16)

            @block.vector
            def _(dve):
                M.give("DVE", dve)
                dve.wait_ge(e_in, 16 * len(loads))
                v = nc.vector
                with dve.Fori(0, B) as b:
                    M.done(dve, "e_turned", b - 1)
                    for t in range(TPB):
                        ins = v.tensor_scalar(xn[:, t, :], x[:, bass.ds(b * TPB + t, 1), :].rearrange("p o d -> p (o d)"),
                                              mv[:, 1, bass.ds(b * TPB + t, 1)], mv[:, 6, bass.ds(b * TPB + t, 1)],
                                              ALU.subtract, ALU.mult)
                    M.mark("e_norm", ins)
                    M.done(dve, "e_turned", b)
                    M.done(dve, "e_lg", b - 1)
                    M.done(dve, "e_copy", b - 1)
                    M.mark("e_hTs", v.tensor_scalar(hT[:, :], ps[:, 0, 0:S], colmod[:, 4, bass.ds(b, 1)],
                                                    colmod[:, 3, bass.ds(b, 1)], ALU.mult, ALU.add))
                link = Chain(dve, sch, 5, 0)
                dve.wait_ge(M.s["e_log"], B + CR)
                bc = lambda t: view(t, 0, P, 0, [[1, NT], [0, EXPERTS]])
                link(v.tensor_reduce(small[:, :], G[:, :, :], AX, ALU.max))
                link(v.tensor_tensor(G[:, :, :], G[:, :, :], bc(small), ALU.subtract))
                dve.wait_ge(M.s["e_log"], B + 1 + CR)
                link(v.tensor_reduce(small[:, :], G[:, :, :], AX, ALU.add))
                link(v.reciprocal(small[:, :], small[:, :]))
                link(v.tensor_tensor(G[:, :, :], G[:, :, :], bc(small), ALU.mult))
                link.end()

            @block.tensor
            def _(pe):
                M.give("PE", pe)
                pe.wait_ge(e_in, 16 * len(loads))
                with pe.Fori(0, B) as b:
                    M.done(pe, "e_norm", b)
                    M.done(pe, "e_hTs", b - 1)
                    for t in range(TPB):
                        mm = nc.tensor.transpose(ps[:, 0, t * P:t * P + P], xn[:, t, :], ident[:, :])
                    M.mark("e_turned", mm)
                    M.done(pe, "e_hTs", b)
                    M.done(pe, "e_log", b - 1)
                    for t in range(TPB):
                        mm = nc.tensor.matmul(ps[:, 1, t * EXPERTS:(t + 1) * EXPERTS], hT[:, t * P:t * P + P], wr[:, :], start=True, stop=True)
                    M.mark("e_lg", mm)

            @block.scalar
            def _(act):
                M.give("ACT", act)
                with act.Fori(0, B) as b:
                    M.done(act, "e_hTs", b)
                    M.mark("e_copy", nc.scalar.activation(hall[:, bass.ds(b * S, S)], hT[:, :], ACT.Copy))
                    M.done(act, "e_lg", b)
                    M.mark("e_log", nc.scalar.activation(G[:, bass.ds(b * TPB, TPB), :].rearrange("p t e -> p (t e)"),
                                                         ps[:, 1, 0:TPB * EXPERTS], ACT.Copy))
                act.wait_ge(sch, 2)
                M.mark("e_log", nc.scalar.activation(G[:, :, :], G[:, :, :], ACT.Exp))

        BITS = 30
        with nc.Block() as block:
            @block.vector
            def _(dve):
                v = nc.vector
                over = lambda t: view(t, 0, P, 0, [[0, NT], [1, EXPERTS]])
                link = Chain(dve, ch, 2, 0)
                link(v.memset(thr[:, :], 0))
                link(v.memset(bit[:, :], 1 << (BITS - 1)))
                with dve.Fori(0, BITS) as i:
                    link = Chain(dve, bch, 6, i)
                    link(v.tensor_tensor(cand[:, :], thr[:, :], bit[:, :], ALU.bitwise_or))
                    link(v.tensor_tensor(GE[:, :, :], G[:, :, :], over(cand).bitcast(F32), ALU.is_ge))
                    M.mark("e_cmpd", v.tensor_reduce(cnt[:, :], GE[:, :, :].rearrange("p t e -> p e t"), AX, ALU.add))
                    M.done(dve, "e_count", i)
                    link(v.tensor_scalar(oki[:, :], ps[:, 0, 0:EXPERTS], float(KEEP), None, ALU.is_ge))
                    link(v.tensor_tensor(oki[:, :], oki[:, :], bit[:, :], ALU.mult))
                    link(v.tensor_tensor(thr[:, :], thr[:, :], oki[:, :], ALU.bitwise_or))
                    link(v.tensor_scalar(bit[:, :], bit[:, :], 1, None, ALU.logical_shift_right))
                    link.end()
                link = Chain(dve, ach, 6 + 5 + 5, 0)
                thf = view(thr, 0, P, 0, [[0, NT], [1, EXPERTS]]).bitcast(F32)
                link(v.tensor_tensor(GE[:, :, :], G[:, :, :], thf, ALU.is_gt))
                link(v.tensor_tensor(eq[:, :, :], G[:, :, :], thf, ALU.is_equal))
                link(v.tensor_reduce(cnt[:, :], GE[:, :, :].rearrange("p t e -> p e t"), AX, ALU.add))
                v.sem_inc(M.s["e_cmpd"], 1)
                M.done(dve, "e_count", BITS)
                link(v.tensor_scalar(need[:, :], ps[:, 0, 0:EXPERTS], -1.0, float(KEEP), ALU.mult, ALU.add))
                link(v.tensor_copy(rank[:, :, :].rearrange("p t e -> p (t e)"), ps[:, 1, 0:NT * EXPERTS]))
                link(v.tensor_copy(tot[:, :, :].rearrange("p t e -> p (t e)"), ps[:, 2, 0:NT * EXPERTS]))
                src, dst, k = tot, tot2, 1
                while k < NT:
                    v.tensor_copy(dst[:, 0:k, :], src[:, 0:k, :])
                    link(v.tensor_tensor(dst[:, k:NT, :], src[:, k:NT, :], src[:, 0:NT - k, :], ALU.add))
                    src, dst, k = dst, src, 2 * k
                link(v.tensor_tensor(rank[:, 1:NT, :], rank[:, 1:NT, :], src[:, 0:NT - 1, :], ALU.add))
                link(v.tensor_tensor(rank[:, :, :], rank[:, :, :], view(need, 0, P, 0, [[0, NT], [1, EXPERTS]]), ALU.is_lt))
                link(v.tensor_tensor(eq[:, :, :], eq[:, :, :], rank[:, :, :], ALU.mult))
                link(v.tensor_tensor(GE[:, :, :], GE[:, :, :], eq[:, :, :], ALU.add))
                link(v.tensor_tensor(G[:, :, :], G[:, :, :], GE[:, :, :], ALU.mult))
                link.end()

            @block.tensor
            def _(pe):
                with pe.Fori(0, BITS) as i:
                    M.done(pe, "e_cmpd", i)
                    M.mark("e_count", nc.tensor.matmul(ps[:, 0, 0:EXPERTS], ones[:, :], cnt[:, :], start=True, stop=True))
                M.done(pe, "e_cmpd", BITS)
                nc.tensor.matmul(ps[:, 1, 0:NT * EXPERTS], below[:, :], eq[:, :, :].rearrange("p t e -> p (t e)"), start=True, stop=True)
                nc.tensor.matmul(ps[:, 2, 0:NT * EXPERTS], ones[:, :], eq[:, :, :].rearrange("p t e -> p (t e)"), start=True, stop=True)
                M.mark("e_count", nc.tensor.matmul(ps[:, 0, 0:EXPERTS], ones[:, :], cnt[:, :], start=True, stop=True))

        NCH = NT // CHUNK
        with nc.Block() as block:
            @block.tensor
            def _(pe):
                with pe.Fori(0, NCH) as c:
                    M.done(pe, "e_g4s", c)
                    M.mark("e_gt", nc.tensor.transpose(ps[0:CHUNK * EXPERTS, 7, 0:P], g4[:, :], ident[:, :]))

                    def up(e):
                        u = c * EXPERTS + e
                        M.done(pe, "e_gelu", u - 1)
                        for k in range(DI // P):
                            mm = nc.tensor.matmul(ps[:, k, :], w1[:, e, k * P:k * P + P], hall[:, bass.ds(c * (CHUNK * P), CHUNK * P)], start=True, stop=True)
                        M.mark("e_h", mm)

                    def down(e):
                        u = c * EXPERTS + e
                        M.done(pe, "e_gelu", u)
                        M.done(pe, "e_acc", u - 2)
                        for t in range(CHUNK):
                            for k in range(DI // P):
                                mm = nc.tensor.matmul(ps[:, 4 + e % 2, t * P:t * P + P], hid[:, e % 2, k, t * P:t * P + P], w2[:, e, k, :],
                                                      start=(k == 0), stop=(k == DI // P - 1))
                        M.mark("e_y", mm)
                    up(0)
                    M.done(pe, "e_gTs", c)
                    M.done(pe, "e_b", c - 1)
                    for t in range(CHUNK):
                        mm = nc.tensor.matmul(ps[:, 6, t * P:t * P + P], gT[:, :], b2[:, t, :], start=True, stop=True)
                    M.mark("e_b2s", mm)
                    for e in range(EXPERTS):
                        if e + 1 < EXPERTS:
                            up(e + 1)
                        down(e)

            @block.scalar
            def _(act):
                with act.Fori(0, NCH) as c:
                    for e in range(EXPERTS):
                        u = c * EXPERTS + e
                        M.done(act, "e_h", u)
                        M.done(act, "e_y", u - 2)
                        for k in range(DI // P):
                            ins = nc.scalar.activation(hid[:, e % 2, k, :], ps[:, k, :], ACT.Gelu, bias=b1[:, e, k:k + 1])
                        M.mark("e_gelu", ins)

            @block.vector
            def _(dve):
                v = nc.vector
                with dve.Fori(0, NCH) as c:
                    M.done(dve, "e_x", c - 1)
                    M.done(dve, "e_gt", c - 1)
                    M.mark("e_g4s", v.tensor_copy(g4[:, :].rearrange("p (t e) -> p t e", e=EXPERTS), G[:, bass.ds(c * CHUNK, CHUNK), :]))
                    M.done(dve, "e_gt", c)
                    M.done(dve, "e_b2s", c - 1)
                    M.mark("e_gTs", v.tensor_copy(gT[:, :], ps[0:CHUNK * EXPERTS, 7, 0:P]))
                    M.done(dve, "e_b2s", c)
                    M.mark("e_b", v.tensor_copy(acc[:, :, :].rearrange("p t d -> p (t d)"), ps[:, 6, :]))
                    M.done(dve, "e_b", c)
                    for e in range(EXPERTS):
                        u = c * EXPERTS + e
                        M.done(dve, "e_y", u)
                        for t in range(CHUNK):
                            ins = v.scalar_tensor_tensor(acc[:, t, :], ps[:, 4 + e % 2, t * P:t * P + P], g4[:, t * EXPERTS + e:t * EXPERTS + e + 1],
                                                         acc[:, t, :], ALU.mult, ALU.add)
                        M.mark("e_acc", ins)
                        M.done(dve, "e_acc", u)
                    for t in range(CHUNK):
                        bt = c * (CHUNK // TPB) + t // TPB
                        ins = v.tensor_tensor(acc[:, t, :], acc[:, t, :], rows[:, bass.ds(bt, 1), 3, :].rearrange("p o d -> p (o d)"), ALU.mult)
                    ins.then_inc(bch, 1)
                    dve.wait_ge(bch, 6 * BITS + c + 1)
                    xt = x[:, bass.ds(c * CHUNK, CHUNK), :]
                    M.mark("e_x", v.tensor_tensor(xt, xt, acc[:, :, :], ALU.add))
                    M.done(dve, "e_x", c)


def local_transformer(nc, a, sem, ps, y, ident, identb, ones):
    with ExitStack() as ctx:
        def sb(name, shape, dt=F32):
            return ctx.enter_context(nc.sbuf_tensor(name, shape, dt))

        wqkv = sb("wqkv", [P, 3 * INNER])
        wo = sb("wo", [P, HEADS // 2, D])
        w1 = sb("w1", [P, 2 * FF])
        w2 = sb("w2", [P, len(FFC), D])
        ffcols = sb("ffcols", [P, 8])
        b2row = sb("b2row", [1, D])
        scales = sb("scales", [P, 4, DH])
        tab0 = sb("tab0", [P, TPB, 4, DH])
        tab = sb("tab", [P, TPB, 4, DH])
        yl = sb("yl", [P, TPB, D])
        hT = sb("hT", [P, S])
        raw = sb("raw", [P, 2, H2, DH])
        sq = sb("sq", [P, 2, H2, DH])
        t1 = sb("t1", [P, 2, H2, DH])
        t2 = sb("t2", [P, 2, H2, DH])
        qkn = sb("qkn", [P, 2, H2, DH])
        ss = sb("ss", [P, 2 * H2])
        rn = sb("rn", [P, 2 * H2])
        rtmp = sb("rtmp", [P, 2 * H2])
        qT = sb("qT", [P, H2 // 2, P])
        kT = sb("kT", [P, HEADS // 2, WIN + S])
        V = sb("V", [P, TPB, INNER])
        Vp = sb("Vp", [P, TPB, INNER])
        maskb = sb("maskb", [P, 2, H2 // 2 * 2 * WIN], BF16)
        rowmax = sb("rowmax", [P, H2])
        sim = sb("sim", [P, H2, 2 * WIN])
        prob = sb("prob", [P, H2, 2 * WIN])
        rowsum = sb("rowsum", [P, 2, H2])
        rsum = sb("rsum", [P, 2, H2])
        pT = sb("pT", [P, 2, H2, 2, WIN])
        on = sb("on", [P, H2 // 2, P])
        oT = sb("oT", [P, H2 // 2, P])
        yf = sb("yf", [P, 2, TPB, D])
        st = sb("st", [P, TPB, 6])
        mv = sb("mv", [P, 8, TPB])
        xn = sb("xn", [P, TPB, D])
        fT = sb("fT", [P, S])
        gg = sb("gg", [P, 2, len(FFC), S])
        hid = sb("hid", [P, len(FFC), S])

        w_in, w_in2 = sem("w_in"), sem("w_in2")
        tab_sem = sem("tab_ready")
        N = {k: sem(k) for k in (
            "yl_ready", "hT_ps", "hT_sb", "proj_ps", "raw_sb", "v_sb", "sq_sb", "ropech", "summed", "normed",
            "qkT_ps", "qkT_sb", "sim_ps", "smch", "shifted", "prob_sb", "sumch", "pT_sb", "pv_ps", "on_sb",
            "oT_ps", "oT_sb", "wo_ps", "y_sum", "rn_sb",
            "f_yl0", "f_yl1", "f_lnch", "f_xn", "f_hT_ps", "f_hT", "f_a_ps", "f_gate_ps", "f_g", "f_hid", "f_o_ps", "f_y", "f_dve_gate", "f_pe_gate")}
        vp_sem = [sem(f"vp_ready{u}") for u in range(UPB)]
        by = {"PE": ("hT_ps", "proj_ps", "qkT_ps", "sim_ps", "pv_ps", "oT_ps", "wo_ps", "f_hT_ps", "f_a_ps", "f_gate_ps", "f_o_ps"),
              "ACT": ("hT_sb", "raw_sb", "v_sb", "sq_sb", "qkT_sb", "prob_sb", "oT_sb", "f_g"),
              "DVE": ("summed", "rn_sb", "shifted", "pT_sb", "on_sb", "y_sum", "f_xn", "f_hT", "f_hid", "f_y"),
              "POOL": ("normed",)}

        def credit(eng, who):
            for k in by[who]:
                eng.sem_inc(N[k], CR * PER_UNIT.get(k, 1))

        once = sem("lt_once")
        pe_gate, sp_gate = sem("pe_gate"), sem("sp_gate")
        with nc.Block() as block:
            @block.sync
            def _(sp):
                sp.dma_start(tab0[:, :, :, :], a["tables"]).then_inc(once, 16)
                sp.wait_ge(once, 16)

            @block.tensor
            def _(pe):
                credit(pe, "PE")

            @block.scalar
            def _(act):
                credit(act, "ACT")

            @block.gpsimd
            def _(pool):
                credit(pool, "POOL")
                lt_m = sem("lt_mask")
                nc.gpsimd.memset(maskb[:, :, :], 0.0).then_inc(lt_m, 1)
                pool.wait_ge(lt_m, 1)
                k = 1
                for v in range(2):
                    for w in range(4):
                        part = maskb[32 * w:32 * w + 32, v, :].rearrange("p (h c) -> p h c", c=2 * WIN)
                        low = WIN if (v == 0 and w == 0) else 0
                        if low:
                            nc.gpsimd.memset(part[:, :, 0:low], MASKED).then_inc(lt_m, 1)
                            k += 1
                            pool.wait_ge(lt_m, k)
                        else:
                            nc.gpsimd.affine_select(out=part, in_=part, compare_op=ALU.is_ge, fill=MASKED, base=0,
                                                    pattern=[[0, H2 // 2], [1, 2 * WIN]], channel_multiplier=-1).then_inc(lt_m, 1)
                            k += 1
                            pool.wait_ge(lt_m, k)
                        nc.gpsimd.affine_select(out=part, in_=part, compare_op=ALU.is_ge, fill=MASKED, base=WIN,
                                                pattern=[[0, H2 // 2], [-1, 2 * WIN]], channel_multiplier=1).then_inc(lt_m, 1)
                        k += 1
                        pool.wait_ge(lt_m, k)

            @block.vector
            def _(dve):
                credit(dve, "DVE")
                z = sem("lt_zero")
                nc.vector.memset(yl[0:1, 0, D // 2:D], 0.0).then_inc(z, 1)
                nc.vector.memset(yf[0:1, :, 0, D // 2:D], 0.0).then_inc(z, 1)
                nc.vector.memset(kT[:, :, 0:WIN], 0.0).then_inc(z, 1)
                nc.vector.memset(Vp[0:32, 0, :], 0.0).then_inc(z, 1)
                dve.wait_ge(z, 4)

        def load_shifted(sp, dst, b, ready):
            half = slice(D // 2, D)
            sp.dma_start(dst[:, :, 0:D // 2], y[:, bass.ds(TPB * b, TPB), 0:D // 2]).then_inc(ready, 16)
            sp.dma_start(dst[1:P, :, half], y[0:P - 1, bass.ds(TPB * b, TPB), half]).then_inc(ready, 16)
            sp.dma_start(dst[0:1, 1:2, half], y[P - 1:P, bass.ds(TPB * b, 1), half]).then_inc(ready, 16)

        LAGS = 6
        PEELED = -(-LAGS // UPB)
        units_left = [0]

        def staged(eng, i, stages):
            def slots(b, first, last):
                for j in range(LAGS if last else UPB):
                    for lag, fn in stages:
                        k = j - lag
                        if (first and b * UPB + k < 0) or (last and k >= 0):
                            continue
                        units_left[0] = -k - 1 if last else UPB
                        fn(i * (B * UPB) + b * UPB + k, k % UPB, b + k // UPB)
            for b in range(PEELED):
                slots(b, True, False)
            with eng.Fori(PEELED, B) as b:
                slots(b, False, False)
            slots(B, False, True)

        with nc.Fori(0, DEPTH) as i:
            with nc.Block() as block:
                @block.sync
                def _(sp):
                    sp.dma_start(wqkv[:, :], a["Wqkv"][bass.ds(i, 1), :, :].rearrange("o p n -> p (o n)")).then_inc(w_in, 16)
                    sp.dma_start(wo[:, :, :], a["Wo"][bass.ds(i, 1), :, :, :].rearrange("o p c n -> p (o c) n")).then_inc(w_in, 16)
                    sp.dma_start(scales[:, :, :], a["scales"][bass.ds(i, 1), :, :, :].rearrange("o p c n -> p (o c) n")).then_inc(w_in, 16)

                    def load(U, u, b):
                        if u == 0:
                            sp.wait_ge(N["hT_ps"], U - UPB + 1 + CR)
                            load_shifted(sp, yl, b, N["yl_ready"])

                    def shift_v(U, u, b):
                        t, c = u // 2, slice((u % 2) * 512, (u % 2) * 512 + 512)
                        sp.wait_ge(N["v_sb"], U + 1 + CR)
                        sp.sem_inc(sp_gate, 1)
                        if t == 0:
                            sp.wait_ge(N["pv_ps"], (U - 2 + 1 + CR) * 4)
                            sp.dma_start(Vp[0:32, 1, c], V[96:128, 0, c]).then_inc(vp_sem[u], 16)
                        else:
                            sp.wait_ge(N["pv_ps"], (U - 4 + 1 + CR) * 4)
                        sp.dma_start(Vp[32:128, t, c], V[0:96, t, c]).then_inc(vp_sem[u], 16)

                    staged(sp, i, [(0, load), (3, shift_v)])

                @block.tensor
                def _(pe):
                    pe.wait_ge(w_in, 16 * 3 * (i + 1))

                    def turn_qk(U, u, b):
                        pe.wait_ge(N["normed"], U + 1 + CR)
                        pe.wait_ge(N["oT_sb"], U - 4 + 1 + CR)
                        pe.wait_ge(N["y_sum"], U - 4 + 1 + CR)
                        for qk in range(2):
                            for hp in range(H2 // 2):
                                mm = nc.tensor.transpose(ps[:, 3 + qk, hp * P:hp * P + P],
                                                         qkn[:, qk, 2 * hp:2 * hp + 2, :].rearrange("p h d -> p (h d)"), ident[:, :])
                        mm.then_inc(N["qkT_ps"], 1)

                    def project(U, u, b):
                        t, c = u // 2, (u % 2) * 512
                        if u == 0:
                            pe.wait_ge(N["hT_sb"], U + 4 + CR)
                        pe.wait_ge(N["v_sb"], U - 1 + 1 + CR)
                        pe.wait_ge(N["raw_sb"], U - 1 + 1 + CR)
                        pe.wait_ge(N["sq_sb"], U - 1 + 1 + CR)
                        for m in range(3):
                            mm = nc.tensor.matmul(ps[:, m, :], hT[:, t * P:t * P + P], wqkv[:, m * INNER + c:m * INNER + c + 512],
                                                  start=True, stop=True)
                        mm.then_inc(N["proj_ps"], 1)

                    def turn_h(U, u, b):
                        if u == 0:
                            pe.wait_ge(N["yl_ready"], (i * B + b) * 48 + 48)
                            pe.wait_ge(N["qkT_sb"], U - 2 + 1 + CR)
                            for t in range(TPB):
                                mm = nc.tensor.transpose(ps[:, 4, t * P:t * P + P], yl[:, t, :], ident[:, :])
                            mm.then_inc(N["hT_ps"], 4)

                    def turn_o(U, u, b):
                        pe.wait_ge(N["on_sb"], U + 1 + CR)
                        pe.wait_ge(N["qkT_sb"], U + min(3, units_left[0]) + 1 + CR)
                        for hp in range(H2 // 2):
                            mm = nc.tensor.transpose(ps[:, 3, hp * P:hp * P + P], on[:, hp, :], ident[:, :])
                        mm.then_inc(N["oT_ps"], 1)

                    def scores(U, u, b):
                        t, c = u // 2, (u % 2) * (H2 // 2)
                        pe.wait_ge(N["qkT_sb"], U + 1 + CR)
                        pe.wait_ge(N["shifted"], U - 1 + 1 + CR)
                        for odd in range(2):
                            nc.tensor.matmul(ps[:, 5 + odd, 0:256], identb[:, :], maskb[:, t, :], start=True, stop=False,
                                             skip_group_check=True)
                        for h in range(H2):
                            r = 64 * (h % 2)
                            for w in range(4):
                                mm = nc.tensor.matmul(ps[32 * w:32 * w + 32, 5 + h % 2, (h // 2) * 64:(h // 2) * 64 + 64],
                                                      qT[r:r + 64, h // 2, 32 * w:32 * w + 32],
                                                      kT[r:r + 64, c + h // 2, t * P + 32 * w:t * P + 32 * w + 64],
                                                      start=False, stop=(h >= H2 - 2), skip_group_check=True)
                            if h >= H2 - 2:
                                mm.then_inc(N["sim_ps"], 1)

                    def attend(U, u, b):
                        t, c = u // 2, (u % 2) * 512
                        pe.wait_ge(N["pT_sb"], U + 1 + CR)
                        pe.wait_ge(vp_sem[u], ((i * B + b) + 1) * (32 if t == 0 else 16))
                        if t == 1:
                            pe.wait_ge(vp_sem[u - 2], ((i * B + b) + 1) * 32)
                        pe.wait_ge(N["on_sb"], U - 1 + 1 + CR)
                        pe.sem_inc(pe_gate, 1)
                        for h in range(H2):
                            for part, v in ((1, V), (0, Vp)):
                                for w in range(4):
                                    mm = nc.tensor.matmul(ps[32 * w:32 * w + 32, 7, h * 64:h * 64 + 64],
                                                          pT[32 * w:32 * w + 32, u % 2, 4 * (h % 2) + h // 2, part, :],
                                                          v[32 * w:32 * w + 32, t, c + h * 64:c + h * 64 + 64],
                                                          start=(part == 1), stop=(part == 0), skip_group_check=True)
                                    if h == H2 - 1 and part == 0:
                                        mm.then_inc(N["pv_ps"], 1)

                    def out_proj(U, u, b):
                        c = (u % 2) * (H2 // 2)
                        pe.wait_ge(N["oT_sb"], U + 1 + CR)
                        pe.wait_ge(N["y_sum"], U - 1 + 1 + CR)
                        for hp in range(H2 // 2):
                            mm = nc.tensor.matmul(ps[:, 4, 0:D], oT[:, hp, :], wo[:, c + hp, :], start=(hp == 0), stop=(hp == H2 // 2 - 1))
                        mm.then_inc(N["wo_ps"], 1)

                    staged(pe, i, [(1, project), (2, turn_qk), (4, attend), (0, turn_h), (5, turn_o), (2, scores), (5, out_proj)])

                @block.scalar
                def _(act):
                    def evac_qk(U, u, b):
                        t, c = u // 2, (u % 2) * (H2 // 2)
                        act.wait_ge(N["qkT_ps"], U + 1 + CR)
                        act.wait_ge(N["sim_ps"], (U - 1 + 1 + CR) * 2)
                        nc.scalar.activation(qT[:, :, :], ps[:, 3, :].rearrange("p (c n) -> p c n", n=P), ACT.Copy)
                        nc.scalar.activation(kT[:, c:c + H2 // 2, WIN + t * P:WIN + t * P + P],
                                             ps[:, 4, :].rearrange("p (c n) -> p c n", n=P), ACT.Copy).then_inc(N["qkT_sb"], 1)

                    def evac_proj(U, u, b):
                        t, c = u // 2, (u % 2) * 512
                        act.wait_ge(N["proj_ps"], U + 1 + CR)
                        act.wait_ge(N["summed"], U - 1 + 1 + CR)
                        nc.scalar.activation(raw[:, :, :, :].rearrange("p a h d -> p (a h d)"),
                                             ps[:, 0:2, :].rearrange("p a n -> p (a n)"), ACT.Copy).then_inc(N["raw_sb"], 1)
                        act.wait_ge(N["rn_sb"], U - 1 + 1 + CR)
                        nc.scalar.activation(sq[:, :, :, :].rearrange("p a h d -> p (a h d)"),
                                             ps[:, 0:2, :].rearrange("p a n -> p (a n)"), ACT.Square).then_inc(N["sq_sb"], 1)
                        act.wait_ge(N["pv_ps"], (U - 4 + 1 + CR) * 4)
                        nc.scalar.activation(V[:, t, c:c + 512], ps[:, 2, :], ACT.Copy).then_inc(N["v_sb"], 1)

                    def evac_h(U, u, b):
                        if u == 0:
                            act.wait_ge(N["hT_ps"], U + 4 + CR)
                            act.wait_ge(N["proj_ps"], U - 1 + 1 + CR)
                            nc.scalar.activation(hT[:, :], ps[:, 4, 0:S], ACT.Copy).then_inc(N["hT_sb"], 4)

                    def evac_o(U, u, b):
                        act.wait_ge(N["oT_ps"], U + 1 + CR)
                        act.wait_ge(N["wo_ps"], U - 1 + 1 + CR)
                        nc.scalar.activation(oT[:, :, :], ps[:, 3, :].rearrange("p (c n) -> p c n", n=P), ACT.Copy).then_inc(N["oT_sb"], 1)

                    def exps(U, u, b):
                        act.wait_ge(N["shifted"], U + 1 + CR)
                        act.wait_ge(N["pT_sb"], U - 1 + 1 + CR)
                        nc.scalar.activation(prob[:, :, :], sim[:, :, :], ACT.Exp, scale=QK_SCALE).then_inc(N["prob_sb"], 1)

                    staged(act, i, [(3, exps), (1, evac_proj), (2, evac_qk), (0, evac_h), (5, evac_o)])

                @block.gpsimd
                def _(pool):
                    def normalise(U, u, b):
                        pool.wait_ge(N["rn_sb"], U + 1 + CR)
                        pool.wait_ge(N["summed"], U + 1 + CR)
                        pool.wait_ge(N["qkT_ps"], U - 1 + 1 + CR)
                        nc.gpsimd.tensor_tensor(qkn[:, :, :, :].rearrange("p a h d -> p (a h) d"),
                                                t1[:, :, :, :].rearrange("p a h d -> p (a h) d"),
                                                view(rn, 0, P, 0, [[1, 2 * H2], [0, DH]]), ALU.mult).then_inc(N["normed"], 1)
                    staged(pool, i, [(1, normalise)])

                @block.vector
                def _(dve):
                    dve.wait_ge(w_in, 16 * 3 * (i + 1))
                    nc.vector.tensor_tensor(tab[:, :, :, :].rearrange("p t c d -> p t (c d)"),
                                            tab0[:, :, :, :].rearrange("p t c d -> p t (c d)"),
                                            view(scales, 0, P, 0, [[0, TPB], [1, 4 * DH]]), ALU.mult).then_inc(tab_sem, 1)
                    dve.wait_ge(tab_sem, i + 1)

                    def rope(U, u, b):
                        t = u // 2
                        link = Chain(dve, N["ropech"], RSQRT_OPS + 3, U)
                        dve.wait_ge(N["raw_sb"], U + 1 + CR)
                        dve.wait_ge(N["normed"], U - 1 + 1 + CR)
                        nc.vector.tensor_tensor(t1[:, :, :, :], raw[:, :, :, :],
                                                view(tab, 0, P, t * 256, [[128, 2], [0, H2], [1, DH]]), ALU.mult)
                        for r in range(2):
                            ins = nc.vector.tensor_tensor(t2[:, :, :, 32 * r:32 * r + 32], raw[:, :, :, 32 - 32 * r:64 - 32 * r],
                                                          view(tab, 0, P, t * 256 + 64 + 32 * r, [[128, 2], [0, H2], [1, 32]]), ALU.mult)
                            if r == 1:
                                link(ins)
                        dve.wait_ge(N["sq_sb"], U + 1 + CR)
                        nc.vector.tensor_tensor(t1[:, :, :, :].rearrange("p a h d -> p (a h d)"),
                                                t1[:, :, :, :].rearrange("p a h d -> p (a h d)"),
                                                t2[:, :, :, :].rearrange("p a h d -> p (a h d)"), ALU.add).then_inc(N["summed"], 1)
                        link(nc.vector.tensor_reduce(ss[:, :], sq[:, :, :, :].rearrange("p a h d -> p (a h) d"), AX, ALU.add))
                        link(nc.vector.tensor_scalar(ss[:, :], ss[:, :], 1e-24, None, ALU.max))
                        rsqrt(nc, link, rn[:, :], ss[:, :], rtmp[:, :])
                        link.end()
                        dve.sem_inc(N["rn_sb"], 1)

                    def softmax_a(U, u, b):
                        link = Chain(dve, N["smch"], 1, U)
                        dve.wait_ge(N["sim_ps"], (U + 1 + CR) * 2)
                        dve.wait_ge(N["prob_sb"], U - 1 + 1 + CR)
                        s5 = view(ps, 0, P, 5 * 512, [[512, 2], [64, 4], [1, 64]])
                        link(nc.vector.tensor_reduce(rowmax[:, :].rearrange("p (a h) -> p a h", a=2), s5, AX, ALU.max))
                        nc.vector.tensor_tensor(sim[:, :, :].rearrange("p (a h) c -> p a h c", a=2), s5,
                                                view(rowmax, 0, P, 0, [[4, 2], [1, 4], [0, 64]]), ALU.subtract)\
                            .then_inc(N["shifted"], 1)
                        link.end()

                    def softmax_b(U, u, b):
                        link = Chain(dve, N["sumch"], 2, U)
                        dve.wait_ge(N["prob_sb"], U + 1 + CR)
                        dve.wait_ge(N["pv_ps"], (U - 2 + 1 + CR) * 4)
                        link(nc.vector.tensor_reduce(rowsum[:, u % 2, :], prob[:, :, :], AX, ALU.add))
                        link(nc.vector.reciprocal(rsum[:, u % 2, :], rowsum[:, u % 2, :]))
                        nc.vector.transpose(pT[:, u % 2, :, :, :].rearrange("p h a q -> p (h a q)"),
                                            prob[:, :, :].rearrange("p h c -> p (h c)")).then_inc(N["pT_sb"], 1)
                        link.end()

                    def scale_out(U, u, b):
                        dve.wait_ge(N["pv_ps"], (U + 1 + CR) * 4)
                        dve.wait_ge(N["oT_ps"], U - 1 + 1 + CR)
                        nc.vector.tensor_tensor(on[:, :, :].rearrange("p c (a d) -> p c a d", d=DH),
                                                ps[:, 7, :].rearrange("p (c a d) -> p c a d", a=2, d=DH),
                                                view(rsum, 0, P, (u % 2) * H2, [[1, 4], [4, 2], [0, DH]]), ALU.mult).then_inc(N["on_sb"], 1)

                    def residual(U, u, b):
                        dve.wait_ge(N["wo_ps"], U + 1 + CR)
                        dve.wait_ge(N["y_sum"], U - 1 + 1 + CR)
                        yt = y[:, bass.ds(b * TPB + u // 2, 1), :].rearrange("p o d -> p (o d)")
                        nc.vector.tensor_tensor(yt, ps[:, 4, 0:D], yt, ALU.add).then_inc(N["y_sum"], 1)

                    staged(dve, i, [(3, softmax_a), (6, residual), (3, softmax_b), (1, rope), (4, scale_out)])

            ffn_layer(nc, a, ps, y, ident, ones, i, N, w1, w2, ffcols, b2row, yf, st, mv, xn, fT, gg, hid, load_shifted, w_in2)


def ffn_layer(nc, a, ps, y, ident, ones, i, N, w1, w2, ffcols, b2row, yf, st, mv, xn, fT, gg, hid, load_shifted, w_in):
    NLN = 1 + 7 + RSQRT_OPS

    def hg(k, g, c):
        bank, side = {(0, 0): (0, 0), (0, 1): (0, 1), (1, 0): (1, 0), (1, 1): (1, 1), (0, 2): (2, 0), (1, 2): (2, 1)}[g, c]
        return ps[:, 1 + 3 * k + bank, side * S:side * S + S]

    with nc.Block() as block:
        @block.sync
        def _(sp):
            sp.dma_start(w1[:, :], a["W1"][bass.ds(i, 1), :, :].rearrange("o p n -> p (o n)")).then_inc(w_in, 16)
            for c, (c0, cn) in enumerate(FFC):
                sp.dma_start(w2[0:cn, c, :], a["W2"][bass.ds(i, 1), c0:c0 + cn, :].rearrange("o p n -> p (o n)")).then_inc(w_in, 16)
            sp.dma_start(ffcols[:, :], a["ffcols"][bass.ds(i, 1), :, :].rearrange("o p n -> p (o n)")).then_inc(w_in, 16)
            sp.dma_start(b2row[:, :], a["b2"][bass.ds(i, 1), :]).then_inc(w_in, 16)
            def load(b, k):
                sp.wait_ge(N["f_xn"], i * B + b - 1 + CR)
                load_shifted(sp, yf[:, k, :, :], b, N[f"f_yl{k}"])
            staged_batches(sp, 0, [(0, load)], 2)

        @block.vector
        def _(dve):
            dve.wait_ge(w_in, 16 * 6 * (i + 1))
            dve.sem_inc(N["f_dve_gate"], 1)

            def normalise(b, k):
                n = i * B + b
                link = Chain(dve, N["f_lnch"], NLN, n)
                dve.wait_ge(N[f"f_yl{k}"], 24 * (n - k) + 48)
                nc.vector.bn_stats(st[:, 0, :], yf[:, k, 0, :])
                link(nc.vector.bn_stats(st[:, 1, :], yf[:, k, 1, :]))
                mean_rstd(nc, link, st, mv)
                link.end()
                dve.wait_ge(N["f_hT_ps"], n + CR)
                for t in range(TPB):
                    ins = nc.vector.tensor_scalar(xn[:, t, :], yf[:, k, t, :], mv[:, 1, t:t + 1], mv[:, 6, t:t + 1],
                                                  ALU.subtract, ALU.mult)
                ins.then_inc(N["f_xn"], 1)

            def scale(b, k):
                n = i * B + b
                dve.wait_ge(N["f_hT_ps"], n + 1 + CR)
                dve.wait_ge(N["f_a_ps"], n + CR)
                nc.vector.tensor_scalar(fT[:, :], ps[:, 0, 0:S], ffcols[:, 0:1], ffcols[:, 1:2], ALU.mult, ALU.add)\
                    .then_inc(N["f_hT"], 1)

            def gated(b, k):
                n = i * B + b
                dve.wait_ge(N["f_g"], n + 1 + CR)
                dve.wait_ge(N["f_a_ps"], n + 1 + CR)
                dve.wait_ge(N["f_o_ps"], n + CR)
                for c, (c0, cn) in enumerate(FFC):
                    ins = nc.vector.scalar_tensor_tensor(hid[0:cn, c, :], hg(k, 0, c)[0:cn, :], ffcols[0:cn, 2 + c:3 + c],
                                                         gg[0:cn, k, c, :], ALU.add, ALU.mult)
                ins.then_inc(N["f_hid"], 1)

            def residual(b, k):
                n = i * B + b
                dve.wait_ge(N["f_o_ps"], n + 1 + CR)
                yt = y[:, bass.ds(b * TPB, TPB), :].rearrange("p t d -> p (t d)")
                nc.vector.tensor_tensor(yt, ps[:, 7, 0:S], yt, ALU.add).then_inc(N["f_y"], 1)

            staged_batches(dve, 3, [(1, scale), (2, gated), (0, normalise), (3, residual)], 2)

        @block.tensor
        def _(pe):
            pe.wait_ge(w_in, 16 * 6 * (i + 1))
            pe.sem_inc(N["f_pe_gate"], 1)

            def turn(b, k):
                n = i * B + b
                pe.wait_ge(N["f_xn"], n + 1 + CR)
                pe.wait_ge(N["f_hT"], n + CR)
                for t in range(TPB):
                    mm = nc.tensor.transpose(ps[:, 0, t * P:t * P + P], xn[:, t, :], ident[:, :])
                mm.then_inc(N["f_hT_ps"], 1)

            def up(b, k):
                n = i * B + b
                pe.wait_ge(N["f_hT"], n + 1 + CR)
                pe.wait_ge(N["f_hid"], n - 1 + CR)
                for g in (1, 0):
                    for c, (c0, cn) in enumerate(FFC):
                        mm = nc.tensor.matmul(hg(k, g, c)[0:cn, :], w1[:, g * FF + c0:g * FF + c0 + cn], fT[:, :],
                                              start=True, stop=True)
                    mm.then_inc(N["f_gate_ps" if g else "f_a_ps"], 1)

            def down(b, k):
                n = i * B + b
                pe.wait_ge(N["f_hid"], n + 1 + CR)
                pe.wait_ge(N["f_y"], n + CR)
                for t in range(TPB):
                    for c, (c0, cn) in enumerate(FFC):
                        nc.tensor.matmul(ps[:, 7, t * P:t * P + P], hid[0:cn, c, t * P:t * P + P], w2[0:cn, c, :],
                                         start=(c == 0), stop=False)
                    mm = nc.tensor.matmul(ps[:, 7, t * P:t * P + P], ones[0:1, :], b2row[0:1, :], start=False, stop=True)
                mm.then_inc(N["f_o_ps"], 1)

            staged_batches(pe, 2, [(1, up), (2, down), (0, turn)], 2)

        @block.scalar
        def _(act):
            def gelu(b, k):
                n = i * B + b
                act.wait_ge(N["f_gate_ps"], n + 1 + CR)
                act.wait_ge(N["f_a_ps"], n + 1 + CR)
                act.wait_ge(N["f_hid"], n - 1 + CR)
                for c, (c0, cn) in enumerate(FFC):
                    ins = nc.scalar.activation(gg[0:cn, k, c, :], hg(k, 1, c)[0:cn, :], ACT.Gelu, bias=ffcols[0:cn, 5 + c:6 + c])
                ins.then_inc(N["f_g"], 1)

            staged_batches(act, 0, [(0, gelu)], 2)


def mean_rstd(nc, link, st, mv):
    me, ve, mo, vo = (st[:, :, k] for k in (1, 2, 4, 5))
    v = nc.vector
    link(v.tensor_tensor(mv[:, 0, :], me, mo, ALU.add))
    link(v.tensor_scalar(mv[:, 1, :], mv[:, 0, :], 0.5, None, ALU.mult))
    link(v.tensor_tensor(mv[:, 2, :], me, mo, ALU.subtract))
    link(v.scalar_tensor_tensor(mv[:, 3, :], mv[:, 2, :], 0.25, mv[:, 2, :], ALU.mult, ALU.mult))
    link(v.tensor_tensor(mv[:, 4, :], ve, vo, ALU.add))
    link(v.scalar_tensor_tensor(mv[:, 5, :], mv[:, 4, :], 1.0 / D, mv[:, 3, :], ALU.mult, ALU.add))
    link(v.tensor_scalar(mv[:, 5, :], mv[:, 5, :], 1e-5, None, ALU.add))
    rsqrt(nc, link, mv[:, 6, :], mv[:, 5, :], mv[:, 7, :])


def rotary_tables():
    half = np.arange(0, DH, 2, dtype=np.float32)
    inv_freq = (1.0 / np.float32(10000.0) ** (half / np.float32(DH))).astype(np.float32)
    t = np.arange(S, dtype=np.float32)
    freqs = t[:, None] * inv_freq[None, :]
    base = (half + np.float32(0.4 * DH)) / np.float32(1.4 * DH)
    power = (t - S // 2) / np.float32(WIN // 2)
    scale = (base[None, :] ** power[:, None]).astype(np.float32)
    c, s = np.cos(freqs), np.sin(freqs)
    two = lambda u, w: np.concatenate([u, w], -1)
    rows = np.stack([two(c * scale, c * scale), two(-s * scale, s * scale),
                     two(c / scale, c / scale), two(-s / scale, s / scale)], 1)
    return np.ascontiguousarray(rows.reshape(TPB, P, 4, DH).transpose(1, 0, 2, 3), np.float32)


def third_order_masks():
    sp, k, s, j = (np.arange(n) for n in (G3, 3, G3, W3))
    out = np.full((3, G3, 3, G3, W3), MASKED, np.float32)
    for g in range(3):
        tok = G3 * g + s[None, None, :, None]
        key = G3 * (g - 2 + k[None, :, None, None]) + sp[:, None, None, None]
        ok = (tok - key >= 0) & (tok - key < W3)
        if g < 2:
            ok = ok & (key >= 0) & (tok - W3 + 1 + j[None, None, None, :] >= 0)
        ok = np.broadcast_to(ok, (G3, 3, G3, W3))
        out[g][ok] = 0.0
    out = out.reshape(3, G3, 3 * P).transpose(1, 0, 2)
    return np.ascontiguousarray(np.tile(out, (H3, 1, 1)))


def lay_out(inp):
    g = lambda n: np.asarray(inp[n])
    c = np.ascontiguousarray
    tiles = lambda v: c(v.reshape(NT, P, D).transpose(1, 0, 2))
    sw = lambda v: np.concatenate([v[:, DH // 2:], v[:, :DH // 2]], -1)
    qs, ks = g("L0_ffn_q_scale"), g("L0_ffn_k_scale")
    scales = np.stack([qs, sw(qs), ks, sw(ks)], 1)
    b1 = g("L0_ffn_b1").reshape(DEPTH, 2, FF)
    b1p = np.zeros((DEPTH, 2, 3 * P), np.float32)
    b1p[:, :, :FF] = b1
    cols = np.concatenate([g("L0_ffn_ln_g")[:, :, None], g("L0_ffn_ln_b")[:, :, None],
                           b1p.reshape(DEPTH, 6, P).transpose(0, 2, 1)], -1)
    b2big = np.zeros((CHUNK, EXPERTS, CHUNK, D), np.float32)
    for t in range(CHUNK):
        b2big[t, :, t] = g("L1_ffn_b2")
    b2big = b2big.reshape(CHUNK * EXPERTS, CHUNK, D)
    return {
        "x": tiles(g("L0_attn_x")),
        "ident": np.eye(P, dtype=np.float32),
        "Wqkv": c(g("L0_ffn_Wqkv")),
        "Wo": c(g("L0_ffn_Wo").reshape(DEPTH, HEADS // 2, P, D).transpose(0, 2, 1, 3)),
        "scales": c(np.broadcast_to(scales[:, None], (DEPTH, P, 4, DH))),
        "tables": rotary_tables(),
        "cT0": c(g("L0_c").T), "wmod0": c(g("L0_wmod")), "cT1": c(g("L1_c").T), "wmod1": c(g("L1_wmod")),
        "a_w": c(np.stack([g("L0_attn_W" + n).T for n in "qkv"], 1)),
        "a_b": c(np.stack([g("L0_attn_bq"), g("L0_attn_bk")], 1)), "a_bv": c(g("L0_attn_bv")[None]),
        "d_w": c(np.stack([g("L1_attn_" + n).T for n in ("Wq", "Wk", "Wkp", "Wv", "Wo")], 1)),
        "d_bd": np.repeat(np.eye(H3, dtype=np.float32), D3, 0), "d_mask": third_order_masks(),
        "d_ln": c(np.broadcast_to(np.stack([g("L1_attn_gamma"), g("L1_attn_beta")])[None], (P, 2, D))),
        "e_wr": c(g("L1_ffn_Wr")), "e_w1": c(g("L1_ffn_W1").transpose(1, 0, 2)),
        "e_w2": c(g("L1_ffn_W2").reshape(EXPERTS, DI // P, P, D).transpose(2, 0, 1, 3)),
        "e_b1": c(g("L1_ffn_b1").reshape(EXPERTS, DI // P, P).transpose(2, 0, 1)), "e_b2": b2big,
        "e_below": np.triu(np.ones((P, P), np.float32), 1),
        "W1": c(g("L0_ffn_W1")), "W2": c(g("L0_ffn_W2")), "ffcols": c(cols), "b2": c(g("L0_ffn_b2")),
    }


def kernel(**inputs):
    import concourse.bacc as bacc
    from concourse.bass_utils import run_bass_kernel_spmd

    nc = bacc.Bacc("TRN2", target_bir_lowering=False, num_devices=1)
    arrays = lay_out(inputs)
    aps = {k: nc.dram_tensor(f"in_{k}", v.shape, mybir.dt.from_np(v.dtype), kind="ExternalInput").ap() for k, v in arrays.items()}
    out = nc.dram_tensor("out", (P, NT, D), F32, kind="ExternalOutput").ap()
    build(nc, aps, out)
    r = run_bass_kernel_spmd(nc, [{f"in_{k}": v for k, v in arrays.items()}], core_ids=[0])
    got = r.results[0]["out"]
    return np.ascontiguousarray(got.transpose(1, 0, 2)).reshape(B, S, D)
```

```python
from contextlib import ExitStack

import numpy as np

import concourse.bass as bass
from concourse import mybir

F32 = mybir.dt.float32
BF16 = mybir.dt.bfloat16
I32 = mybir.dt.int32
ACT = mybir.ActivationFunctionType
ALU = mybir.AluOpType
AX = mybir.AxisListType.X

P = 128
B = 16
S = 256
D = 128
TPB = S // P
NT = B * TPB
DEPTH = 6
HEADS, DH = 16, 64
INNER = HEADS * DH
WIN = 32
FF = int(D * 4 * 2 / 3)
FFC = [(0, 128), (128, 128), (256, FF - 256)]
TOPK = 32
NEG = -3.0e38
MASKED = -1.0e30
MAGIC = float(0x5F3759DF)
CR = 8
UPB = 4
H2 = HEADS // 2
QK_SCALE = 8.0
PER_UNIT = {"sim_ps": 2, "pv_ps": 4}


def view(t, part0, nparts, offset, dims):
    a = t[part0:part0 + nparts]
    row = a.ap[0][0]
    return bass.AP(tensor=a.tensor, offset=a.offset + offset, ap=[[row, nparts]] + [list(d) for d in dims])


class Chain:

    def __init__(self, eng, sem, per, turn, gate=None, between=()):
        self.between = list(between)
        self.eng, self.sem, self.k, self.per, self.base, self.gate = eng, sem, 0, per, turn * per, gate

    def __call__(self, ins):
        self.k += 1
        assert self.k <= self.per, self.sem
        ins.then_inc(self.sem, 1)
        if self.between:
            self.between.pop(0)()
        self.eng.wait_ge(self.sem, self.base + self.k)
        if self.gate is not None:
            self.eng.sem_inc(self.gate, 1)

    def end(self):
        assert self.k == self.per and not self.between, (self.sem, self.k)


RSQRT_OPS = 2 + 3 * 3


def rsqrt(nc, link, y, v, tmp):
    link(nc.vector.tensor_scalar(y.bitcast(I32), v.bitcast(I32), 1, None, ALU.logical_shift_right))
    link(nc.vector.tensor_scalar(y.bitcast(I32), y.bitcast(I32), -1.0, MAGIC, ALU.mult, ALU.add))
    for _ in range(3):
        link(nc.vector.tensor_tensor(tmp, y, y, ALU.mult))
        link(nc.vector.scalar_tensor_tensor(tmp, tmp, -0.5, v, ALU.mult, ALU.mult))
        link(nc.vector.scalar_tensor_tensor(y, tmp, 1.5, y, ALU.add, ALU.mult))


def build(nc, a, out):
    with ExitStack() as ctx:
        def sb(name, shape, dt=F32):
            return ctx.enter_context(nc.sbuf_tensor(name, shape, dt))

        def sem(name):
            return ctx.enter_context(nc.semaphore(name))

        ps = ctx.enter_context(nc.psum_tensor("ps", [P, 8, 512], F32))
        x = sb("x", [P, NT, D])
        ident = sb("ident", [P, P])
        identb = sb("identb", [P, P], BF16)
        ones = sb("ones", [P, P])

        loaded = sem("loaded")
        consts = sem("consts")
        with nc.Block() as block:
            @block.sync
            def _(sp):
                sp.dma_start(x[:, :, :], a["x"]).then_inc(loaded, 16)
                sp.dma_start(ident[:, :], a["ident"]).then_inc(loaded, 16)
                sp.wait_ge(loaded, 32)

            @block.vector
            def _(dve):
                dve.wait_ge(loaded, 32)
                nc.vector.tensor_copy(identb[:, :], ident[:, :]).then_inc(consts, 1)
                nc.vector.memset(ones[:, :], 1.0).then_inc(consts, 1)
                dve.wait_ge(consts, 2)

        y = sb("y", [P, NT, D])
        rows = sb("rows", [P, B, 4, D])
        colmod = sb("colmod", [P, 6, B])
        mv = sb("mv_x", [P, 8, NT])
        modulation(nc, a, 0, sem, ps, colmod, rows)
        norm_stats(nc, sem, x, mv, "a")
        top32_attention(nc, a, sem, ps, x, y, mv, colmod, rows, ident, ones)
        norm_stats(nc, sem, x, mv, "b")
        into_y(nc, sem, x, y, mv, rows)
        local_transformer(nc, a, sem, ps, y, ident, identb, ones)
        add_gated(nc, sem, x, y, rows)
        modulation(nc, a, 1, sem, ps, colmod, rows)
        norm_stats(nc, sem, x, mv, "d")
        third_order_attention(nc, a, sem, ps, x, y, mv, colmod, rows, ident, identb)
        norm_stats(nc, sem, x, mv, "e")
        expert_choice(nc, a, sem, ps, x, y, mv, colmod, rows, ident, ones)

        stored = sem("stored")
        with nc.Block() as block:
            @block.sync
            def _(sp):
                sp.dma_start(out, x[:, :, :]).then_inc(stored, 16)
                sp.wait_ge(stored, 16)


class Marks:

    def __init__(self, sem, **by_engine):
        self.s, self.by, self.f = {}, {}, {}
        for who, names in by_engine.items():
            self.by[who] = names
            for n in names:
                self.s[n] = sem(n)

    def give(self, who, eng):
        for n in self.by[who]:
            eng.sem_inc(self.s[n], CR)

    def done(self, eng, name, unit):
        eng.wait_ge(self.s[name], unit + 1 + CR)

    def mark(self, name, ins):
        ins.then_inc(self.s[name], 1)


def staged_batches(eng, lags, stages, step=1):
    peeled = -(-lags // step) * step
    args = (lambda b, k: (b,)) if step == 1 else (lambda b, k: (b, k % step))

    def slot(batch, k, exists):
        for lag, fn, *inner in stages:
            between = [lambda f=f, g=g: f(*args(batch(g), k - g)) for g, f in (inner[0] if inner else ()) if exists(g)]
            if exists(lag):
                fn(*args(batch(lag), k - lag), *([between] if inner else []))
            else:
                for f in between:
                    f()
    for b in range(peeled):
        slot(lambda lag: b - lag, b, lambda lag: b >= lag)
    with eng.Fori(peeled // step, B // step) as g:
        for k in range(step):
            slot(lambda lag: step * g + (k - lag), k, lambda lag: True)
    for b in range(B, B + lags):
        slot(lambda lag: b - lag, b, lambda lag: b - lag < B)


def modulation(nc, a, l, sem, ps, colmod, rows):
    with ExitStack() as ctx:
        sb = lambda n, s, d=F32: ctx.enter_context(nc.sbuf_tensor(n + str(l), s, d))
        cT, sT, wmod = sb("cT", [P, B]), sb("sT", [P, B]), sb("wmod", [P, 6 * D])
        big, sign = sb("big", [P, B, 2, D]), sb("sign", [P, B, 2, D])
        m_in, m_silu, m_ps, m_sb, m_d = (sem(f"{n}{l}") for n in ("m_in", "m_silu", "m_ps", "m_sb", "m_d"))
        with nc.Block() as block:
            @block.sync
            def _(sp):
                sp.dma_start(cT[:, :], a[f"cT{l}"]).then_inc(m_in, 16)
                sp.dma_start(wmod[:, :], a[f"wmod{l}"]).then_inc(m_in, 16)

            @block.scalar
            def _(act):
                act.wait_ge(m_in, 32)
                nc.scalar.activation(sT[:, :], cT[:, :], ACT.Silu).then_inc(m_silu, 1)
                for b in range(B):
                    act.wait_ge(m_ps, b + 2)
                    nc.scalar.activation(rows[:, b, :, :].rearrange("p r d -> p (r d)"), ps[:, 1 + b % 4, :], ACT.Copy).then_inc(m_sb, 1)

            @block.tensor
            def _(pe):
                pe.wait_ge(m_in, 32)
                pe.wait_ge(m_silu, 1)
                for j in range(6):
                    mm = nc.tensor.matmul(ps[:, 0, j * B:(j + 1) * B], wmod[:, j * D:(j + 1) * D], sT[:, :], start=True, stop=True)
                mm.then_inc(m_ps, 1)
                for b in range(B):
                    if b >= 4:
                        pe.wait_ge(m_sb, b - 3)
                    nc.tensor.matmul(ps[:, 1 + b % 4, :], view(sT, 0, P, b, [[0, P]]), wmod[:, 2 * D:6 * D],
                                     start=True, stop=True).then_inc(m_ps, 1)

            @block.vector
            def _(dve):
                v = nc.vector
                dve.wait_ge(m_ps, 1)
                v.tensor_copy(colmod[:, :, :].rearrange("p j b -> p (j b)"), ps[:, 0, 0:6 * B]).then_inc(m_d, 1)
                dve.wait_ge(m_d, 1)
                v.tensor_scalar(colmod[:, 1, :], colmod[:, 1, :], 1.0, None, ALU.add).then_inc(m_d, 1)
                v.tensor_scalar(colmod[:, 4, :], colmod[:, 4, :], 1.0, None, ALU.add).then_inc(m_d, 1)
                dve.wait_ge(m_sb, B)
                v.tensor_scalar(rows[:, :, 2, :], rows[:, :, 2, :], 1.0, None, ALU.add).then_inc(m_d, 1)
                for k, r in enumerate((0, 3)):
                    v.tensor_scalar(sign[:, :, k, :], rows[:, :, r, :], 0.0, 2.0, ALU.is_ge, ALU.mult).then_inc(m_d, 1)
                dve.wait_ge(m_d, 6)
                for k, r in enumerate((0, 3)):
                    v.scalar_tensor_tensor(big[:, :, k, :], sign[:, :, k, :], -1.0, rows[:, :, r, :], ALU.add, ALU.mult).then_inc(m_d, 1)
                dve.wait_ge(m_d, 8)
                v.tensor_scalar(big[:, :, :, :], big[:, :, :, :], 0.25, None, ALU.max).then_inc(m_d, 1)
                dve.wait_ge(m_d, 9)
                for k, r in enumerate((0, 3)):
                    v.scalar_tensor_tensor(rows[:, :, r, :], sign[:, :, k, :], -1.0, big[:, :, k, :], ALU.add, ALU.mult).then_inc(m_d, 1)
                dve.wait_ge(m_d, 11)


def norm_stats(nc, sem, src, mv, name):
    with ExitStack() as ctx:
        st = ctx.enter_context(nc.sbuf_tensor("st_" + name, [P, NT, 6], F32))
        s_st, s_ch = sem("st_" + name), sem("stch_" + name)
        with nc.Block() as block:
            @block.vector
            def _(dve):
                for t in range(NT):
                    nc.vector.bn_stats(st[:, t, :], src[:, t, :]).then_inc(s_st, 1)
                dve.wait_ge(s_st, NT)
                link = Chain(dve, s_ch, 7 + RSQRT_OPS, 0)
                mean_rstd(nc, link, st, mv)
                link.end()


def top32_attention(nc, a, sem, ps, x, v_all, mv, colmod, rows, ident, ones):
    with ExitStack() as ctx:
        sb = lambda n, s, d=F32: ctx.enter_context(nc.sbuf_tensor(n, s, d))
        w, bcol, bvrow = sb("a_w", [P, 3, D]), sb("a_b", [P, 2]), sb("a_bv", [1, D])
        xn, hT = sb("a_xn", [P, TPB, D]), sb("a_hT", [P, S])
        qT, kT = sb("a_qT", [P, S]), sb("a_kT", [P, S])
        sc, work = sb("a_sc", [P, 2, TPB, S]), sb("a_work", [P, TPB, S])
        m8, kept = sb("a_m8", [P, TPB, 8]), sb("a_kept", [P, TPB, S])
        den, rden = sb("a_den", [P, 2, TPB]), sb("a_rden", [P, 2, TPB])
        kT2, upd = sb("a_keptT", [P, TPB, S]), sb("a_upd", [P, TPB, D])
        M = Marks(sem, DVE=("a_norm", "a_hTs", "a_top", "a_den", "a_x"), PE=("a_turned", "a_qkv", "a_scores", "a_keptT", "a_out"),
                  ACT=("a_qk", "a_s", "a_kT", "a_vs"))
        a_in, topch, resch, gate, act_gate = sem("a_in"), sem("a_topch"), sem("a_resch"), sem("a_gate"), sem("a_actgate")
        with nc.Block() as block:
            @block.sync
            def _(sp):
                for dst, key in ((w[:, :, :], "a_w"), (bcol[:, :], "a_b"), (bvrow[:, :], "a_bv")):
                    sp.dma_start(dst, a[key]).then_inc(a_in, 16)

            @block.tensor
            def _(pe):
                M.give("PE", pe)
                pe.wait_ge(a_in, 48)

                def turn(b, k):
                    M.done(pe, "a_norm", b)
                    M.done(pe, "a_hTs", b - 1)
                    for t in range(TPB):
                        mm = nc.tensor.transpose(ps[:, 0, t * P:t * P + P], xn[:, t, :], ident[:, :])
                    M.mark("a_turned", mm)

                def project(b, k):
                    M.done(pe, "a_hTs", b)
                    M.done(pe, "a_qk", b - 1)
                    M.done(pe, "a_vs", b - 1)
                    for m in range(2):
                        nc.tensor.matmul(ps[:, 1, m * S:m * S + S], w[:, m, :], hT[:, :], start=True, stop=True)
                    for t in range(TPB):
                        nc.tensor.matmul(ps[:, 2, t * P:t * P + P], hT[:, t * P:t * P + P], w[:, 2, :], start=True, stop=False)
                        mm = nc.tensor.matmul(ps[:, 2, t * P:t * P + P], ones[0:1, :], bvrow[0:1, :], start=False, stop=True)
                    M.mark("a_qkv", mm)

                def score(b, k):
                    M.done(pe, "a_qk", b)
                    M.done(pe, "a_s", b - 1)
                    for t in range(TPB):
                        mm = nc.tensor.matmul(ps[:, 3, t * S:t * S + S], qT[:, t * P:t * P + P], kT[:, :], start=True, stop=True)
                    M.mark("a_scores", mm)

                def turn_kept(b, k):
                    M.done(pe, "a_top", b)
                    M.done(pe, "a_kT", b - 1)
                    for c in range(TPB):
                        for t in range(TPB):
                            mm = nc.tensor.transpose(ps[:, 4, c * S + t * P:c * S + t * P + P], kept[:, t, c * P:c * P + P], ident[:, :])
                    M.mark("a_keptT", mm)

                def attend(b, k):
                    M.done(pe, "a_kT", b)
                    M.done(pe, "a_vs", b)
                    M.done(pe, "a_x", b - 1)
                    for t in range(TPB):
                        for c in range(TPB):
                            mm = nc.tensor.matmul(ps[:, 5, t * P:t * P + P], kT2[:, c, t * P:t * P + P],
                                                  v_all[:, bass.ds(b * TPB + c, 1), :].rearrange("p o d -> p (o d)"),
                                                  start=(c == 0), stop=(c == TPB - 1))
                    M.mark("a_out", mm)

                staged_batches(pe, 3, [(3, turn_kept), (1, project), (1, score), (3, attend), (0, turn)], 2)

            @block.scalar
            def _(act):
                M.give("ACT", act)
                act.wait_ge(a_in, 48)

                def evac_qk(b, k):
                    M.done(act, "a_qkv", b)
                    M.done(act, "a_scores", b - 1)
                    nc.scalar.activation(qT[:, :], ps[:, 1, 0:S], ACT.Identity, bias=bcol[:, 0:1])
                    M.mark("a_qk", nc.scalar.activation(kT[:, :], ps[:, 1, S:2 * S], ACT.Identity, bias=bcol[:, 1:2]))

                def evac_scores(b, k):
                    M.done(act, "a_scores", b)
                    M.done(act, "a_top", b - 2)
                    M.mark("a_s", nc.scalar.activation(sc[:, k, :, :].rearrange("p t s -> p (t s)"), ps[:, 3, :], ACT.Copy))

                def evac_kept(b, k):
                    M.done(act, "a_keptT", b)
                    M.done(act, "a_out", b - 1)
                    M.mark("a_kT", nc.scalar.activation(kT2[:, :, :].rearrange("p t s -> p (t s)"), ps[:, 4, :], ACT.Copy))

                def evac_v(b, k):
                    M.done(act, "a_qkv", b)
                    act.sem_inc(act_gate, 1)
                    M.mark("a_vs", nc.scalar.activation(v_all[:, bass.ds(b * TPB, TPB), :].rearrange("p t d -> p (t d)"), ps[:, 2, 0:TPB * D], ACT.Copy))

                staged_batches(act, 3, [(3, evac_kept), (1, evac_qk), (1, evac_scores), (1, evac_v)], 2)

            @block.vector
            def _(dve):
                M.give("DVE", dve)
                dve.wait_ge(a_in, 48)

                def normalise(b, k):
                    M.done(dve, "a_turned", b - 1)
                    for t in range(TPB):
                        ins = nc.vector.tensor_scalar(xn[:, t, :], x[:, bass.ds(b * TPB + t, 1), :].rearrange("p o d -> p (o d)"),
                                                      mv[:, 1, bass.ds(b * TPB + t, 1)], mv[:, 6, bass.ds(b * TPB + t, 1)],
                                                      ALU.subtract, ALU.mult)
                    M.mark("a_norm", ins)

                def modulate(b, k):
                    M.done(dve, "a_turned", b)
                    M.done(dve, "a_qkv", b - 1)
                    M.mark("a_hTs", nc.vector.tensor_scalar(hT[:, :], ps[:, 0, 0:S], colmod[:, 1, bass.ds(b, 1)],
                                                            colmod[:, 0, bass.ds(b, 1)], ALU.mult, ALU.add))

                def top(b, k):
                    link = Chain(dve, topch, 2 * TOPK // 8 + 1, b, gate)
                    M.done(dve, "a_s", b)
                    M.done(dve, "a_keptT", b - 1)
                    dve.sem_inc(gate, 1)
                    for r in range(TOPK // 8):
                        src = sc[:, k, :, :] if r == 0 else work[:, :, :]
                        for t in range(TPB):
                            ins = nc.vector.max(m8[:, t, :], src[:, t, :])
                        link(ins)
                        for t in range(TPB):
                            ins = nc.vector.match_replace(work[:, t, :], m8[:, t, :], src[:, t, :], NEG)
                        link(ins)
                    for t in range(TPB):
                        ins = nc.vector.scalar_tensor_tensor(kept[:, t, :], work[:, t, :], NEG, sc[:, k, t, :], ALU.is_equal, ALU.mult,
                                                             accum_out=den[:, k, t:t + 1])
                    M.mark("a_top", ins)
                    M.done(dve, "a_top", b)
                    link(nc.vector.tensor_scalar(den[:, k, :], den[:, k, :], 1e-10, None, ALU.add))
                    nc.vector.reciprocal(rden[:, k, :], den[:, k, :]).then_inc(M.s["a_den"], 1)
                    link.end()

                def residual(b, k):
                    link = Chain(dve, resch, 1, b)
                    M.done(dve, "a_out", b)
                    M.done(dve, "a_den", b)
                    for t in range(TPB):
                        ins = nc.vector.scalar_tensor_tensor(upd[:, t, :], ps[:, 5, t * P:t * P + P], rden[:, k, t:t + 1],
                                                             rows[:, bass.ds(b, 1), 0, :].rearrange("p o d -> p (o d)"), ALU.mult, ALU.mult)
                    link(ins)
                    xt = x[:, bass.ds(b * TPB, TPB), :]
                    M.mark("a_x", nc.vector.tensor_tensor(xt, xt, upd[:, :, :], ALU.add))
                    M.done(dve, "a_x", b)

                staged_batches(dve, 3, [(1, modulate), (0, normalise), (2, top), (3, residual)], 2)


def into_y(nc, sem, x, y, mv, rows):
    s = sem("into_y")
    with nc.Block() as block:
        @block.vector
        def _(dve):
            for t in range(NT):
                nc.vector.tensor_scalar(y[:, t, :], x[:, t, :], mv[:, 1, t:t + 1], mv[:, 6, t:t + 1], ALU.subtract, ALU.mult).then_inc(s, 1)
            dve.wait_ge(s, NT)
            yv = y[:, :, :].rearrange("p (b t) d -> p b t d", t=TPB)
            nc.vector.tensor_tensor(yv, yv, view(rows, 0, P, 2 * D, [[4 * D, B], [0, TPB], [1, D]]), ALU.mult).then_inc(s, 1)
            dve.wait_ge(s, NT + 1)
            nc.vector.tensor_tensor(yv, yv, view(rows, 0, P, D, [[4 * D, B], [0, TPB], [1, D]]), ALU.add).then_inc(s, 1)
            dve.wait_ge(s, NT + 2)


def add_gated(nc, sem, x, y, rows):
    s = sem("add_y")
    with nc.Block() as block:
        @block.vector
        def _(dve):
            yv = y[:, :, :].rearrange("p (b t) d -> p b t d", t=TPB)
            nc.vector.tensor_tensor(yv, yv, view(rows, 0, P, 3 * D, [[4 * D, B], [0, TPB], [1, D]]), ALU.mult).then_inc(s, 1)
            dve.wait_ge(s, 1)
            nc.vector.tensor_tensor(x[:, :, :], x[:, :, :], y[:, :, :], ALU.add).then_inc(s, 1)
            dve.wait_ge(s, 2)


H3, D3, W3 = 16, 8, 16
G3 = 8
PAIRS = S // (2 * G3)
BLKS = S // G3
CB = 4
CHUNKS = BLKS // CB
AT_PIECE = {1: ("block", 6), 3: ("block", 7), 4: ("out", 1), 5: ("turn",), 6: ("project", 0), 7: ("project", 1),
            9: ("block", 0), 10: ("block", 1), 11: ("block", 2), 12: ("block", 3), 13: ("block", 4),
            14: ("out", 0), 15: ("block", 5)}


def third_order_attention(nc, a, sem, ps, x, y, mv, colmod, rows, ident, identb):
    with ExitStack() as ctx:
        sb = lambda n, s, d=F32: ctx.enter_context(nc.sbuf_tensor(n, s, d))
        pad = W3 - 1
        half = S // 2
        w = sb("d_w", [P, 5, D])
        bd = sb("d_bd", [P, H3])
        mask_in, mask = sb("d_mask_in", [P, 3, 3 * P]), sb("d_mask", [P, 3, 3 * P], BF16)
        xn, hT, hTo = sb("d_xn", [P, TPB, D]), sb("d_hT", [P, S]), sb("d_hTo", [P, S])
        QT, KT, KpT = sb("d_QT", [P, S]), sb("d_KT", [P, pad + S]), sb("d_KpT", [P, S])
        VTn, VT = sb("d_VTn", [P, S]), sb("d_VT", [P, pad + S])
        U = sb("d_U", [P, S, W3])
        KBD, VBD = sb("d_KBD", [P, 2 + BLKS, P]), sb("d_VBD", [P, 2 + BLKS, P])
        VTrep = sb("d_VTrep", [P, 2, CB, H3, G3])
        onesBD = sb("d_onesBD", [P, P])
        mx, mxh = sb("d_mx", [P, 2, 2, G3]), sb("d_mxh", [2 * G3, 2, H3])
        mxr = sb("d_mxr", [2 * G3, 2, 4, H3])
        hl = sb("d_hl_t", [4 * H3, 2, 2 * G3], BF16)
        spread_in, spread = sb("d_spread_in", [4 * H3, P]), sb("d_spread", [4 * H3, P], BF16)
        pr = sb("d_pr", [P, 2, 2, 3 * P])
        psum = sb("d_psum", [P, 2, 2, P])
        wv = sb("d_wv", [P, 2, 2 * P])
        zs, sj, rdn = sb("d_zs", [P, 2, 2 * G3]), sb("d_sj", [P, 2, 2 * G3]), sb("d_rdn", [P, 2, 2 * G3])
        ZT = sb("d_ZT", [P, S])
        M = Marks(sem,
                  DVE=("d_norm", "d_hTs", "d_mx", "d_mxh", "d_hl", "d_z", "d_vbd", "d_zd", "d_sjd"),
                  PE=("d_turned", "d_proj", "d_vt", "d_a", "d_t", "d_r", "d_sub", "d_w_", "d_o"),
                  ACT=("d_pj", "d_exp", "d_vr", "d_vc", "d_hc", "d_oy"), POOL=("d_ukbd", "d_ps", "d_psa"))
        d_in, once, z_ch, h_ch, r_ch, act_gate = (sem(n) for n in ("d_in", "d_once", "d_zch", "d_hch", "d_rch", "d_actg"))
        with nc.Block() as block:
            @block.sync
            def _(sp):
                for dst, key in ((w[:, :, :], "d_w"), (bd[:, :], "d_bd"), (mask_in[:, :, :], "d_mask"),
                                 (spread_in[:, :], "d_spread")):
                    sp.dma_start(dst, a[key]).then_inc(d_in, 16)

            @block.vector
            def _(dve):
                M.give("DVE", dve)
                v = nc.vector
                for t in (KT, VT):
                    v.memset(t[:, 0:pad], 0.0).then_inc(once, 1)
                for t in (KBD, VBD):
                    v.memset(t[:, 0:2, :], 0.0).then_inc(once, 1)
                dve.wait_ge(d_in, 64)
                v.tensor_copy(mask[:, :, :], mask_in[:, :, :]).then_inc(once, 1)
                v.tensor_copy(spread[:, :], spread_in[:, :]).then_inc(once, 1)
                v.tensor_copy(onesBD[:, :].rearrange("p (h d) -> p h d", d=D3), view(bd, 0, P, 0, [[1, H3], [0, D3]])).then_inc(once, 1)
                dve.wait_ge(once, 7)

            @block.tensor
            def _(pe):
                M.give("PE", pe)

            @block.scalar
            def _(act):
                M.give("ACT", act)

            @block.gpsimd
            def _(pool):
                M.give("POOL", pool)

        def groups(gp):
            return [2 * gp, 2 * gp + 1]

        def is_batch(n, k):
            return type(n) is int and n == k

        def blocks_free(eng, n, q):
            if not is_batch(n, 0) or q > CHUNKS - 3:
                M.done(eng, "d_w_", PAIRS * (n - 1) + min(2 * q + 2, PAIRS - 1))

        def batches(eng, slot, piece, lags):
            def pieces(b, s, first, last):
                what = AT_PIECE.get(s)
                if what is None or (what == ("out", 1) and first):
                    return
                own = what[0] == "out" or (what[0] == "block" and what[1] > CHUNKS - 3)
                if last and not own:
                    return
                piece(what, b - 1 if what == ("out", 1) else b if own else b + 1, last)

            def body(b, first=False, last=False):
                for s in range(PAIRS):
                    slot(b, s, first, lambda: pieces(b, s, first, last))
            for s in (5, 6, 7, 9, 10, 11, 12, 13, 15):
                piece(AT_PIECE[s], 0, False)
            body(0, first=True)
            with eng.Fori(1, B - 1) as b:
                body(b)
            body(B - 1, last=True)
            for s in range(lags):
                slot(B, s, False, lambda: None, tail=True)
            piece(("out", 1), B - 1, True)

        def late(b, s, lag, first, fn):
            if s >= lag:
                fn(b, s - lag)
            elif not first:
                fn(b - 1, s - lag + PAIRS)

        with nc.Block() as block:
            @block.tensor
            def _(pe):
                def piece(what, n, last):
                    if what[0] == "turn":
                        M.done(pe, "d_norm", n)
                        M.done(pe, "d_oy", 2 * n - 3)
                        for t in range(TPB):
                            mm = nc.tensor.transpose(ps[:, 7, t * P:t * P + P], xn[:, t, :], ident[:, :])
                        M.mark("d_turned", mm)
                    elif what[0] == "project":
                        M.done(pe, "d_hTs", n)
                        M.done(pe, "d_pj", 2 * n + what[1] - 1)
                        for m in range(2):
                            mm = nc.tensor.matmul(ps[:, 7, m * S:m * S + S], w[:, 2 * what[1] + m, :], hT[:, :], start=True, stop=True)
                        M.mark("d_proj", mm)
                    elif what[0] == "block":
                        q = what[1]
                        M.done(pe, "d_vr", CHUNKS * n + q)
                        M.done(pe, "d_vbd", CHUNKS * n + q - 1)
                        if q == 0:
                            M.done(pe, "d_pj", 2 * n + 1)
                        if q == 5:
                            M.done(pe, "d_oy", 2 * n - 2)
                        for k in range(CB):
                            mm = nc.tensor.transpose(ps[:, 7, k * P:k * P + P], VTrep[:, q % 2, k, :, :].rearrange("p h s -> p (h s)"), ident[:, :])
                        M.mark("d_vt", mm)
                    else:
                        t = what[1]
                        M.done(pe, "d_z", PAIRS * n + (PAIRS // 2) * (t + 1) - 1)
                        M.done(pe, "d_hc", n)
                        M.done(pe, "d_oy", 2 * n + t - 1)
                        if not last:
                            M.done(pe, "d_vbd", CHUNKS * (n + 1) + (4 if t == 0 else 7))
                        elif t == 1:
                            M.done(pe, "d_vbd", CHUNKS * B - 1)
                        nc.tensor.matmul(ps[:, 7, 0:D], ZT[:, t * P:t * P + P], w[:, 4, :], start=True, stop=False)
                        M.mark("d_o", nc.tensor.matmul(ps[:, 7, 0:D], hTo[:, t * P:t * P + P], ident[:, :], start=False, stop=True))

                def score(b, gp, gi):
                    u = PAIRS * b + gp
                    g = groups(gp)[gi]
                    bank = 1 + 2 * (gp % 2) + gi
                    if gi == 0:
                        M.done(pe, "d_exp", u - 2)
                        M.done(pe, "d_ukbd", CHUNKS * b + gp // 2)
                    nc.tensor.matmul(ps[:, bank, 0:3 * P], identb[:, :], mask[:, min(g, 2), :], start=True, stop=False,
                                     skip_group_check=True)
                    for k in range(3):
                        mm = nc.tensor.matmul(ps[:, bank, k * P:k * P + P], KBD[:, g + k, :],
                                              U[:, g * G3:g * G3 + G3, :].rearrange("p s j -> p (s j)"),
                                              start=False, stop=(k == 2), skip_group_check=True)
                    M.mark("d_a", mm)

                def turn_max(b, gp):
                    u = PAIRS * b + gp
                    M.done(pe, "d_mx", u)
                    M.done(pe, "d_hl", u - 1)
                    M.mark("d_t", nc.tensor.transpose(ps[0:2 * G3, 0, 0:P], mx[:, gp % 2, :, :].rearrange("p g s -> p (g s)"), ident[:, :]))

                def spread_max(b, gp):
                    u = PAIRS * b + gp
                    M.done(pe, "d_mxh", u)
                    M.mark("d_r", nc.tensor.matmul(ps[0:4 * H3, 0, 128:128 + 2 * G3], mxr[:, gp % 2, :, :].rearrange("p r h -> p (r h)"),
                                                   ident[0:2 * G3, 0:2 * G3], start=True, stop=True))

                def subtract_max(b, gp):
                    u = PAIRS * b + gp
                    M.done(pe, "d_hl", u)
                    for gi in range(2):
                        mm = nc.tensor.matmul(ps[:, 1 + 2 * (gp % 2) + gi, 0:3 * P], spread[:, :],
                                              view(hl, 0, 4 * H3, (gp % 2) * 2 * G3 + gi * G3, [[0, 3], [1, G3], [0, W3]]),
                                              start=False, stop=True, skip_group_check=True)
                    M.mark("d_sub", mm)

                def weigh(b, gp, gi):
                    u = PAIRS * b + gp
                    if gi == 0:
                        M.done(pe, "d_exp", u)
                        M.done(pe, "d_vbd", CHUNKS * b + gp // 2)
                        M.done(pe, "d_zd", u - 1)
                    for k in range(3):
                        mm = nc.tensor.matmul(ps[:, 5, gi * P:gi * P + P], VBD[:, groups(gp)[gi] + k, :],
                                              pr[:, gp % 2, gi, k * P:k * P + P], start=(k == 0), stop=(k == 2))
                    if gi == 1:
                        M.done(pe, "d_sjd", u)
                        mm = nc.tensor.matmul(ps[:, 6, 0:2 * G3], onesBD[:, :], sj[:, gp % 2, :], start=True, stop=True)
                        M.mark("d_w_", mm)

                def slot(b, s, first, piece_now, tail=False):
                    if s < 1 or not tail:
                        late(b, s, 1, first, turn_max)
                    if not tail:
                        score(b, s, 0)
                    if s < 1 or not tail:
                        late(b, s, 1, first, spread_max)
                    if not tail:
                        score(b, s, 1)
                    piece_now()
                    late(b, s, 2, first, lambda n, gp: weigh(n, gp, 0))
                    if s < 1 or not tail:
                        late(b, s, 1, first, subtract_max)
                    late(b, s, 2, first, lambda n, gp: weigh(n, gp, 1))

                batches(pe, slot, piece, 2)

            @block.scalar
            def _(act):
                def evacuate(c, n):
                    M.done(act, "d_proj", 2 * n + c)
                    M.done(act, "d_ukbd", CHUNKS * n - 1)
                    if c == 0:
                        nc.scalar.activation(QT[:, :], ps[:, 7, 0:S], ACT.Copy, scale=float(D3) ** -0.5)
                        M.mark("d_pj", nc.scalar.activation(KT[:, pad:pad + S], ps[:, 7, S:2 * S], ACT.Copy))
                    else:
                        M.done(act, "d_vr", CHUNKS * n - 1)
                        M.done(act, "d_vc", 2 * n - 1)
                        nc.scalar.activation(KpT[:, :], ps[:, 7, 0:S], ACT.Copy)
                        M.mark("d_pj", nc.scalar.activation(VTn[:, :], ps[:, 7, S:2 * S], ACT.Copy))

                def repeat_v(n, q):
                    M.done(act, "d_pj", 2 * n + 1)
                    M.done(act, "d_vt", CHUNKS * n + q - 2)
                    M.mark("d_vr", nc.scalar.activation(VTrep[:, q % 2, :, :, :], view(VTn, 0, P, q * CB * G3, [[G3, CB], [0, H3], [1, G3]]), ACT.Copy))

                def take_v(b, part):
                    M.done(act, "d_pj", 2 * b + 1)
                    M.done(act, "d_zd", PAIRS * (b - 1) + (PAIRS // 2 if part == 0 else PAIRS - 1))
                    M.mark("d_vc", nc.scalar.activation(VT[:, pad + part * half:pad + part * half + half], VTn[:, part * half:part * half + half], ACT.Copy))

                def take_h(b):
                    M.done(act, "d_hTs", b)
                    M.done(act, "d_o", 2 * b - 1)
                    M.mark("d_hc", nc.scalar.activation(hTo[:, :], hT[:, :], ACT.Copy))

                def keep_out(n, t):
                    M.done(act, "d_o", 2 * n + t)
                    act.sem_inc(act_gate, 1)
                    M.mark("d_oy", nc.scalar.activation(y[:, bass.ds(n * TPB + t, 1), :].rearrange("p o d -> p (o d)"), ps[:, 7, 0:D], ACT.Copy))

                def piece(what, n, last):
                    if what[0] == "project":
                        evacuate(what[1], n)
                    elif what[0] == "block":
                        repeat_v(n, what[1])
                    elif what[0] == "out":
                        keep_out(n, what[1])

                def exps(b, gp):
                    u = PAIRS * b + gp
                    M.done(act, "d_sub", u)
                    M.done(act, "d_w_", u - 2)
                    M.done(act, "d_ps", u - 2)
                    bank = 1 + 2 * (gp % 2)
                    M.mark("d_exp", nc.scalar.activation(pr[:, gp % 2, :, :], ps[:, bank:bank + 2, 0:3 * P], ACT.Exp))

                def slot(b, s, first, piece_now, tail=False):
                    if not tail:
                        before = AT_PIECE.get(s - 1)
                        now = AT_PIECE.get(s)
                        more = not is_batch(b, B - 1)
                        if before == ("out", 1) and not first:
                            keep_out(b - 1, 1)
                        if before == ("out", 0):
                            keep_out(b, 0)
                        if before is not None and before[0] == "project" and more:
                            evacuate(before[1], b + 1)
                        if s in (0, 3):
                            take_v(b, s // 3)
                        if s == 5:
                            take_h(b)
                        if now is not None and now[0] == "block":
                            own = now[1] > CHUNKS - 3
                            if own or more:
                                repeat_v(b if own else b + 1, now[1])
                    if s < 1 or not tail:
                        late(b, s, 1, first, exps)

                batches(act, slot, piece, 1)

            @block.gpsimd
            def _(pool):
                def piece(what, n, last):
                    if what[0] == "block":
                        q = what[1]
                        M.done(pool, "d_pj", 2 * n + 1)
                        blocks_free(pool, n, q)
                        b0, t0 = q * CB, q * CB * G3
                        nc.gpsimd.tensor_tensor(view(KBD, 0, P, (2 + b0) * P, [[P, CB], [G3, H3], [1, G3]]),
                                                view(KpT, 0, P, t0, [[G3, CB], [0, H3], [1, G3]]),
                                                view(bd, 0, P, 0, [[0, CB], [1, H3], [0, G3]]), ALU.mult)
                        M.mark("d_ukbd", nc.gpsimd.tensor_tensor(U[:, t0:t0 + CB * G3, :], view(QT, 0, P, t0, [[1, CB * G3], [0, W3]]),
                                                                 view(KT, 0, P, t0, [[1, CB * G3], [1, W3]]), ALU.mult))

                def add_up(b, gp):
                    u = PAIRS * b + gp
                    M.done(pool, "d_exp", u)
                    M.done(pool, "d_sjd", u - 2)
                    M.mark("d_psa", nc.gpsimd.tensor_tensor(psum[:, gp % 2, :, :], pr[:, gp % 2, :, 0:P], pr[:, gp % 2, :, P:2 * P], ALU.add))
                    M.done(pool, "d_psa", u)
                    M.mark("d_ps", nc.gpsimd.tensor_tensor(psum[:, gp % 2, :, :], psum[:, gp % 2, :, :], pr[:, gp % 2, :, 2 * P:3 * P], ALU.add))

                def slot(b, s, first, piece_now, tail=False):
                    if s < 1 or not tail:
                        late(b, s, 1, first, add_up)
                    piece_now()
                batches(pool, slot, piece, 1)

            @block.vector
            def _(dve):
                v = nc.vector

                def normalise(n):
                    M.done(dve, "d_turned", n - 1)
                    for t in range(TPB):
                        ins = v.tensor_scalar(xn[:, t, :], x[:, bass.ds(n * TPB + t, 1), :].rearrange("p o d -> p (o d)"),
                                              mv[:, 1, bass.ds(n * TPB + t, 1)], mv[:, 6, bass.ds(n * TPB + t, 1)],
                                              ALU.subtract, ALU.mult)
                    M.mark("d_norm", ins)

                def piece(what, n, last):
                    if what[0] == "turn":
                        if is_batch(n, 0):
                            normalise(0)
                        M.done(dve, "d_turned", n)
                        M.done(dve, "d_proj", 2 * n - 1)
                        M.done(dve, "d_hc", n - 1)
                        M.mark("d_hTs", v.tensor_scalar(hT[:, :], ps[:, 7, 0:S], colmod[:, 1, bass.ds(n, 1)],
                                                        colmod[:, 0, bass.ds(n, 1)], ALU.mult, ALU.add))
                    elif what[0] == "block":
                        q = what[1]
                        M.done(dve, "d_vt", CHUNKS * n + q)
                        blocks_free(dve, n, q)
                        M.mark("d_vbd", v.tensor_tensor(view(VBD, 0, P, (2 + CB * q) * P, [[P, CB], [D3, H3], [1, D3]]),
                                                        view(ps, 0, P, 7 * 512, [[P, CB], [D3, H3], [1, D3]]),
                                                        view(bd, 0, P, 0, [[0, CB], [1, H3], [0, D3]]), ALU.mult))

                def maxima(b, gp):
                    u = PAIRS * b + gp
                    for gi in range(2):
                        dve.wait_ge(M.s["d_a"], 2 * u + gi + 1 + CR)
                        if gi == 0:
                            M.done(dve, "d_t", u - 2)
                        ins = v.tensor_reduce(mx[:, gp % 2, gi, :], view(ps, 0, P, (1 + 2 * (gp % 2) + gi) * 512, [[W3, G3], [P, 3], [1, W3]]),
                                              mybir.AxisListType.XY, ALU.max)
                    M.mark("d_mx", ins)

                def head_maxima(b, gp):
                    u = PAIRS * b + gp
                    M.done(dve, "d_t", u)
                    M.done(dve, "d_r", u - 2)
                    link = Chain(dve, r_ch, 1, u)
                    link(v.tensor_reduce(mxh[:, gp % 2, :], view(ps, 0, 2 * G3, 0, [[G3, H3], [1, G3]]), AX, ALU.max))
                    M.mark("d_mxh", v.tensor_copy(mxr[:, gp % 2, :, :], view(mxh, 0, 2 * G3, (gp % 2) * H3, [[0, 4], [1, H3]])))

                def split_max(b, gp):
                    u = PAIRS * b + gp
                    link = Chain(dve, h_ch, 1, u)
                    M.done(dve, "d_r", u)
                    M.done(dve, "d_sub", u - 2)
                    link(v.tensor_scalar(hl[:, gp % 2, :], ps[0:4 * H3, 0, 128:128 + 2 * G3], -1.0, None, ALU.mult))
                    low = slice(2 * H3, 4 * H3)
                    M.mark("d_hl", v.scalar_tensor_tensor(hl[low, gp % 2, :], ps[low, 0, 128:128 + 2 * G3], -1.0, hl[low, gp % 2, :],
                                                          ALU.mult, ALU.subtract))

                def sum_places(b, gp):
                    u = PAIRS * b + gp
                    M.done(dve, "d_ps", u)
                    M.done(dve, "d_w_", u - 2)
                    M.mark("d_sjd", v.tensor_reduce(sj[:, gp % 2, :], psum[:, gp % 2, :, :].rearrange("p g (s j) -> p (g s) j", j=W3), AX, ALU.add))

                def combine(b, gp):
                    u = PAIRS * b + gp
                    link = Chain(dve, z_ch, 2, u)
                    M.done(dve, "d_w_", u)
                    M.done(dve, "d_vc", 2 * b + gp // (PAIRS // 2))
                    M.done(dve, "d_o", 2 * (b - 1) + gp // (PAIRS // 2))
                    s0, q = 2 * G3 * gp, gp % 2
                    v.reciprocal(rdn[:, q, :], ps[:, 6, 0:2 * G3])
                    M.mark("d_zd", v.tensor_tensor(wv[:, q, :].rearrange("p (s j) -> p s j", j=W3),
                                                   view(ps, 0, P, 5 * 512, [[W3, 2 * G3], [1, W3]]),
                                                   view(VT, 0, P, s0, [[1, 2 * G3], [1, W3]]), ALU.mult))
                    M.done(dve, "d_zd", u)
                    link(v.tensor_reduce(zs[:, q, :], wv[:, q, :].rearrange("p (s j) -> p s j", j=W3), AX, ALU.add))
                    link(v.tensor_tensor(ZT[:, s0:s0 + 2 * G3], zs[:, q, :], rdn[:, q, :], ALU.mult))
                    v.sem_inc(M.s["d_z"], 1)

                def slot(b, s, first, piece_now, tail=False):
                    if s < 1 or not tail:
                        late(b, s, 1, first, head_maxima)
                        late(b, s, 1, first, split_max)
                    late(b, s, 3, first, combine)
                    if s < 2 or not tail:
                        late(b, s, 2, first, sum_places)
                    if not tail:
                        maxima(b, s)
                        if s == 4 and not is_batch(b, B - 1):
                            normalise(b + 1)
                    piece_now()
                batches(dve, slot, piece, 3)

        st, mv2, lnrow = sb("d_st", [P, NT, 6]), sb("d_mv", [P, 8, NT]), sb("d_lnrow", [P, 2, D])
        ln_in, ln_st, ln_ch = sem("d_ln_in"), sem("d_ln_st"), sem("d_ln_ch")
        with nc.Block() as block:
            @block.sync
            def _(sp):
                sp.dma_start(lnrow[:, :, :], a["d_ln"]).then_inc(ln_in, 16)

            @block.vector
            def _(dve):
                v = nc.vector
                for t in range(NT):
                    v.bn_stats(st[:, t, :], y[:, t, :]).then_inc(ln_st, 1)
                dve.wait_ge(ln_st, NT)
                link = Chain(dve, ln_ch, 7 + RSQRT_OPS + 5, 0)
                mean_rstd(nc, link, st, mv2)
                for t in range(NT):
                    ins = v.tensor_scalar(y[:, t, :], y[:, t, :], mv2[:, 1, t:t + 1], mv2[:, 6, t:t + 1], ALU.subtract, ALU.mult)
                link(ins)
                dve.wait_ge(ln_in, 16)
                yv = y[:, :, :].rearrange("p (b t) d -> p b t d", t=TPB)
                link(v.tensor_tensor(y[:, :, :], y[:, :, :], view(lnrow, 0, P, 0, [[0, NT], [1, D]]), ALU.mult))
                link(v.tensor_tensor(y[:, :, :], y[:, :, :], view(lnrow, 0, P, D, [[0, NT], [1, D]]), ALU.add))
                link(v.tensor_tensor(yv, yv, view(rows, 0, P, 0, [[4 * D, B], [0, TPB], [1, D]]), ALU.mult))
                link(v.tensor_tensor(x[:, :, :], x[:, :, :], y[:, :, :], ALU.add))
                link.end()


EXPERTS, DI = 8, 512
KEEP = max(4, -(-B * S * 2 // EXPERTS))
CHUNK = 4


def expert_choice(nc, a, sem, ps, x, y, mv, colmod, rows, ident, ones):
    with ExitStack() as ctx:
        sb = lambda n, s, d=F32: ctx.enter_context(nc.sbuf_tensor(n, s, d))
        wr, w1, w2 = sb("e_wr", [P, EXPERTS]), sb("e_w1", [P, EXPERTS, DI]), sb("e_w2", [P, EXPERTS, DI // P, D])
        b1, b2 = sb("e_b1", [P, EXPERTS, DI // P]), sb("e_b2", [CHUNK * EXPERTS, CHUNK, D])
        below = sb("e_below", [P, P])
        xn, hT, hall = sb("e_xn", [P, TPB, D]), sb("e_hT", [P, S]), sb("e_hall", [P, NT * P])
        G, GE = sb("e_G", [P, NT, EXPERTS]), sb("e_cmp", [P, NT, EXPERTS])
        eq, rank = sb("e_eq", [P, NT, EXPERTS]), sb("e_rank", [P, NT, EXPERTS])
        tot, tot2 = sb("e_tot", [P, NT, EXPERTS]), sb("e_tot2", [P, NT, EXPERTS])
        small = sb("e_small", [P, NT])
        cnt, need = sb("e_cnt", [P, EXPERTS]), sb("e_need", [P, EXPERTS])
        thr, cand, bit, oki = (sb(n, [P, EXPERTS], I32) for n in ("e_thr", "e_cand", "e_bit", "e_oki"))
        gT = sb("e_gT", [CHUNK * EXPERTS, NT // CHUNK, P])
        hid = sb("e_hid", [P, 2, DI // P, CHUNK * P])
        M = Marks(sem, DVE=("e_norm", "e_hTs", "e_cmpd", "e_gTs", "e_acc", "e_x"),
                  PE=("e_turned", "e_lg", "e_count", "e_gt", "e_b2s", "e_h", "e_y"), ACT=("e_log", "e_gelu", "e_copy"))
        e_in, ch, sch, bch, ach = (sem(n) for n in ("e_in", "e_ch", "e_sch", "e_bch", "e_ach"))
        loads = ((wr[:, :], "e_wr"), (w1[:, :, :], "e_w1"), (w2[:, :, :, :], "e_w2"), (b1[:, :, :], "e_b1"),
                 (b2[:, :, :], "e_b2"), (below[:, :], "e_below"))
        with nc.Block() as block:
            @block.sync
            def _(sp):
                for dst, key in loads:
                    sp.dma_start(dst, a[key]).then_inc(e_in, 16)

            @block.vector
            def _(dve):
                M.give("DVE", dve)
                dve.wait_ge(e_in, 16 * len(loads))
                v = nc.vector

                def normalise(b):
                    M.done(dve, "e_turned", b - 1)
                    for t in range(TPB):
                        ins = v.tensor_scalar(xn[:, t, :], x[:, bass.ds(b * TPB + t, 1), :].rearrange("p o d -> p (o d)"),
                                              mv[:, 1, bass.ds(b * TPB + t, 1)], mv[:, 6, bass.ds(b * TPB + t, 1)],
                                              ALU.subtract, ALU.mult)
                    M.mark("e_norm", ins)

                def modulate(b):
                    M.done(dve, "e_turned", b)
                    M.done(dve, "e_lg", b - 1)
                    M.done(dve, "e_copy", b - 1)
                    M.mark("e_hTs", v.tensor_scalar(hT[:, :], ps[:, 0, 0:S], colmod[:, 4, bass.ds(b, 1)],
                                                    colmod[:, 3, bass.ds(b, 1)], ALU.mult, ALU.add))
                staged_batches(dve, 1, [(1, modulate), (0, normalise)])
                link = Chain(dve, sch, 5, 0)
                dve.wait_ge(M.s["e_log"], B + CR)
                bc = lambda t: view(t, 0, P, 0, [[1, NT], [0, EXPERTS]])
                link(v.tensor_reduce(small[:, :], G[:, :, :], AX, ALU.max))
                link(v.tensor_tensor(G[:, :, :], G[:, :, :], bc(small), ALU.subtract))
                dve.wait_ge(M.s["e_log"], B + 1 + CR)
                link(v.tensor_reduce(small[:, :], G[:, :, :], AX, ALU.add))
                link(v.reciprocal(small[:, :], small[:, :]))
                link(v.tensor_tensor(G[:, :, :], G[:, :, :], bc(small), ALU.mult))
                link.end()

            @block.tensor
            def _(pe):
                M.give("PE", pe)
                pe.wait_ge(e_in, 16 * len(loads))

                def turn(b):
                    M.done(pe, "e_norm", b)
                    M.done(pe, "e_hTs", b - 1)
                    for t in range(TPB):
                        mm = nc.tensor.transpose(ps[:, 0, t * P:t * P + P], xn[:, t, :], ident[:, :])
                    M.mark("e_turned", mm)

                def logits(b):
                    M.done(pe, "e_hTs", b)
                    M.done(pe, "e_log", b - 1)
                    for t in range(TPB):
                        mm = nc.tensor.matmul(ps[:, 1, t * EXPERTS:(t + 1) * EXPERTS], hT[:, t * P:t * P + P], wr[:, :], start=True, stop=True)
                    M.mark("e_lg", mm)
                staged_batches(pe, 1, [(1, logits), (0, turn)])

            @block.scalar
            def _(act):
                M.give("ACT", act)
                with act.Fori(0, B) as b:
                    M.done(act, "e_hTs", b)
                    M.mark("e_copy", nc.scalar.activation(hall[:, bass.ds(b * S, S)], hT[:, :], ACT.Copy))
                    M.done(act, "e_lg", b)
                    M.mark("e_log", nc.scalar.activation(G[:, bass.ds(b * TPB, TPB), :].rearrange("p t e -> p (t e)"),
                                                         ps[:, 1, 0:TPB * EXPERTS], ACT.Copy))
                act.wait_ge(sch, 2)
                M.mark("e_log", nc.scalar.activation(G[:, :, :], G[:, :, :], ACT.Exp))

        BITS = 30
        with nc.Block() as block:
            @block.vector
            def _(dve):
                v = nc.vector
                over = lambda t: view(t, 0, P, 0, [[0, NT], [1, EXPERTS]])
                link = Chain(dve, ch, 2, 0)
                link(v.memset(thr[:, :], 0))
                link(v.memset(bit[:, :], 1 << (BITS - 1)))
                with dve.Fori(0, BITS) as i:
                    link = Chain(dve, bch, 6, i)
                    link(v.tensor_tensor(cand[:, :], thr[:, :], bit[:, :], ALU.bitwise_or))
                    link(v.tensor_tensor(GE[:, :, :], G[:, :, :], over(cand).bitcast(F32), ALU.is_ge))
                    M.mark("e_cmpd", v.tensor_reduce(cnt[:, :], GE[:, :, :].rearrange("p t e -> p e t"), AX, ALU.add))
                    M.done(dve, "e_count", i)
                    link(v.tensor_scalar(oki[:, :], ps[:, 0, 0:EXPERTS], float(KEEP), None, ALU.is_ge))
                    link(v.tensor_tensor(oki[:, :], oki[:, :], bit[:, :], ALU.mult))
                    link(v.tensor_tensor(thr[:, :], thr[:, :], oki[:, :], ALU.bitwise_or))
                    link(v.tensor_scalar(bit[:, :], bit[:, :], 1, None, ALU.logical_shift_right))
                    link.end()
                link = Chain(dve, ach, 6 + 5 + 5, 0)
                thf = view(thr, 0, P, 0, [[0, NT], [1, EXPERTS]]).bitcast(F32)
                link(v.tensor_tensor(GE[:, :, :], G[:, :, :], thf, ALU.is_gt))
                link(v.tensor_tensor(eq[:, :, :], G[:, :, :], thf, ALU.is_equal))
                link(v.tensor_reduce(cnt[:, :], GE[:, :, :].rearrange("p t e -> p e t"), AX, ALU.add))
                v.sem_inc(M.s["e_cmpd"], 1)
                M.done(dve, "e_count", BITS)
                link(v.tensor_scalar(need[:, :], ps[:, 0, 0:EXPERTS], -1.0, float(KEEP), ALU.mult, ALU.add))
                link(v.tensor_copy(rank[:, :, :].rearrange("p t e -> p (t e)"), ps[:, 1, 0:NT * EXPERTS]))
                link(v.tensor_copy(tot[:, :, :].rearrange("p t e -> p (t e)"), ps[:, 2, 0:NT * EXPERTS]))
                src, dst, k = tot, tot2, 1
                while k < NT:
                    v.tensor_copy(dst[:, 0:k, :], src[:, 0:k, :])
                    link(v.tensor_tensor(dst[:, k:NT, :], src[:, k:NT, :], src[:, 0:NT - k, :], ALU.add))
                    src, dst, k = dst, src, 2 * k
                link(v.tensor_tensor(rank[:, 1:NT, :], rank[:, 1:NT, :], src[:, 0:NT - 1, :], ALU.add))
                link(v.tensor_tensor(rank[:, :, :], rank[:, :, :], view(need, 0, P, 0, [[0, NT], [1, EXPERTS]]), ALU.is_lt))
                link(v.tensor_tensor(eq[:, :, :], eq[:, :, :], rank[:, :, :], ALU.mult))
                link(v.tensor_tensor(GE[:, :, :], GE[:, :, :], eq[:, :, :], ALU.add))
                link(v.tensor_tensor(G[:, :, :], G[:, :, :], GE[:, :, :], ALU.mult))
                link.end()

            @block.tensor
            def _(pe):
                with pe.Fori(0, BITS) as i:
                    M.done(pe, "e_cmpd", i)
                    M.mark("e_count", nc.tensor.matmul(ps[:, 0, 0:EXPERTS], ones[:, :], cnt[:, :], start=True, stop=True))
                M.done(pe, "e_cmpd", BITS)
                nc.tensor.matmul(ps[:, 1, 0:NT * EXPERTS], below[:, :], eq[:, :, :].rearrange("p t e -> p (t e)"), start=True, stop=True)
                nc.tensor.matmul(ps[:, 2, 0:NT * EXPERTS], ones[:, :], eq[:, :, :].rearrange("p t e -> p (t e)"), start=True, stop=True)
                M.mark("e_count", nc.tensor.matmul(ps[:, 0, 0:EXPERTS], ones[:, :], cnt[:, :], start=True, stop=True))

        NCH = NT // CHUNK
        with nc.Block() as block:
            @block.tensor
            def _(pe):
                for c in range(NCH):
                    mm = nc.tensor.transpose(ps[0:CHUNK * EXPERTS, 6 + c // 4, (c % 4) * P:(c % 4) * P + P],
                                             G[:, c * CHUNK:(c + 1) * CHUNK, :].rearrange("p t e -> p (t e)"), ident[:, :])
                M.mark("e_gt", mm)
                M.done(pe, "e_gTs", 0)
                for c in range(NCH):
                    M.done(pe, "e_copy", B + c - 4)
                    for t in range(CHUNK):
                        mm = nc.tensor.matmul(ps[:, c % 4, t * P:t * P + P], gT[:, c, :], b2[:, t, :], start=True, stop=True)
                    M.mark("e_b2s", mm)
                M.done(pe, "e_copy", B + NCH - 1)

                def up(c, e):
                    M.done(pe, "e_gelu", c * EXPERTS + e - 1)
                    for k in range(DI // P):
                        mm = nc.tensor.matmul(ps[:, k, :], w1[:, e, k * P:k * P + P], hall[:, bass.ds(c * (CHUNK * P), CHUNK * P)], start=True, stop=True)
                    M.mark("e_h", mm)

                def down(c, e):
                    u = c * EXPERTS + e
                    M.done(pe, "e_gelu", u)
                    M.done(pe, "e_acc", u - 2)
                    for t in range(CHUNK):
                        for k in range(DI // P):
                            mm = nc.tensor.matmul(ps[:, 4 + e % 2, t * P:t * P + P], hid[:, e % 2, k, t * P:t * P + P], w2[:, e, k, :],
                                                  start=(k == 0), stop=(k == DI // P - 1))
                    M.mark("e_y", mm)

                def chunk(c, first=False):
                    for e in range(EXPERTS):
                        up(c, e)
                        if e:
                            down(c, e - 1)
                        elif not first:
                            down(c - 1, EXPERTS - 1)
                chunk(0, first=True)
                with pe.Fori(1, NCH) as c:
                    chunk(c)
                down(NCH - 1, EXPERTS - 1)

            @block.scalar
            def _(act):
                for c in range(NCH):
                    M.done(act, "e_b2s", c)
                    M.mark("e_copy", nc.scalar.activation(y[:, c * CHUNK:(c + 1) * CHUNK, :].rearrange("p t d -> p (t d)"), ps[:, c % 4, :], ACT.Copy))
                with act.Fori(0, NCH) as c:
                    for e in range(EXPERTS):
                        u = c * EXPERTS + e
                        M.done(act, "e_h", u)
                        M.done(act, "e_y", u - 2)
                        for k in range(DI // P):
                            ins = nc.scalar.activation(hid[:, e % 2, k, :], ps[:, k, :], ACT.Gelu, bias=b1[:, e, k:k + 1])
                        M.mark("e_gelu", ins)

            @block.vector
            def _(dve):
                v = nc.vector
                M.done(dve, "e_gt", 0)
                for half in range(2):
                    ins = v.tensor_copy(gT[:, 4 * half:4 * half + 4, :].rearrange("p c n -> p (c n)"), ps[0:CHUNK * EXPERTS, 6 + half, :])
                M.mark("e_gTs", ins)
                M.done(dve, "e_copy", B + NCH - 1)
                with dve.Fori(0, NCH) as c:
                    for e in range(EXPERTS):
                        u = c * EXPERTS + e
                        M.done(dve, "e_y", u)
                        for t in range(CHUNK):
                            yt = y[:, bass.ds(c * CHUNK + t, 1), :].rearrange("p o d -> p (o d)")
                            ins = v.scalar_tensor_tensor(yt, ps[:, 4 + e % 2, t * P:t * P + P],
                                                         G[:, bass.ds(c * CHUNK + t, 1), e:e + 1].rearrange("p o e -> p (o e)"),
                                                         yt, ALU.mult, ALU.add)
                        M.mark("e_acc", ins)
                        M.done(dve, "e_acc", u)
                    for t in range(CHUNK):
                        bt = c * (CHUNK // TPB) + t // TPB
                        yt = y[:, bass.ds(c * CHUNK + t, 1), :].rearrange("p o d -> p (o d)")
                        ins = v.tensor_tensor(yt, yt, rows[:, bass.ds(bt, 1), 3, :].rearrange("p o d -> p (o d)"), ALU.mult)
                    ins.then_inc(bch, 1)
                    dve.wait_ge(bch, 6 * BITS + c + 1)
                    xt = x[:, bass.ds(c * CHUNK, CHUNK), :]
                    M.mark("e_x", v.tensor_tensor(xt, xt, y[:, bass.ds(c * CHUNK, CHUNK), :], ALU.add))
                    M.done(dve, "e_x", c)


def local_transformer(nc, a, sem, ps, y, ident, identb, ones):
    with ExitStack() as ctx:
        def sb(name, shape, dt=F32):
            return ctx.enter_context(nc.sbuf_tensor(name, shape, dt))

        wqkv = sb("wqkv", [P, 3 * INNER])
        wo = sb("wo", [P, HEADS // 2, D])
        w1 = sb("w1", [P, 2 * FF])
        w2 = sb("w2", [P, len(FFC), D])
        ffcols = sb("ffcols", [P, 8])
        b2row = sb("b2row", [1, D])
        scales = sb("scales", [P, 4, DH])
        tab0 = sb("tab0", [P, TPB, 4, DH])
        tab = sb("tab", [P, TPB, 4, DH])
        yl = sb("yl", [P, TPB, D])
        hT = sb("hT", [P, S])
        raw = sb("raw", [P, 2, H2, DH])
        sq = sb("sq", [P, 2, H2, DH])
        t1 = sb("t1", [P, 2, H2, DH])
        t2 = sb("t2", [P, 2, H2, DH])
        qkn = sb("qkn", [P, 2, H2, DH])
        ss = sb("ss", [P, 2 * H2])
        rn = sb("rn", [P, 2 * H2])
        rtmp = sb("rtmp", [P, 2 * H2])
        qT = sb("qT", [P, H2 // 2, P])
        kT = sb("kT", [P, HEADS // 2, WIN + S])
        V = sb("V", [P, TPB, INNER])
        Vp = sb("Vp", [P, TPB, INNER])
        maskb = sb("maskb", [P, 2, H2 // 2 * 2 * WIN], BF16)
        rowmax = sb("rowmax", [P, H2])
        sim = sb("sim", [P, H2, 2 * WIN])
        prob = sb("prob", [P, H2, 2 * WIN])
        rowsum = sb("rowsum", [P, 2, H2])
        rsum = sb("rsum", [P, 2, H2])
        pT = sb("pT", [P, 2, H2, 2, WIN])
        on = sb("on", [P, H2 // 2, P])
        oT = sb("oT", [P, H2 // 2, P])
        yf = sb("yf", [P, 2, TPB, D])
        st = sb("st", [P, TPB, 6])
        mv = sb("mv", [P, 8, TPB])
        xn = sb("xn", [P, TPB, D])
        fT = sb("fT", [P, S])
        gg = sb("gg", [P, 2, len(FFC), S])
        hid = sb("hid", [P, len(FFC), S])

        w_in, w_in2 = sem("w_in"), sem("w_in2")
        tab_sem = sem("tab_ready")
        N = {k: sem(k) for k in (
            "yl_ready", "hT_ps", "hT_sb", "proj_ps", "v_ps", "raw_sb", "v_sb", "sq_sb", "ropech", "roped", "summed", "normed",
            "qkT_ps", "qkT_sb", "sim_ps", "smch", "shifted", "prob_sb", "sumch", "pT_sb", "pv_ps", "on_sb",
            "oT_ps", "oT_sb", "wo_ps", "y_sum", "rn_sb",
            "f_yl0", "f_yl1", "f_lnch", "f_xn", "f_hT_ps", "f_hT", "f_a_ps", "f_gate_ps", "f_g", "f_hid", "f_o_ps", "f_y", "f_dve_gate", "f_pe_gate")}
        vp_sem = [sem(f"vp_ready{u}") for u in range(UPB)]
        by = {"PE": ("hT_ps", "proj_ps", "v_ps", "qkT_ps", "sim_ps", "pv_ps", "oT_ps", "wo_ps", "f_hT_ps", "f_a_ps", "f_gate_ps", "f_o_ps"),
              "ACT": ("hT_sb", "raw_sb", "v_sb", "sq_sb", "qkT_sb", "prob_sb", "oT_sb", "f_g"),
              "DVE": ("roped", "rn_sb", "shifted", "pT_sb", "on_sb", "y_sum", "f_xn", "f_hT", "f_hid", "f_y"),
              "POOL": ("summed", "normed")}

        def credit(eng, who):
            for k in by[who]:
                eng.sem_inc(N[k], CR * PER_UNIT.get(k, 1))

        once = sem("lt_once")
        pe_gate, sp_gate = sem("pe_gate"), sem("sp_gate")
        with nc.Block() as block:
            @block.sync
            def _(sp):
                sp.dma_start(tab0[:, :, :, :], a["tables"]).then_inc(once, 16)
                sp.wait_ge(once, 16)

            @block.tensor
            def _(pe):
                credit(pe, "PE")

            @block.scalar
            def _(act):
                credit(act, "ACT")

            @block.gpsimd
            def _(pool):
                credit(pool, "POOL")
                lt_m = sem("lt_mask")
                nc.gpsimd.memset(maskb[:, :, :], 0.0).then_inc(lt_m, 1)
                pool.wait_ge(lt_m, 1)
                k = 1
                for v in range(2):
                    for w in range(4):
                        part = maskb[32 * w:32 * w + 32, v, :].rearrange("p (h c) -> p h c", c=2 * WIN)
                        low = WIN if (v == 0 and w == 0) else 0
                        if low:
                            nc.gpsimd.memset(part[:, :, 0:low], MASKED).then_inc(lt_m, 1)
                            k += 1
                            pool.wait_ge(lt_m, k)
                        else:
                            nc.gpsimd.affine_select(out=part, in_=part, compare_op=ALU.is_ge, fill=MASKED, base=0,
                                                    pattern=[[0, H2 // 2], [1, 2 * WIN]], channel_multiplier=-1).then_inc(lt_m, 1)
                            k += 1
                            pool.wait_ge(lt_m, k)
                        nc.gpsimd.affine_select(out=part, in_=part, compare_op=ALU.is_ge, fill=MASKED, base=WIN,
                                                pattern=[[0, H2 // 2], [-1, 2 * WIN]], channel_multiplier=1).then_inc(lt_m, 1)
                        k += 1
                        pool.wait_ge(lt_m, k)

            @block.vector
            def _(dve):
                credit(dve, "DVE")
                z = sem("lt_zero")
                nc.vector.memset(yl[0:1, 0, D // 2:D], 0.0).then_inc(z, 1)
                nc.vector.memset(yf[0:1, :, 0, D // 2:D], 0.0).then_inc(z, 1)
                nc.vector.memset(kT[:, :, 0:WIN], 0.0).then_inc(z, 1)
                nc.vector.memset(Vp[0:32, 0, :], 0.0).then_inc(z, 1)
                dve.wait_ge(z, 4)

        def load_shifted(sp, dst, b, ready):
            half = slice(D // 2, D)
            sp.dma_start(dst[:, :, 0:D // 2], y[:, bass.ds(TPB * b, TPB), 0:D // 2]).then_inc(ready, 16)
            sp.dma_start(dst[1:P, :, half], y[0:P - 1, bass.ds(TPB * b, TPB), half]).then_inc(ready, 16)
            sp.dma_start(dst[0:1, 1:2, half], y[P - 1:P, bass.ds(TPB * b, 1), half]).then_inc(ready, 16)

        def load_attention_weights(sp, i):
            sp.dma_start(wqkv[:, :], a["Wqkv"][bass.ds(i, 1), :, :].rearrange("o p n -> p (o n)")).then_inc(w_in, 16)
            sp.dma_start(wo[:, :, :], a["Wo"][bass.ds(i, 1), :, :, :].rearrange("o p c n -> p (o c) n")).then_inc(w_in, 16)
            sp.dma_start(scales[:, :, :], a["scales"][bass.ds(i, 1), :, :, :].rearrange("o p c n -> p (o c) n")).then_inc(w_in, 16)

        def load_ffn_weights(sp, i):
            sp.dma_start(w1[:, :], a["W1"][bass.ds(i, 1), :, :].rearrange("o p n -> p (o n)")).then_inc(w_in2, 16)
            for c, (c0, cn) in enumerate(FFC):
                sp.dma_start(w2[0:cn, c, :], a["W2"][bass.ds(i, 1), c0:c0 + cn, :].rearrange("o p n -> p (o n)")).then_inc(w_in2, 16)
            sp.dma_start(ffcols[:, :], a["ffcols"][bass.ds(i, 1), :, :].rearrange("o p n -> p (o n)")).then_inc(w_in2, 16)
            sp.dma_start(b2row[:, :], a["b2"][bass.ds(i, 1), :]).then_inc(w_in2, 16)

        LAGS = 6
        PEELED = -(-LAGS // UPB)
        units_left = [0]

        def staged(eng, i, stages):
            def slots(b, first, last):
                for j in range(LAGS if last else UPB):
                    for lag, fn in stages:
                        k = j - lag
                        if (first and b * UPB + k < 0) or (last and k >= 0):
                            continue
                        units_left[0] = -k - 1 if last else UPB
                        fn(i * (B * UPB) + b * UPB + k, k % UPB, b + k // UPB)
            for b in range(PEELED):
                slots(b, True, False)
            with eng.Fori(PEELED, B) as b:
                slots(b, False, False)
            slots(B, False, True)

        with nc.Block() as block:
            @block.sync
            def _(sp):
                load_attention_weights(sp, 0)
        with nc.Fori(0, DEPTH) as i:
            with nc.Block() as block:
                @block.sync
                def _(sp):
                    load_ffn_weights(sp, i)

                    def load(U, u, b):
                        if u == 0:
                            sp.wait_ge(N["hT_ps"], U - UPB + 1 + CR)
                            load_shifted(sp, yl, b, N["yl_ready"])

                    def shift_v(U, u, b):
                        t, c = u // 2, slice((u % 2) * 512, (u % 2) * 512 + 512)
                        sp.wait_ge(N["v_sb"], U + 1 + CR)
                        sp.sem_inc(sp_gate, 1)
                        if t == 0:
                            sp.wait_ge(N["pv_ps"], (U - 2 + 1 + CR) * 4)
                            sp.dma_start(Vp[0:32, 1, c], V[96:128, 0, c]).then_inc(vp_sem[u], 16)
                        else:
                            sp.wait_ge(N["pv_ps"], (U - 4 + 1 + CR) * 4)
                        sp.dma_start(Vp[32:128, t, c], V[0:96, t, c]).then_inc(vp_sem[u], 16)

                    staged(sp, i, [(0, load), (3, shift_v)])

                @block.tensor
                def _(pe):
                    pe.wait_ge(w_in, 16 * 3 * (i + 1))

                    def turn_qk(U, u, b):
                        pe.wait_ge(N["normed"], U + 1 + CR)
                        pe.wait_ge(N["oT_sb"], U - 4 + 1 + CR)
                        pe.wait_ge(N["y_sum"], U - 4 + 1 + CR)
                        for qk in range(2):
                            for hp in range(H2 // 2):
                                mm = nc.tensor.transpose(ps[:, 3 + qk, hp * P:hp * P + P],
                                                         qkn[:, qk, 2 * hp:2 * hp + 2, :].rearrange("p h d -> p (h d)"), ident[:, :])
                        mm.then_inc(N["qkT_ps"], 1)

                    def project_qk(U, u, b):
                        if u == 0:
                            pe.wait_ge(N["hT_sb"], U + 4 + CR)
                        pe.wait_ge(N["raw_sb"], U - 1 + 1 + CR)
                        pe.wait_ge(N["sq_sb"], U - 1 + 1 + CR)
                        for m in range(2):
                            mm = project(u, m)
                        mm.then_inc(N["proj_ps"], 1)

                    def project_v(U, u, b):
                        pe.wait_ge(N["v_sb"], U - 1 + 1 + CR)
                        project(u, 2).then_inc(N["v_ps"], 1)

                    def project(u, m):
                        t, c = u // 2, (u % 2) * 512
                        return nc.tensor.matmul(ps[:, m, :], hT[:, t * P:t * P + P], wqkv[:, m * INNER + c:m * INNER + c + 512],
                                                start=True, stop=True)

                    def turn_h(U, u, b):
                        if u == 0:
                            pe.wait_ge(N["yl_ready"], (i * B + b) * 48 + 48)
                            pe.wait_ge(N["qkT_sb"], U - 2 + 1 + CR)
                            for t in range(TPB):
                                mm = nc.tensor.transpose(ps[:, 4, t * P:t * P + P], yl[:, t, :], ident[:, :])
                            mm.then_inc(N["hT_ps"], 4)

                    def turn_o(U, u, b):
                        pe.wait_ge(N["on_sb"], U + 1 + CR)
                        pe.wait_ge(N["qkT_sb"], U + min(3, units_left[0]) + 1 + CR)
                        for hp in range(H2 // 2):
                            mm = nc.tensor.transpose(ps[:, 3, hp * P:hp * P + P], on[:, hp, :], ident[:, :])
                        mm.then_inc(N["oT_ps"], 1)

                    def scores_a(U, u, b):
                        t = u // 2
                        pe.wait_ge(N["qkT_sb"], U + 1 + CR)
                        pe.wait_ge(N["shifted"], U - 1 + 1 + CR)
                        for odd in range(2):
                            nc.tensor.matmul(ps[:, 5 + odd, 0:256], identb[:, :], maskb[:, t, :], start=True, stop=False,
                                             skip_group_check=True)
                        score_heads(u, 0)

                    def scores_b(U, u, b):
                        score_heads(u, H2 // 2)

                    def score_heads(u, h0):
                        t, c = u // 2, (u % 2) * (H2 // 2)
                        for h in range(h0, h0 + H2 // 2):
                            r = 64 * (h % 2)
                            for w in range(4):
                                mm = nc.tensor.matmul(ps[32 * w:32 * w + 32, 5 + h % 2, (h // 2) * 64:(h // 2) * 64 + 64],
                                                      qT[r:r + 64, h // 2, 32 * w:32 * w + 32],
                                                      kT[r:r + 64, c + h // 2, t * P + 32 * w:t * P + 32 * w + 64],
                                                      start=False, stop=(h >= H2 - 2), skip_group_check=True)
                            if h >= H2 - 2:
                                mm.then_inc(N["sim_ps"], 1)

                    def attend_a(U, u, b):
                        t = u // 2
                        pe.wait_ge(N["pT_sb"], U + 1 + CR)
                        pe.wait_ge(vp_sem[u], ((i * B + b) + 1) * (32 if t == 0 else 16))
                        if t == 1:
                            pe.wait_ge(vp_sem[u - 2], ((i * B + b) + 1) * 32)
                        pe.wait_ge(N["on_sb"], U - 1 + 1 + CR)
                        pe.sem_inc(pe_gate, 1)
                        attend_heads(u, 0)

                    def attend_b(U, u, b):
                        attend_heads(u, H2 // 2)

                    def attend_heads(u, h0):
                        t, c = u // 2, (u % 2) * 512
                        for h in range(h0, h0 + H2 // 2):
                            for part, v in ((1, V), (0, Vp)):
                                for w in range(4):
                                    mm = nc.tensor.matmul(ps[32 * w:32 * w + 32, 7, h * 64:h * 64 + 64],
                                                          pT[32 * w:32 * w + 32, u % 2, 4 * (h % 2) + h // 2, part, :],
                                                          v[32 * w:32 * w + 32, t, c + h * 64:c + h * 64 + 64],
                                                          start=(part == 1), stop=(part == 0), skip_group_check=True)
                                    if h == H2 - 1 and part == 0:
                                        mm.then_inc(N["pv_ps"], 1)

                    def out_proj(U, u, b):
                        c = (u % 2) * (H2 // 2)
                        pe.wait_ge(N["oT_sb"], U + 1 + CR)
                        pe.wait_ge(N["y_sum"], U - 1 + 1 + CR)
                        for hp in range(H2 // 2):
                            mm = nc.tensor.matmul(ps[:, 4, 0:D], oT[:, hp, :], wo[:, c + hp, :], start=(hp == 0), stop=(hp == H2 // 2 - 1))
                        mm.then_inc(N["wo_ps"], 1)

                    staged(pe, i, [(1, project_qk), (4, attend_a), (1, project_v), (2, turn_qk), (4, attend_b), (0, turn_h), (5, turn_o),
                                   (2, scores_a), (5, out_proj), (2, scores_b)])

                @block.scalar
                def _(act):
                    def evac_qk(U, u, b):
                        t, c = u // 2, (u % 2) * (H2 // 2)
                        act.wait_ge(N["qkT_ps"], U + 1 + CR)
                        act.wait_ge(N["sim_ps"], (U - 1 + 1 + CR) * 2)
                        nc.scalar.activation(qT[:, :, :], ps[:, 3, :].rearrange("p (c n) -> p c n", n=P), ACT.Copy)
                        nc.scalar.activation(kT[:, c:c + H2 // 2, WIN + t * P:WIN + t * P + P],
                                             ps[:, 4, :].rearrange("p (c n) -> p c n", n=P), ACT.Copy).then_inc(N["qkT_sb"], 1)

                    def evac_proj(U, u, b):
                        act.wait_ge(N["proj_ps"], U + 1 + CR)
                        act.wait_ge(N["rn_sb"], U - 1 + 1 + CR)
                        nc.scalar.activation(sq[:, :, :, :].rearrange("p a h d -> p (a h d)"),
                                             ps[:, 0:2, :].rearrange("p a n -> p (a n)"), ACT.Square).then_inc(N["sq_sb"], 1)
                        act.wait_ge(N["roped"], U - 1 + 1 + CR)
                        nc.scalar.activation(raw[:, :, :, :].rearrange("p a h d -> p (a h d)"),
                                             ps[:, 0:2, :].rearrange("p a n -> p (a n)"), ACT.Copy).then_inc(N["raw_sb"], 1)

                    def evac_v(U, u, b):
                        t, c = u // 2, (u % 2) * 512
                        act.wait_ge(N["v_ps"], U + 1 + CR)
                        act.wait_ge(N["pv_ps"], (U - 4 + 1 + CR) * 4)
                        nc.scalar.activation(V[:, t, c:c + 512], ps[:, 2, :], ACT.Copy).then_inc(N["v_sb"], 1)

                    def evac_h(U, u, b):
                        if u == 0:
                            act.wait_ge(N["hT_ps"], U + 4 + CR)
                            act.wait_ge(N["v_ps"], U - 1 + 1 + CR)
                            nc.scalar.activation(hT[:, :], ps[:, 4, 0:S], ACT.Copy).then_inc(N["hT_sb"], 4)

                    def evac_o(U, u, b):
                        act.wait_ge(N["oT_ps"], U + 1 + CR)
                        act.wait_ge(N["wo_ps"], U - 1 + 1 + CR)
                        nc.scalar.activation(oT[:, :, :], ps[:, 3, :].rearrange("p (c n) -> p c n", n=P), ACT.Copy).then_inc(N["oT_sb"], 1)

                    def exps(U, u, b):
                        act.wait_ge(N["shifted"], U + 1 + CR)
                        act.wait_ge(N["pT_sb"], U - 1 + 1 + CR)
                        nc.scalar.activation(prob[:, :, :], sim[:, :, :], ACT.Exp, scale=QK_SCALE).then_inc(N["prob_sb"], 1)

                    staged(act, i, [(3, exps), (1, evac_proj), (2, evac_qk), (1, evac_v), (0, evac_h), (5, evac_o)])

                @block.gpsimd
                def _(pool):
                    def add_turned(U, u, b):
                        pool.wait_ge(N["roped"], U + 1 + CR)
                        nc.gpsimd.tensor_tensor(t1[:, :, :, :].rearrange("p a h d -> p (a h d)"),
                                                t1[:, :, :, :].rearrange("p a h d -> p (a h d)"),
                                                t2[:, :, :, :].rearrange("p a h d -> p (a h d)"), ALU.add).then_inc(N["summed"], 1)

                    def normalise(U, u, b):
                        pool.wait_ge(N["rn_sb"], U + 1 + CR)
                        pool.wait_ge(N["summed"], U + 1 + CR)
                        pool.wait_ge(N["qkT_ps"], U - 1 + 1 + CR)
                        nc.gpsimd.tensor_tensor(qkn[:, :, :, :].rearrange("p a h d -> p (a h) d"),
                                                t1[:, :, :, :].rearrange("p a h d -> p (a h) d"),
                                                view(rn, 0, P, 0, [[1, 2 * H2], [0, DH]]), ALU.mult).then_inc(N["normed"], 1)
                    staged(pool, i, [(1, add_turned), (1, normalise)])

                @block.vector
                def _(dve):
                    dve.wait_ge(w_in, 16 * 3 * (i + 1))
                    nc.vector.tensor_tensor(tab[:, :, :, :].rearrange("p t c d -> p t (c d)"),
                                            tab0[:, :, :, :].rearrange("p t c d -> p t (c d)"),
                                            view(scales, 0, P, 0, [[0, TPB], [1, 4 * DH]]), ALU.mult).then_inc(tab_sem, 1)
                    dve.wait_ge(tab_sem, i + 1)

                    def rope(U, u, b):
                        t = u // 2

                        def straight(qk):
                            if qk == 0:
                                dve.wait_ge(N["raw_sb"], U + 1 + CR)
                                dve.wait_ge(N["normed"], U - 1 + 1 + CR)
                            nc.vector.tensor_tensor(t1[:, qk, :, :], raw[:, qk, :, :],
                                                    view(tab, 0, P, t * 256 + qk * 128, [[0, H2], [1, DH]]), ALU.mult)

                        def swapped(r):
                            ins = nc.vector.tensor_tensor(t2[:, :, :, 32 * r:32 * r + 32], raw[:, :, :, 32 - 32 * r:64 - 32 * r],
                                                          view(tab, 0, P, t * 256 + 64 + 32 * r, [[128, 2], [0, H2], [1, 32]]), ALU.mult)
                            if r == 1:
                                ins.then_inc(N["roped"], 1)

                        link = Chain(dve, N["ropech"], RSQRT_OPS + 2, U, between=(
                            lambda: straight(0), lambda: straight(1), lambda: swapped(0), lambda: swapped(1)))
                        dve.wait_ge(N["sq_sb"], U + 1 + CR)
                        dve.wait_ge(N["normed"], U - 1 + 1 + CR)
                        link(nc.vector.tensor_reduce(ss[:, :], sq[:, :, :, :].rearrange("p a h d -> p (a h) d"), AX, ALU.add))
                        link(nc.vector.tensor_scalar(ss[:, :], ss[:, :], 1e-24, None, ALU.max))
                        rsqrt(nc, link, rn[:, :], ss[:, :], rtmp[:, :])
                        link.end()
                        dve.sem_inc(N["rn_sb"], 1)

                    def softmax_a(U, u, b):
                        link = Chain(dve, N["smch"], 1, U)
                        dve.wait_ge(N["sim_ps"], (U + 1 + CR) * 2)
                        dve.wait_ge(N["prob_sb"], U - 1 + 1 + CR)
                        s5 = view(ps, 0, P, 5 * 512, [[512, 2], [64, 4], [1, 64]])
                        link(nc.vector.tensor_reduce(rowmax[:, :].rearrange("p (a h) -> p a h", a=2), s5, AX, ALU.max))
                        nc.vector.tensor_tensor(sim[:, :, :].rearrange("p (a h) c -> p a h c", a=2), s5,
                                                view(rowmax, 0, P, 0, [[4, 2], [1, 4], [0, 64]]), ALU.subtract)\
                            .then_inc(N["shifted"], 1)
                        link.end()

                    def softmax_b(U, u, b):
                        link = Chain(dve, N["sumch"], 2, U)
                        dve.wait_ge(N["prob_sb"], U + 1 + CR)
                        dve.wait_ge(N["pv_ps"], (U - 2 + 1 + CR) * 4)
                        dve.wait_ge(N["on_sb"], U - 2 + 1 + CR)
                        link(nc.vector.tensor_reduce(rowsum[:, u % 2, :], prob[:, :, :], AX, ALU.add))
                        link(nc.vector.reciprocal(rsum[:, u % 2, :], rowsum[:, u % 2, :]))
                        nc.vector.transpose(pT[:, u % 2, :, :, :].rearrange("p h a q -> p (h a q)"),
                                            prob[:, :, :].rearrange("p h c -> p (h c)")).then_inc(N["pT_sb"], 1)
                        link.end()

                    def scale_out(U, u, b):
                        dve.wait_ge(N["pv_ps"], (U + 1 + CR) * 4)
                        dve.wait_ge(N["oT_ps"], U - 1 + 1 + CR)
                        nc.vector.tensor_tensor(on[:, :, :].rearrange("p c (a d) -> p c a d", d=DH),
                                                ps[:, 7, :].rearrange("p (c a d) -> p c a d", a=2, d=DH),
                                                view(rsum, 0, P, (u % 2) * H2, [[1, 4], [4, 2], [0, DH]]), ALU.mult).then_inc(N["on_sb"], 1)

                    def residual(U, u, b):
                        dve.wait_ge(N["wo_ps"], U + 1 + CR)
                        dve.wait_ge(N["y_sum"], U - 1 + 1 + CR)
                        yt = y[:, bass.ds(b * TPB + u // 2, 1), :].rearrange("p o d -> p (o d)")
                        nc.vector.tensor_tensor(yt, ps[:, 4, 0:D], yt, ALU.add).then_inc(N["y_sum"], 1)

                    staged(dve, i, [(5, scale_out), (3, softmax_a), (6, residual), (3, softmax_b), (1, rope)])

            ffn_layer(nc, a, ps, y, ident, ones, i, N, w1, w2, ffcols, b2row, yf, st, mv, xn, fT, gg, hid, load_shifted, load_attention_weights, w_in2)
        with nc.Block() as block:
            @block.sync
            def _(sp):
                sp.wait_ge(w_in, 16 * 3 * (DEPTH + 1))


def ffn_layer(nc, a, ps, y, ident, ones, i, N, w1, w2, ffcols, b2row, yf, st, mv, xn, fT, gg, hid, load_shifted,
              load_attention_weights, w_in):
    NLN = 1 + 7 + RSQRT_OPS

    def hg(k, g, c):
        bank, side = {(0, 0): (0, 0), (0, 1): (0, 1), (1, 0): (1, 0), (1, 1): (1, 1), (0, 2): (2, 0), (1, 2): (2, 1)}[g, c]
        return ps[:, 1 + 3 * k + bank, side * S:side * S + S]

    with nc.Block() as block:
        @block.sync
        def _(sp):
            def load(b, k):
                sp.wait_ge(N["f_xn"], i * B + b - 1 + CR)
                load_shifted(sp, yf[:, k, :, :], b, N[f"f_yl{k}"])
            staged_batches(sp, 0, [(0, load)], 2)
            load_attention_weights(sp, i + 1)

        @block.vector
        def _(dve):
            dve.wait_ge(w_in, 16 * 6 * (i + 1))
            dve.sem_inc(N["f_dve_gate"], 1)

            def normalise(b, k, between):
                n = i * B + b
                link = Chain(dve, N["f_lnch"], NLN, n, between=between)
                dve.wait_ge(N[f"f_yl{k}"], 24 * (n - k) + 48)
                nc.vector.bn_stats(st[:, 0, :], yf[:, k, 0, :])
                link(nc.vector.bn_stats(st[:, 1, :], yf[:, k, 1, :]))
                mean_rstd(nc, link, st, mv)
                link.end()
                dve.wait_ge(N["f_hT_ps"], n + CR)
                for t in range(TPB):
                    ins = nc.vector.tensor_scalar(xn[:, t, :], yf[:, k, t, :], mv[:, 1, t:t + 1], mv[:, 6, t:t + 1],
                                                  ALU.subtract, ALU.mult)
                ins.then_inc(N["f_xn"], 1)

            def scale(b, k):
                n = i * B + b
                dve.wait_ge(N["f_hT_ps"], n + 1 + CR)
                dve.wait_ge(N["f_a_ps"], n + CR)
                nc.vector.tensor_scalar(fT[:, :], ps[:, 0, 0:S], ffcols[:, 0:1], ffcols[:, 1:2], ALU.mult, ALU.add)\
                    .then_inc(N["f_hT"], 1)

            def gated(c):
                def chunk(b, k):
                    n = i * B + b
                    c0, cn = FFC[c]
                    if c == 0:
                        dve.wait_ge(N["f_g"], n + 1 + CR)
                        dve.wait_ge(N["f_a_ps"], n + 1 + CR)
                        dve.wait_ge(N["f_o_ps"], n + CR)
                    ins = nc.vector.scalar_tensor_tensor(hid[0:cn, c, :], hg(k, 0, c)[0:cn, :], ffcols[0:cn, 2 + c:3 + c],
                                                         gg[0:cn, k, c, :], ALU.add, ALU.mult)
                    if c == len(FFC) - 1:
                        ins.then_inc(N["f_hid"], 1)
                return chunk

            def residual(b, k):
                n = i * B + b
                dve.wait_ge(N["f_o_ps"], n + 1 + CR)
                yt = y[:, bass.ds(b * TPB, TPB), :].rearrange("p t d -> p (t d)")
                nc.vector.tensor_tensor(yt, ps[:, 7, 0:S], yt, ALU.add).then_inc(N["f_y"], 1)

            staged_batches(dve, 3, [(0, normalise, [(1, scale)] + [(2, gated(c)) for c in range(len(FFC))] + [(3, residual)])], 2)

        @block.tensor
        def _(pe):
            pe.wait_ge(w_in, 16 * 6 * (i + 1))
            pe.sem_inc(N["f_pe_gate"], 1)

            def turn(b, k):
                n = i * B + b
                pe.wait_ge(N["f_xn"], n + 1 + CR)
                pe.wait_ge(N["f_hT"], n + CR)
                for t in range(TPB):
                    mm = nc.tensor.transpose(ps[:, 0, t * P:t * P + P], xn[:, t, :], ident[:, :])
                mm.then_inc(N["f_hT_ps"], 1)

            def up(b, k):
                n = i * B + b
                pe.wait_ge(N["f_hT"], n + 1 + CR)
                pe.wait_ge(N["f_hid"], n - 1 + CR)
                for g in (1, 0):
                    for c, (c0, cn) in enumerate(FFC):
                        mm = nc.tensor.matmul(hg(k, g, c)[0:cn, :], w1[:, g * FF + c0:g * FF + c0 + cn], fT[:, :],
                                              start=True, stop=True)
                    mm.then_inc(N["f_gate_ps" if g else "f_a_ps"], 1)

            def down(b, k):
                n = i * B + b
                pe.wait_ge(N["f_hid"], n + 1 + CR)
                pe.wait_ge(N["f_y"], n + CR)
                for t in range(TPB):
                    for c, (c0, cn) in enumerate(FFC):
                        nc.tensor.matmul(ps[:, 7, t * P:t * P + P], hid[0:cn, c, t * P:t * P + P], w2[0:cn, c, :],
                                         start=(c == 0), stop=False)
                    mm = nc.tensor.matmul(ps[:, 7, t * P:t * P + P], ones[0:1, :], b2row[0:1, :], start=False, stop=True)
                mm.then_inc(N["f_o_ps"], 1)

            staged_batches(pe, 2, [(1, up), (2, down), (0, turn)], 2)

        @block.scalar
        def _(act):
            def gelu(b, k):
                n = i * B + b
                act.wait_ge(N["f_gate_ps"], n + 1 + CR)
                act.wait_ge(N["f_a_ps"], n + 1 + CR)
                act.wait_ge(N["f_hid"], n - 1 + CR)
                for c, (c0, cn) in enumerate(FFC):
                    ins = nc.scalar.activation(gg[0:cn, k, c, :], hg(k, 1, c)[0:cn, :], ACT.Gelu, bias=ffcols[0:cn, 5 + c:6 + c])
                ins.then_inc(N["f_g"], 1)

            staged_batches(act, 0, [(0, gelu)], 2)


def mean_rstd(nc, link, st, mv):
    me, ve, mo, vo = (st[:, :, k] for k in (1, 2, 4, 5))
    v = nc.vector
    link(v.tensor_tensor(mv[:, 0, :], me, mo, ALU.add))
    link(v.tensor_scalar(mv[:, 1, :], mv[:, 0, :], 0.5, None, ALU.mult))
    link(v.tensor_tensor(mv[:, 2, :], me, mo, ALU.subtract))
    link(v.scalar_tensor_tensor(mv[:, 3, :], mv[:, 2, :], 0.25, mv[:, 2, :], ALU.mult, ALU.mult))
    link(v.tensor_tensor(mv[:, 4, :], ve, vo, ALU.add))
    link(v.scalar_tensor_tensor(mv[:, 5, :], mv[:, 4, :], 1.0 / D, mv[:, 3, :], ALU.mult, ALU.add))
    link(v.tensor_scalar(mv[:, 5, :], mv[:, 5, :], 1e-5, None, ALU.add))
    rsqrt(nc, link, mv[:, 6, :], mv[:, 5, :], mv[:, 7, :])


def rotary_tables():
    half = np.arange(0, DH, 2, dtype=np.float32)
    inv_freq = (1.0 / np.float32(10000.0) ** (half / np.float32(DH))).astype(np.float32)
    t = np.arange(S, dtype=np.float32)
    freqs = t[:, None] * inv_freq[None, :]
    base = (half + np.float32(0.4 * DH)) / np.float32(1.4 * DH)
    power = (t - S // 2) / np.float32(WIN // 2)
    scale = (base[None, :] ** power[:, None]).astype(np.float32)
    c, s = np.cos(freqs), np.sin(freqs)
    two = lambda u, w: np.concatenate([u, w], -1)
    rows = np.stack([two(c * scale, c * scale), two(-s * scale, s * scale),
                     two(c / scale, c / scale), two(-s / scale, s / scale)], 1)
    return np.ascontiguousarray(rows.reshape(TPB, P, 4, DH).transpose(1, 0, 2, 3), np.float32)


def spread_heads():
    out = np.zeros((4 * H3, P), np.float32)
    for r in (0, 2 * H3):
        out[r:r + H3] = np.repeat(np.eye(H3, dtype=np.float32), G3, 1)
    return out


def third_order_masks():
    sp, k, s, j = (np.arange(n) for n in (G3, 3, G3, W3))
    out = np.full((3, G3, 3, G3, W3), MASKED, np.float32)
    for g in range(3):
        tok = G3 * g + s[None, None, :, None]
        key = G3 * (g - 2 + k[None, :, None, None]) + sp[:, None, None, None]
        ok = (tok - key >= 0) & (tok - key < W3)
        if g < 2:
            ok = ok & (key >= 0) & (tok - W3 + 1 + j[None, None, None, :] >= 0)
        ok = np.broadcast_to(ok, (G3, 3, G3, W3))
        out[g][ok] = 0.0
    out = out.reshape(3, G3, 3 * P).transpose(1, 0, 2)
    return np.ascontiguousarray(np.tile(out, (H3, 1, 1)))


def lay_out(inp):
    g = lambda n: np.asarray(inp[n])
    c = np.ascontiguousarray
    again = lambda v: c(np.concatenate([v, v[:1]]))
    tiles = lambda v: c(v.reshape(NT, P, D).transpose(1, 0, 2))
    sw = lambda v: np.concatenate([v[:, DH // 2:], v[:, :DH // 2]], -1)
    qs, ks = g("L0_ffn_q_scale"), g("L0_ffn_k_scale")
    scales = np.stack([qs, sw(qs), ks, sw(ks)], 1)
    b1 = g("L0_ffn_b1").reshape(DEPTH, 2, FF)
    b1p = np.zeros((DEPTH, 2, 3 * P), np.float32)
    b1p[:, :, :FF] = b1
    cols = np.concatenate([g("L0_ffn_ln_g")[:, :, None], g("L0_ffn_ln_b")[:, :, None],
                           b1p.reshape(DEPTH, 6, P).transpose(0, 2, 1)], -1)
    b2big = np.zeros((CHUNK, EXPERTS, CHUNK, D), np.float32)
    for t in range(CHUNK):
        b2big[t, :, t] = g("L1_ffn_b2")
    b2big = b2big.reshape(CHUNK * EXPERTS, CHUNK, D)
    return {
        "x": tiles(g("L0_attn_x")),
        "ident": np.eye(P, dtype=np.float32),
        "Wqkv": again(g("L0_ffn_Wqkv")),
        "Wo": again(g("L0_ffn_Wo").reshape(DEPTH, HEADS // 2, P, D).transpose(0, 2, 1, 3)),
        "scales": again(np.broadcast_to(scales[:, None], (DEPTH, P, 4, DH))),
        "tables": rotary_tables(),
        "cT0": c(g("L0_c").T), "wmod0": c(g("L0_wmod")), "cT1": c(g("L1_c").T), "wmod1": c(g("L1_wmod")),
        "a_w": c(np.stack([g("L0_attn_W" + n).T for n in "qkv"], 1)),
        "a_b": c(np.stack([g("L0_attn_bq"), g("L0_attn_bk")], 1)), "a_bv": c(g("L0_attn_bv")[None]),
        "d_w": c(np.stack([g("L1_attn_" + n).T for n in ("Wq", "Wk", "Wkp", "Wv", "Wo")], 1)),
        "d_bd": np.repeat(np.eye(H3, dtype=np.float32), D3, 0), "d_mask": third_order_masks(), "d_spread": spread_heads(),
        "d_ln": c(np.broadcast_to(np.stack([g("L1_attn_gamma"), g("L1_attn_beta")])[None], (P, 2, D))),
        "e_wr": c(g("L1_ffn_Wr")), "e_w1": c(g("L1_ffn_W1").transpose(1, 0, 2)),
        "e_w2": c(g("L1_ffn_W2").reshape(EXPERTS, DI // P, P, D).transpose(2, 0, 1, 3)),
        "e_b1": c(g("L1_ffn_b1").reshape(EXPERTS, DI // P, P).transpose(2, 0, 1)), "e_b2": b2big,
        "e_below": np.triu(np.ones((P, P), np.float32), 1),
        "W1": c(g("L0_ffn_W1")), "W2": c(g("L0_ffn_W2")), "ffcols": c(cols), "b2": c(g("L0_ffn_b2")),
    }


def kernel(**inputs):
    import concourse.bacc as bacc
    from concourse.bass_utils import run_bass_kernel_spmd

    nc = bacc.Bacc("TRN2", target_bir_lowering=False, num_devices=1)
    arrays = lay_out(inputs)
    aps = {k: nc.dram_tensor(f"in_{k}", v.shape, mybir.dt.from_np(v.dtype), kind="ExternalInput").ap() for k, v in arrays.items()}
    out = nc.dram_tensor("out", (P, NT, D), F32, kind="ExternalOutput").ap()
    build(nc, aps, out)
    r = run_bass_kernel_spmd(nc, [{f"in_{k}": v for k, v in arrays.items()}], core_ids=[0])
    got = r.results[0]["out"]
    return np.ascontiguousarray(got.transpose(1, 0, 2)).reshape(B, S, D)
```
